# Optimizing a Trainium2 kernel written in Bass

```python
import numpy as np
import jax
import jax.numpy as jnp

def _softmax(x, axis=-1):
    return jax.nn.softmax(x, axis=axis)

def _gelu(x):
    return jax.nn.gelu(x, approximate=True)

def _silu(x):
    return jax.nn.silu(x)

def _sigmoid(x):
    return jax.nn.sigmoid(x)

def _layernorm(x, axis=-1, eps=1e-05):
    m = jnp.mean(x, axis=axis, keepdims=True)
    v = jnp.var(x, axis=axis, keepdims=True)
    return (x - m) / jnp.sqrt(v + eps)

def _scatter_add(tgt, idx, src, axis=0):
    return tgt.at[idx].add(src)

def _segment_sum(src, seg, n):
    return jax.ops.segment_sum(src, seg, n)
kernel_name = 'mk_flamingo_gated_d4_seqx_r8_608335'

def setup_inputs(seed: int=0):
    np.random.seed(seed)
    _w = jnp.asarray

    def _rec_inputs():
        import jax
        import jax.numpy as jnp
        _rk = jax.random.key(seed)
        x = 2.818e-05 + 1 * jax.random.normal(jax.random.fold_in(_rk, 1), (4, 256, 256), jnp.float32)
        _lenS = 256 - jax.random.randint(jax.random.fold_in(_rk, 7), (4,), 0, max(1, 256 // 4) + 1, jnp.int32)
        _lenS2 = 256 - jax.random.randint(jax.random.fold_in(_rk, 8), (4,), 0, max(1, 256 // 4) + 1, jnp.int32)
        _ctx_1024P = jax.random.normal(jax.random.fold_in(_rk, 11), (4, 16, 128), jnp.float32)
        _ctx_1024c = jax.random.dirichlet(jax.random.fold_in(_rk, 511), 0.3 * jnp.ones((16,), jnp.float32), (4, 256))
        _ctx_1024t = jnp.einsum('bsk,bkd->bsd', _ctx_1024c, _ctx_1024P)
        _ctx_1024t = _ctx_1024t * jax.lax.rsqrt(jnp.mean(jnp.square(_ctx_1024t)) + 1e-12) * 0.953939
        ctx_1024 = 7.22013e-05 + 1.00017 * (_ctx_1024t + 0.3 * jax.random.normal(jax.random.fold_in(_rk, 611), (4, 256, 128), jnp.float32))
        fside_BxS2xS2_0 = -3.05549e-07 + 0.0199987 * jax.random.normal(jax.random.fold_in(_rk, 12), (4, 256, 256), jnp.float32)
        _g = jax.random.normal(jax.random.fold_in(_rk, 9001), (2, 4), jnp.float32)
        _g = jnp.sign(_g) * jnp.maximum(jnp.abs(_g), 1.0) + (_g == 0) * 1.0
        g_xattn = _g[0]
        g_ffn = _g[1]
        return (x, ctx_1024, fside_BxS2xS2_0, g_xattn, g_ffn)
    x, ctx_1024, fside_BxS2xS2_0, g_xattn, g_ffn = _rec_inputs()

    def _L0_xattn_setup():
        import jax, jax.numpy as jnp
        import numpy as np
        B_, L_, D_MODEL = (4, 256, 128)
        D_STATE, D_CONV, EXPAND = (16, 4, 2)
        D_INNER = EXPAND * D_MODEL
        DT_RANK = (D_MODEL + 15) // 16

        def silu(x):
            return x * jax.nn.sigmoid(x)
        key = jax.random.key(seed)
        ks = jax.random.split(key, 10)
        f32 = jnp.float32
        hidden_states = jax.random.normal(ks[0], (B_, L_, D_MODEL), dtype=f32)
        z = jax.random.normal(ks[1], (B_, D_INNER, L_), dtype=f32)
        in_proj_w = jax.random.normal(ks[2], (D_INNER, D_MODEL), dtype=f32) * 0.02
        conv_w = jax.random.normal(ks[3], (D_INNER, 1, D_CONV), dtype=f32) * 0.1
        conv_b = jax.random.normal(ks[4], (D_INNER,), dtype=f32) * 0.02
        x_proj_w = jax.random.normal(ks[5], (DT_RANK + 2 * D_STATE, D_INNER), dtype=f32) * 0.02
        dt_proj_w = jax.random.uniform(ks[6], (D_INNER, DT_RANK), dtype=f32, minval=-DT_RANK ** (-0.5), maxval=DT_RANK ** (-0.5))
        dt = jnp.exp(jax.random.uniform(ks[7], (D_INNER,), dtype=f32, minval=np.log(0.001), maxval=np.log(0.1)))
        dt_proj_b = jnp.log(jnp.expm1(dt))
        A_log = jnp.log(jnp.broadcast_to(jnp.arange(1, D_STATE + 1, dtype=f32), (D_INNER, D_STATE)))
        D = jnp.ones((D_INNER,), f32)
        return {'hidden_states': hidden_states, 'z': z, 'in_proj_w': in_proj_w, 'conv_w': conv_w, 'conv_b': conv_b, 'x_proj_w': x_proj_w, 'dt_proj_w': dt_proj_w, 'dt_proj_b': dt_proj_b, 'A_log': A_log, 'D': D}
    _L0_xattn_all = _L0_xattn_setup()
    _L0_xattn_in = {k: v for k, v in _L0_xattn_all.items() if k in ('in_proj_w', 'conv_w', 'conv_b', 'x_proj_w', 'dt_proj_w', 'dt_proj_b', 'A_log', 'D')}
    del _L0_xattn_all

    def _L0_ffn_setup():
        import jax, jax.numpy as jnp
        import numpy as np
        HIDDEN = 256
        INTER = 704
        B, S = (2, 256)

        def _ternary(key, shape):
            return jax.random.randint(key, shape, -1, 2).astype(jnp.float32)
        key = jax.random.key(seed)
        ks = jax.random.split(key, 7)
        x = jax.random.normal(ks[0], (B, S, HIDDEN), dtype=jnp.float32)
        gate_w = _ternary(ks[1], (INTER, HIDDEN))
        up_w = _ternary(ks[2], (INTER, HIDDEN))
        down_w = _ternary(ks[3], (HIDDEN, INTER))
        gate_s = jax.random.uniform(ks[4], (INTER,), minval=0.01, maxval=0.1, dtype=jnp.float32)
        up_s = jax.random.uniform(ks[5], (INTER,), minval=0.01, maxval=0.1, dtype=jnp.float32)
        down_s = jax.random.uniform(ks[6], (HIDDEN,), minval=0.01, maxval=0.1, dtype=jnp.float32)
        return {'x': x, 'gate_w': gate_w, 'up_w': up_w, 'down_w': down_w, 'gate_s': gate_s, 'up_s': up_s, 'down_s': down_s}
    _L0_ffn_all = _L0_ffn_setup()
    _L0_ffn_in = {k: v for k, v in _L0_ffn_all.items() if k in ('gate_w', 'up_w', 'down_w', 'gate_s', 'up_s', 'down_s')}
    del _L0_ffn_all

    def _L1_xattn_setup():
        import jax, jax.numpy as jnp
        import numpy as np
        EPS = 1e-05

        def rmsnorm(x, g, eps=EPS):
            var = jnp.mean(jnp.square(x), axis=-1, keepdims=True)
            return x * jax.lax.rsqrt(var + eps) * g
        key = jax.random.key(seed)
        ks = jax.random.split(key, 8)
        B, Sq, Skv = (2, 512, 64)
        dim, cdim, H, D = (256, 128, 16, 128)
        inner = H * D
        s = lambda f: 1.0 / np.sqrt(f)
        return {'hidden_states': jax.random.normal(ks[0], (B, Sq, dim), jnp.float32), 'encoder_hidden_states': jax.random.normal(ks[1], (B, Skv, cdim), jnp.float32), 'Wq': jax.random.normal(ks[2], (dim, inner), jnp.float32) * s(dim), 'Wk': jax.random.normal(ks[3], (cdim, inner), jnp.float32) * s(cdim), 'Wv': jax.random.normal(ks[4], (cdim, inner), jnp.float32) * s(cdim), 'Wo': jax.random.normal(ks[5], (inner, dim), jnp.float32) * s(inner), 'gq': jnp.ones((D,), jnp.float32), 'gk': jnp.ones((D,), jnp.float32)}
    _L1_xattn_all = _L1_xattn_setup()
    _L1_xattn_in = {k: v for k, v in _L1_xattn_all.items() if k in ('Wq', 'Wk', 'Wv', 'Wo', 'gq', 'gk')}
    del _L1_xattn_all

    def _L1_ffn_setup():
        import jax, jax.numpy as jnp
        import numpy as np
        from jax import lax
        TOP_K = 4
        ROUTED_SCALING = 1.0
        RENORMALIZE = True

        def _swiglu_ffn(x, wg, wu, wd):
            return jax.nn.silu(x @ wg.T) * (x @ wu.T) @ wd.T
        key = jax.random.key(seed)
        ks = jax.random.split(key, 9)
        H, I, E = (256, 128, 16)
        s = 0.02
        return {'hidden_states': jax.random.normal(ks[0], (2, 128, H), jnp.float32), 'gate_w': jax.random.normal(ks[1], (E, H), jnp.float32) * s, 'expert_bias': jax.random.normal(ks[2], (E,), jnp.float32) * s, 'w_gate': jax.random.normal(ks[3], (E, I, H), jnp.float32) * s, 'w_up': jax.random.normal(ks[4], (E, I, H), jnp.float32) * s, 'w_down': jax.random.normal(ks[5], (E, H, I), jnp.float32) * s, 'sw_gate': jax.random.normal(ks[6], (I, H), jnp.float32) * s, 'sw_up': jax.random.normal(ks[7], (I, H), jnp.float32) * s, 'sw_down': jax.random.normal(ks[8], (H, I), jnp.float32) * s}
    _L1_ffn_all = _L1_ffn_setup()
    _L1_ffn_in = {k: v for k, v in _L1_ffn_all.items() if k in ('gate_w', 'expert_bias', 'w_gate', 'w_up', 'w_down', 'sw_gate', 'sw_up', 'sw_down')}
    del _L1_ffn_all

    def _L2_xattn_setup():
        import jax, jax.numpy as jnp
        import numpy as np
        B, S1, S2, DCA = (2, 256, 128, 16)
        QDIM, KDIM, H = (256, 128, 16)
        HD = QDIM // H
        SCALE = HD ** (-0.5)
        EPS = 1e-06
        DCA_WEIGHT = 1.0

        def _ln(t, w, b):
            m = jnp.mean(t, axis=-1, keepdims=True)
            v = jnp.var(t, axis=-1, keepdims=True)
            return (t - m) * jax.lax.rsqrt(v + EPS) * w + b

        def _attn(q, k, v):
            s = jnp.einsum('bhqd,bhkd->bhqk', q, k) * SCALE
            p = jax.nn.softmax(s, axis=-1)
            return jnp.einsum('bhqk,bhkd->bhqd', p, v)
        key = jax.random.key(seed)
        ks = jax.random.split(key, 8)
        w = lambda k, shape: jax.random.normal(k, shape, jnp.float32) * 0.02
        return {'x': jax.random.normal(ks[0], (B, S1, QDIM), jnp.float32), 'y': jax.random.normal(ks[1], (B, S2 + DCA, KDIM), jnp.float32), 'Wq': w(ks[2], (QDIM, QDIM)), 'bq': jnp.zeros((QDIM,), jnp.float32), 'Wk': w(ks[3], (KDIM, QDIM)), 'bk': jnp.zeros((QDIM,), jnp.float32), 'Wv': w(ks[4], (KDIM, QDIM)), 'bv': jnp.zeros((QDIM,), jnp.float32), 'Wkv_dca': w(ks[5], (KDIM, 2 * QDIM)), 'bkv_dca': jnp.zeros((2 * QDIM,), jnp.float32), 'qn_w': jnp.ones((HD,), jnp.float32), 'qn_b': jnp.zeros((HD,), jnp.float32), 'kn_w': jnp.ones((HD,), jnp.float32), 'kn_b': jnp.zeros((HD,), jnp.float32), 'kn_dca_w': jnp.ones((HD,), jnp.float32), 'kn_dca_b': jnp.zeros((HD,), jnp.float32), 'Wo': w(ks[6], (QDIM, QDIM)), 'bo': jnp.zeros((QDIM,), jnp.float32)}
    _L2_xattn_all = _L2_xattn_setup()
    _L2_xattn_in = {k: v for k, v in _L2_xattn_all.items() if k in ('Wq', 'bq', 'Wk', 'bk', 'Wv', 'bv', 'Wkv_dca', 'bkv_dca', 'qn_w', 'qn_b', 'kn_w', 'kn_b', 'kn_dca_w', 'kn_dca_b', 'Wo', 'bo')}
    del _L2_xattn_all

    def _L2_ffn_setup():
        import jax, jax.numpy as jnp
        import numpy as np
        N_EXPERTS = 8
        TOP_K = 2
        D_MODEL = 256
        D_FF = 128
        BATCH, SEQ = (2, 256)

        def _trunc_normal(key, shape, fan_in):
            std = jnp.sqrt(1.0 / 3.0) / jnp.sqrt(float(fan_in))
            return jax.random.truncated_normal(key, -2.0, 2.0, shape, dtype=jnp.float32) * std
        key = jax.random.key(seed)
        kx, kr, k1, k2, k3 = jax.random.split(key, 5)
        x = jax.random.normal(kx, (BATCH, SEQ, D_MODEL), dtype=jnp.float32)
        router_w = jax.random.uniform(kr, (N_EXPERTS, D_MODEL), dtype=jnp.float32, minval=-1.0, maxval=1.0) / jnp.sqrt(float(D_MODEL))
        w1 = _trunc_normal(k1, (N_EXPERTS, D_MODEL, D_FF), D_MODEL)
        w2 = _trunc_normal(k2, (N_EXPERTS, D_MODEL, D_FF), D_MODEL)
        w3 = _trunc_normal(k3, (N_EXPERTS, D_FF, D_MODEL), D_FF)
        return {'x': x, 'router_w': router_w, 'w1': w1, 'w2': w2, 'w3': w3}
    _L2_ffn_all = _L2_ffn_setup()
    _L2_ffn_in = {k: v for k, v in _L2_ffn_all.items() if k in ('router_w', 'w1', 'w2', 'w3')}
    del _L2_ffn_all

    def _L3_xattn_setup():
        import jax, jax.numpy as jnp
        import numpy as np
        EPS = 1e-06
        QMAX = 127.0

        def _smooth_quant_linear(x, w):
            amax_x = jnp.max(jnp.abs(x), axis=0)
            amax_w = jnp.max(jnp.abs(w), axis=0)
            s = jnp.sqrt(jnp.maximum(amax_x, EPS) / jnp.maximum(amax_w, EPS))
            s = jnp.maximum(s, EPS)
            xs = x / s
            ws = w * s
            x_scale = jnp.maximum(jnp.max(jnp.abs(xs), axis=-1, keepdims=True), EPS) / QMAX
            w_scale = jnp.maximum(jnp.max(jnp.abs(ws), axis=-1, keepdims=True), EPS) / QMAX
            x_q = jnp.clip(jnp.round(xs / x_scale), -QMAX, QMAX)
            w_q = jnp.clip(jnp.round(ws / w_scale), -QMAX, QMAX)
            return x_q @ w_q.T * x_scale * w_scale.T

        def _expert_forward(xe, guw, dw):
            h = _smooth_quant_linear(xe, guw)
            gate, up = jnp.split(h, 2, axis=-1)
            a = jax.nn.silu(gate) * up
            return _smooth_quant_linear(a, dw)
        key = jax.random.key(seed)
        k1, k2, k3 = jax.random.split(key, 3)
        E, T, D, I = (8, 256, 256, 128)
        x = jax.random.normal(k1, (E, T, D), dtype=jnp.float32)
        gate_up_weight = jax.random.normal(k2, (E, 2 * I, D), dtype=jnp.float32) * 0.02
        down_weight = jax.random.normal(k3, (E, D, I), dtype=jnp.float32) * 0.02
        return {'x': x, 'gate_up_weight': gate_up_weight, 'down_weight': down_weight}
    _L3_xattn_all = _L3_xattn_setup()
    _L3_xattn_in = {k: v for k, v in _L3_xattn_all.items() if k in ()}
    del _L3_xattn_all

    def _L3_ffn_setup():
        import jax, jax.numpy as jnp
        import numpy as np
        B, S, D = (4, 512, 256)
        DFF = 4 * D
        CAPACITY = 0.125
        K = int(CAPACITY * S)
        key = jax.random.key(seed)
        ks = jax.random.split(key, 8)
        sc = 1.0 / np.sqrt(D)
        return {'x': jax.random.normal(ks[0], (B, S, D), dtype=jnp.float32), 'W_r': jax.random.normal(ks[1], (D, 1), dtype=jnp.float32) * sc, 'b_r': jnp.zeros((1,), dtype=jnp.float32), 'W1': jax.random.normal(ks[2], (D, DFF), dtype=jnp.float32) * sc, 'b1': jnp.zeros((DFF,), dtype=jnp.float32), 'W2': jax.random.normal(ks[3], (DFF, D), dtype=jnp.float32) * (1.0 / np.sqrt(DFF)), 'b2': jnp.zeros((D,), dtype=jnp.float32), 'position_ids': jnp.arange(B * S, dtype=jnp.int64 if jax.config.jax_enable_x64 else jnp.int32).reshape(B, S), 'cache_position': jnp.arange(S, dtype=jnp.int64 if jax.config.jax_enable_x64 else jnp.int32)}
    _L3_ffn_all = _L3_ffn_setup()
    _L3_ffn_in = {k: v for k, v in _L3_ffn_all.items() if k in ('W_r', 'b_r', 'W1', 'b1', 'W2', 'b2', 'position_ids', 'cache_position')}
    del _L3_ffn_all
    return {'x': x, 'ctx_1024': ctx_1024, 'fside_BxS2xS2_0': fside_BxS2xS2_0, 'g_xattn': g_xattn, 'g_ffn': g_ffn, 'L0_xattn_in_proj_w': _L0_xattn_in['in_proj_w'], 'L0_xattn_conv_w': _L0_xattn_in['conv_w'], 'L0_xattn_conv_b': _L0_xattn_in['conv_b'], 'L0_xattn_x_proj_w': _L0_xattn_in['x_proj_w'], 'L0_xattn_dt_proj_w': _L0_xattn_in['dt_proj_w'], 'L0_xattn_dt_proj_b': _L0_xattn_in['dt_proj_b'], 'L0_xattn_A_log': _L0_xattn_in['A_log'], 'L0_xattn_D': _L0_xattn_in['D'], 'L0_ffn_gate_w': _L0_ffn_in['gate_w'], 'L0_ffn_up_w': _L0_ffn_in['up_w'], 'L0_ffn_down_w': _L0_ffn_in['down_w'], 'L0_ffn_gate_s': _L0_ffn_in['gate_s'], 'L0_ffn_up_s': _L0_ffn_in['up_s'], 'L0_ffn_down_s': _L0_ffn_in['down_s'], 'L1_xattn_Wq': _L1_xattn_in['Wq'], 'L1_xattn_Wk': _L1_xattn_in['Wk'], 'L1_xattn_Wv': _L1_xattn_in['Wv'], 'L1_xattn_Wo': _L1_xattn_in['Wo'], 'L1_xattn_gq': _L1_xattn_in['gq'], 'L1_xattn_gk': _L1_xattn_in['gk'], 'L1_ffn_gate_w': _L1_ffn_in['gate_w'], 'L1_ffn_expert_bias': _L1_ffn_in['expert_bias'], 'L1_ffn_w_gate': _L1_ffn_in['w_gate'], 'L1_ffn_w_up': _L1_ffn_in['w_up'], 'L1_ffn_w_down': _L1_ffn_in['w_down'], 'L1_ffn_sw_gate': _L1_ffn_in['sw_gate'], 'L1_ffn_sw_up': _L1_ffn_in['sw_up'], 'L1_ffn_sw_down': _L1_ffn_in['sw_down'], 'L2_xattn_Wq': _L2_xattn_in['Wq'], 'L2_xattn_bq': _L2_xattn_in['bq'], 'L2_xattn_Wk': _L2_xattn_in['Wk'], 'L2_xattn_bk': _L2_xattn_in['bk'], 'L2_xattn_Wv': _L2_xattn_in['Wv'], 'L2_xattn_bv': _L2_xattn_in['bv'], 'L2_xattn_Wkv_dca': _L2_xattn_in['Wkv_dca'], 'L2_xattn_bkv_dca': _L2_xattn_in['bkv_dca'], 'L2_xattn_qn_w': _L2_xattn_in['qn_w'], 'L2_xattn_qn_b': _L2_xattn_in['qn_b'], 'L2_xattn_kn_w': _L2_xattn_in['kn_w'], 'L2_xattn_kn_b': _L2_xattn_in['kn_b'], 'L2_xattn_kn_dca_w': _L2_xattn_in['kn_dca_w'], 'L2_xattn_kn_dca_b': _L2_xattn_in['kn_dca_b'], 'L2_xattn_Wo': _L2_xattn_in['Wo'], 'L2_xattn_bo': _L2_xattn_in['bo'], 'L2_ffn_router_w': _L2_ffn_in['router_w'], 'L2_ffn_w1': _L2_ffn_in['w1'], 'L2_ffn_w2': _L2_ffn_in['w2'], 'L2_ffn_w3': _L2_ffn_in['w3'], 'L3_ffn_W_r': _L3_ffn_in['W_r'], 'L3_ffn_b_r': _L3_ffn_in['b_r'], 'L3_ffn_W1': _L3_ffn_in['W1'], 'L3_ffn_b1': _L3_ffn_in['b1'], 'L3_ffn_W2': _L3_ffn_in['W2'], 'L3_ffn_b2': _L3_ffn_in['b2'], 'L3_ffn_position_ids': _L3_ffn_in['position_ids'], 'L3_ffn_cache_position': _L3_ffn_in['cache_position']}

def reference(x, ctx_1024, fside_BxS2xS2_0, g_xattn, g_ffn, L0_xattn_in_proj_w, L0_xattn_conv_w, L0_xattn_conv_b, L0_xattn_x_proj_w, L0_xattn_dt_proj_w, L0_xattn_dt_proj_b, L0_xattn_A_log, L0_xattn_D, L0_ffn_gate_w, L0_ffn_up_w, L0_ffn_down_w, L0_ffn_gate_s, L0_ffn_up_s, L0_ffn_down_s, L1_xattn_Wq, L1_xattn_Wk, L1_xattn_Wv, L1_xattn_Wo, L1_xattn_gq, L1_xattn_gk, L1_ffn_gate_w, L1_ffn_expert_bias, L1_ffn_w_gate, L1_ffn_w_up, L1_ffn_w_down, L1_ffn_sw_gate, L1_ffn_sw_up, L1_ffn_sw_down, L2_xattn_Wq, L2_xattn_bq, L2_xattn_Wk, L2_xattn_bk, L2_xattn_Wv, L2_xattn_bv, L2_xattn_Wkv_dca, L2_xattn_bkv_dca, L2_xattn_qn_w, L2_xattn_qn_b, L2_xattn_kn_w, L2_xattn_kn_b, L2_xattn_kn_dca_w, L2_xattn_kn_dca_b, L2_xattn_Wo, L2_xattn_bo, L2_ffn_router_w, L2_ffn_w1, L2_ffn_w2, L2_ffn_w3, L3_ffn_W_r, L3_ffn_b_r, L3_ffn_W1, L3_ffn_b1, L3_ffn_W2, L3_ffn_b2, L3_ffn_position_ids, L3_ffn_cache_position):
    import jax
    import jax.numpy as jnp

    def _L0_xattn_ref(hidden_states, z, in_proj_w, conv_w, conv_b, x_proj_w, dt_proj_w, dt_proj_b, A_log, D):
        import jax, jax.numpy as jnp
        import numpy as np
        B_, L_, D_MODEL = (4, 256, 128)
        D_STATE, D_CONV, EXPAND = (16, 4, 2)
        D_INNER = EXPAND * D_MODEL
        DT_RANK = (D_MODEL + 15) // 16

        def silu(x):
            return x * jax.nn.sigmoid(x)
        Bsz, L, _ = hidden_states.shape
        d_inner, _, d_conv = conv_w.shape
        dt_rank = dt_proj_w.shape[1]
        d_state = A_log.shape[1]
        x = jnp.einsum('bld,ed->bel', hidden_states, in_proj_w)
        xc = jax.lax.conv_general_dilated(x, conv_w, window_strides=(1,), padding=[(d_conv - 1, 0)], feature_group_count=d_inner, dimension_numbers=('NCH', 'OIH', 'NCH'))
        x = silu(xc + conv_b[None, :, None])
        x_dbl = jnp.einsum('bdl,ed->bel', x, x_proj_w)
        dt_low, Bm, Cm = jnp.split(x_dbl, [dt_rank, dt_rank + d_state], axis=1)
        dt = jnp.einsum('brl,dr->bdl', dt_low, dt_proj_w)
        dt = jax.nn.softplus(dt + dt_proj_b[None, :, None])
        A = -jnp.exp(A_log)
        dt_t = jnp.moveaxis(dt, -1, 0)
        B_t = jnp.moveaxis(Bm, -1, 0)
        C_t = jnp.moveaxis(Cm, -1, 0)
        u_t = jnp.moveaxis(x, -1, 0)

        def step(state, inp):
            d, b, c, u = inp
            dA = jnp.exp(d[..., None] * A)
            state = state * dA + (d * u)[..., None] * b[:, None, :]
            y = jnp.einsum('bdn,bn->bd', state, c)
            return (state, y)
        state0 = jnp.zeros((Bsz, d_inner, d_state), x.dtype)
        _, ys = jax.lax.scan(step, state0, (dt_t, B_t, C_t, u_t))
        y = jnp.moveaxis(ys, 0, 2)
        y = y + D[None, :, None] * x
        y = y * silu(z)
        return jnp.swapaxes(y, 1, 2)

    def _L0_ffn_ref(x, gate_w, up_w, down_w, gate_s, up_s, down_s):
        import jax, jax.numpy as jnp
        import numpy as np
        HIDDEN = 256
        INTER = 704
        B, S = (2, 256)

        def _ternary(key, shape):
            return jax.random.randint(key, shape, -1, 2).astype(jnp.float32)
        b, s, h = x.shape
        xf = x.reshape(b * s, h)
        g = jnp.einsum('th,ih->ti', xf, gate_w) * gate_s
        u = jnp.einsum('th,ih->ti', xf, up_w) * up_s
        hdn = jax.nn.silu(g) * u
        out = jnp.einsum('ti,hi->th', hdn, down_w) * down_s
        return out.reshape(b, s, -1)

    def _L1_xattn_ref(hidden_states, encoder_hidden_states, Wq, Wk, Wv, Wo, gq, gk):
        import jax, jax.numpy as jnp
        import numpy as np
        EPS = 1e-05

        def rmsnorm(x, g, eps=EPS):
            var = jnp.mean(jnp.square(x), axis=-1, keepdims=True)
            return x * jax.lax.rsqrt(var + eps) * g
        B, Sq, _ = hidden_states.shape
        Skv = encoder_hidden_states.shape[1]
        D = gq.shape[0]
        H = Wq.shape[1] // D
        scale = 1.0 / np.sqrt(D)
        q = (hidden_states @ Wq).reshape(B, Sq, H, D)
        k = (encoder_hidden_states @ Wk).reshape(B, Skv, H, D)
        v = (encoder_hidden_states @ Wv).reshape(B, Skv, H, D)
        q = rmsnorm(q, gq)
        k = rmsnorm(k, gk)
        scores = jnp.einsum('bqhd,bkhd->bhqk', q, k) * scale
        attn = jax.nn.softmax(scores, axis=-1)
        out = jnp.einsum('bhqk,bkhd->bqhd', attn, v)
        out = out.reshape(B, Sq, H * D)
        return out @ Wo

    def _L1_ffn_ref(hidden_states, gate_w, expert_bias, w_gate, w_up, w_down, sw_gate, sw_up, sw_down):
        import jax, jax.numpy as jnp
        import numpy as np
        from jax import lax
        TOP_K = 4
        ROUTED_SCALING = 1.0
        RENORMALIZE = True

        def _swiglu_ffn(x, wg, wu, wd):
            return jax.nn.silu(x @ wg.T) * (x @ wu.T) @ wd.T
        orig_shape = hidden_states.shape
        H = orig_shape[-1]
        x = hidden_states.reshape(-1, H)
        T = x.shape[0]
        logits = x.astype(jnp.float32) @ gate_w.T
        scores = jax.nn.sigmoid(logits)
        _, topk_idx = lax.top_k(scores + expert_bias[None, :], TOP_K)
        topk_w = jnp.take_along_axis(scores, topk_idx, axis=-1)
        if RENORMALIZE:
            topk_w = topk_w / jnp.sum(topk_w, axis=-1, keepdims=True)
        topk_w = topk_w * ROUTED_SCALING
        E = gate_w.shape[0]
        combine = jnp.zeros((T, E), dtype=x.dtype).at[jnp.arange(T)[:, None], topk_idx].set(topk_w.astype(x.dtype))

        def step(acc, ws):
            wg, wu, wd, cw = ws
            return (acc + cw[:, None] * _swiglu_ffn(x, wg, wu, wd), None)
        routed, _ = lax.scan(step, jnp.zeros_like(x), (w_gate, w_up, w_down, combine.T))
        shared = _swiglu_ffn(x, sw_gate, sw_up, sw_down)
        return (routed + shared).reshape(orig_shape)

    def _L2_xattn_ref(x, y, Wq, bq, Wk, bk, Wv, bv, Wkv_dca, bkv_dca, qn_w, qn_b, kn_w, kn_b, kn_dca_w, kn_dca_b, Wo, bo):
        import jax, jax.numpy as jnp
        import numpy as np
        B, S1, S2, DCA = (2, 256, 128, 16)
        QDIM, KDIM, H = (256, 128, 16)
        HD = QDIM // H
        SCALE = HD ** (-0.5)
        EPS = 1e-06
        DCA_WEIGHT = 1.0

        def _ln(t, w, b):
            m = jnp.mean(t, axis=-1, keepdims=True)
            v = jnp.var(t, axis=-1, keepdims=True)
            return (t - m) * jax.lax.rsqrt(v + EPS) * w + b

        def _attn(q, k, v):
            s = jnp.einsum('bhqd,bhkd->bhqk', q, k) * SCALE
            p = jax.nn.softmax(s, axis=-1)
            return jnp.einsum('bhqk,bhkd->bhqd', p, v)
        b, s1, _ = x.shape
        y_dca = y[:, -DCA:, :]
        y_main = y[:, :-DCA, :]
        kv_dca = (y_dca @ Wkv_dca + bkv_dca).reshape(b, DCA, 2, H, HD)
        k_dca = _ln(kv_dca[:, :, 0], kn_dca_w, kn_dca_b)
        v_dca = kv_dca[:, :, 1]
        s2 = y_main.shape[1]
        q = _ln((x @ Wq + bq).reshape(b, s1, H, HD), qn_w, qn_b)
        kv = jnp.concatenate([y_main @ Wk + bk, y_main @ Wv + bv], axis=-1)
        kv = kv.reshape(b, s2, H, 2 * HD)
        k = _ln(kv[..., :HD], kn_w, kn_b)
        v = kv[..., HD:]
        qT = q.transpose(0, 2, 1, 3)
        ctx = _attn(qT, k.transpose(0, 2, 1, 3), v.transpose(0, 2, 1, 3))
        ctx = ctx.transpose(0, 2, 1, 3).reshape(b, s1, QDIM)
        ctx_dca = _attn(qT, k_dca.transpose(0, 2, 1, 3), v_dca.transpose(0, 2, 1, 3))
        ctx_dca = ctx_dca.transpose(0, 2, 1, 3).reshape(b, s1, QDIM)
        ctx = ctx + DCA_WEIGHT * ctx_dca
        return ctx @ Wo + bo

    def _L2_ffn_ref(x, router_w, w1, w2, w3):
        import jax, jax.numpy as jnp
        import numpy as np
        N_EXPERTS = 8
        TOP_K = 2
        D_MODEL = 256
        D_FF = 128
        BATCH, SEQ = (2, 256)

        def _trunc_normal(key, shape, fan_in):
            std = jnp.sqrt(1.0 / 3.0) / jnp.sqrt(float(fan_in))
            return jax.random.truncated_normal(key, -2.0, 2.0, shape, dtype=jnp.float32) * std
        B, S, D = x.shape
        xf = x.reshape(-1, D)
        n_tokens = xf.shape[0]
        logits = xf @ router_w.T
        topk_vals, topk_idx = jax.lax.top_k(logits, TOP_K)
        topk_weights = jax.nn.softmax(topk_vals, axis=-1)
        gate = jax.nn.silu(jnp.einsum('nd,edf->enf', xf, w1))
        value = jnp.einsum('nd,edf->enf', xf, w2)
        expert_out = jnp.einsum('enf,efd->end', gate * value, w3)
        tok = jnp.arange(n_tokens)[:, None]
        selected = expert_out[topk_idx, tok]
        out = jnp.sum(selected * topk_weights[..., None], axis=1)
        return out.reshape(B, S, D)

    def _L3_xattn_ref(x, gate_up_weight, down_weight):
        import jax, jax.numpy as jnp
        import numpy as np
        EPS = 1e-06
        QMAX = 127.0

        def _smooth_quant_linear(x, w):
            amax_x = jnp.max(jnp.abs(x), axis=0)
            amax_w = jnp.max(jnp.abs(w), axis=0)
            s = jnp.sqrt(jnp.maximum(amax_x, EPS) / jnp.maximum(amax_w, EPS))
            s = jnp.maximum(s, EPS)
            xs = x / s
            ws = w * s
            x_scale = jnp.maximum(jnp.max(jnp.abs(xs), axis=-1, keepdims=True), EPS) / QMAX
            w_scale = jnp.maximum(jnp.max(jnp.abs(ws), axis=-1, keepdims=True), EPS) / QMAX
            x_q = jnp.clip(jnp.round(xs / x_scale), -QMAX, QMAX)
            w_q = jnp.clip(jnp.round(ws / w_scale), -QMAX, QMAX)
            return x_q @ w_q.T * x_scale * w_scale.T

        def _expert_forward(xe, guw, dw):
            h = _smooth_quant_linear(xe, guw)
            gate, up = jnp.split(h, 2, axis=-1)
            a = jax.nn.silu(gate) * up
            return _smooth_quant_linear(a, dw)
        return jax.vmap(_expert_forward)(x, gate_up_weight, down_weight)

    def _L3_ffn_ref(x, W_r, b_r, W1, b1, W2, b2, position_ids, cache_position):
        import jax, jax.numpy as jnp
        import numpy as np
        B, S, D = (4, 512, 256)
        DFF = 4 * D
        CAPACITY = 0.125
        K = int(CAPACITY * S)
        b, s, d = x.shape
        weights = jnp.einsum('bsd,do->bso', x, W_r).squeeze(-1) + b_r
        topk_vals, topk_idx = jax.lax.top_k(weights, K)
        threshold = topk_vals[:, -1]
        sel_mask = weights > threshold[:, None]
        xg = jnp.take_along_axis(x, topk_idx[..., None], axis=1)
        h = jax.nn.gelu(jnp.einsum('bkd,df->bkf', xg, W1) + b1)
        blk = jnp.einsum('bkf,fd->bkd', h, W2) + b2
        gate = (topk_vals > threshold[:, None]).astype(x.dtype)
        wg = jnp.take_along_axis(weights, topk_idx, axis=1)
        vals = blk * (wg * gate)[..., None]
        bidx = jnp.arange(b)[:, None]
        processed = jnp.zeros_like(x).at[bidx, topk_idx].add(vals)
        return processed + x * (~sel_mask)[..., None].astype(x.dtype)
    x = x + jnp.tanh(g_xattn[0]) * _L0_xattn_ref(ctx_1024, _layernorm(x, axis=-1), L0_xattn_in_proj_w, L0_xattn_conv_w, L0_xattn_conv_b, L0_xattn_x_proj_w, L0_xattn_dt_proj_w, L0_xattn_dt_proj_b, L0_xattn_A_log, L0_xattn_D)
    x = x + jnp.tanh(g_ffn[0]) * _L0_ffn_ref(_layernorm(x, axis=-1), L0_ffn_gate_w, L0_ffn_up_w, L0_ffn_down_w, L0_ffn_gate_s, L0_ffn_up_s, L0_ffn_down_s)
    x = x + jnp.tanh(g_xattn[1]) * _L1_xattn_ref(_layernorm(x, axis=-1), ctx_1024, L1_xattn_Wq, L1_xattn_Wk, L1_xattn_Wv, L1_xattn_Wo, L1_xattn_gq, L1_xattn_gk)
    x = x + jnp.tanh(g_ffn[1]) * _L1_ffn_ref(_layernorm(x, axis=-1), L1_ffn_gate_w, L1_ffn_expert_bias, L1_ffn_w_gate, L1_ffn_w_up, L1_ffn_w_down, L1_ffn_sw_gate, L1_ffn_sw_up, L1_ffn_sw_down)
    x = x + jnp.tanh(g_xattn[2]) * _L2_xattn_ref(_layernorm(x, axis=-1), ctx_1024, L2_xattn_Wq, L2_xattn_bq, L2_xattn_Wk, L2_xattn_bk, L2_xattn_Wv, L2_xattn_bv, L2_xattn_Wkv_dca, L2_xattn_bkv_dca, L2_xattn_qn_w, L2_xattn_qn_b, L2_xattn_kn_w, L2_xattn_kn_b, L2_xattn_kn_dca_w, L2_xattn_kn_dca_b, L2_xattn_Wo, L2_xattn_bo)
    x = x + jnp.tanh(g_ffn[2]) * _L2_ffn_ref(_layernorm(x, axis=-1), L2_ffn_router_w, L2_ffn_w1, L2_ffn_w2, L2_ffn_w3)
    x = x + jnp.tanh(g_xattn[3]) * _L3_xattn_ref(_layernorm(x, axis=-1), fside_BxS2xS2_0, ctx_1024)
    x = x + jnp.tanh(g_ffn[3]) * _L3_ffn_ref(_layernorm(x, axis=-1), L3_ffn_W_r, L3_ffn_b_r, L3_ffn_W1, L3_ffn_b1, L3_ffn_W2, L3_ffn_b2, L3_ffn_position_ids, L3_ffn_cache_position)
    return x

_drawn_inputs = setup_inputs


def setup_inputs(seed=0):
    import zlib

    import numpy as np

    out = dict(_drawn_inputs(seed))
    spreads = {'L0_xattn_D': (1.0, 0.6),
     'L1_xattn_gq': (1.0, 0.2),
     'L1_xattn_gk': (1.0, 0.2),
     'L2_xattn_bq': (0.0, 0.278),
     'L2_xattn_bk': (0.0, 0.1),
     'L2_xattn_bv': (0.0, 0.1),
     'L2_xattn_bkv_dca': (0.0, 0.1),
     'L2_xattn_qn_w': (1.0, 0.557),
     'L2_xattn_qn_b': (0.0, 0.282),
     'L2_xattn_kn_w': (1.0, 0.6),
     'L2_xattn_kn_b': (0.0, 0.8),
     'L2_xattn_kn_dca_w': (1.0, 0.6),
     'L2_xattn_kn_dca_b': (0.0, 0.8),
     'L2_xattn_bo': (0.0, 0.1),
     'L3_ffn_b1': (0.0, 0.384),
     'L3_ffn_b2': (0.0, 0.1)}
    factors = {'g_ffn': 3.116,
     'L0_xattn_conv_b': 3.528,
     'L0_xattn_x_proj_w': 8.0,
     'L0_xattn_dt_proj_w': 8.0,
     'L0_xattn_dt_proj_b': 8.0,
     'L0_xattn_A_log': 8.0,
     'L1_ffn_expert_bias': 2.774,
     'L1_ffn_w_up': 2.696,
     'L1_ffn_w_down': 3.661}
    for name, (base, spread) in spreads.items():
        noise = np.random.default_rng([zlib.crc32(name.encode()), seed]).standard_normal(out[name].shape)
        drawn = base * np.exp(spread * noise) if base else spread * noise
        out[name] = jnp.asarray(drawn.astype(out[name].dtype))
    for name, factor in factors.items():
        out[name] = (out[name] * factor).astype(out[name].dtype)
    return out
```

```python
from contextlib import ExitStack

import concourse.bass as bass
from concourse import mybir
from concourse.alu_op_type import AluOpType as ALU

F32 = mybir.dt.float32
BF16 = mybir.dt.bfloat16
ACT = mybir.ActivationFunctionType
AX = mybir.AxisListType.X

P = 128
B, S, D = 4, 256, 256
T = B * S
NT = T // P
DC = D // P
C = 128
HALF = T // 2
F0 = 704
FB = [(f, min(P, F0 - f)) for f in range(0, F0, P)]
E1, E1K = 16, 4
E2, E2K = 8, 2
KEEP3 = 64
BIG = 3.0e38
LAYERS = range(8)


class Token:

    def __init__(self, sem, k, loop=None):
        self.sem, self.k, self.loop = sem, k, loop


class Loop:
    def __init__(self, number, n, base):
        self.number, self.n, self.base, self.i, self.now = number, n, base, None, {}


class Signals:

    START = 2048

    def __init__(self, nc, ctx, plan):
        self.nc, self.ctx, self.plan, self.found = nc, ctx, plan, {}
        self.sems, self.count, self.waited, self.last = {}, {}, {}, {}
        self.loop, self.loops = None, 0
        self.engines = {"pe": nc.tensor, "act": nc.scalar, "dve": nc.vector,
                        "pool": nc.gpsimd, "sp": nc.sync}
        for e in ("pe", "act", "dve", "pool"):
            self.sem(e)
            self.engines[e].sem_inc(self.sems[e], self.START)
            self.count[e] = self.START

    def sem(self, name):
        if name not in self.sems:
            self.sems[name] = self.ctx.enter_context(self.nc.semaphore("s_" + name))
            self.count[name] = 0
        return self.sems[name]

    def done(self, name, ins, label=None, by=1):
        ins.then_inc(self.sem(name), by)
        if self.loop is None:
            self.count[name] += by
            t = Token(name, self.count[name])
        else:
            now = self.loop.now
            now[name] = now.get(name, 0) + by
            t = Token(name, now[name], self.loop)
            if label:
                self.found["k", self.loop.number, label] = (name, now[name])
        if label:
            self.last[label] = t
        return t

    def relabel(self, label, other):
        t = self.last[label] = self.last[other]
        if self.loop is not None:
            self.found["k", self.loop.number, label] = (t.sem, t.k)
        return t

    def loaded(self, name, ins, label=None):
        return self.done("d_" + name, ins, label, 16)

    def before(self, label):
        found = self.plan.get(("k", self.loop.number, label))
        if found is None:
            assert not self.plan, label
            return None
        name, k = found
        return Token(name, k - self.gain(self.loop, name), self.loop)

    def latest(self, *labels):
        got = []
        for label in labels:
            t = self.last.get(label)
            if self.loop is not None and (t is None or t.loop is not self.loop) and (
                    not self.plan or ("k", self.loop.number, label) in self.plan):
                t = self.before(label)
            got.append(t)
        return got

    def gain(self, loop, name):
        return self.plan.get(("m", loop.number, name), 1)

    def wait(self, eng, *tokens):
        for t in tokens:
            if t is None:
                continue
            seen = self.waited.setdefault((eng, t.sem), {"const": 0, "loop": None})
            if t.loop is None:
                if t.k > seen["const"]:
                    self.engines[eng].wait_ge(self.sem(t.sem), t.k)
                    seen["const"] = t.k
                continue
            m, base = self.gain(t.loop, t.sem), t.loop.base.get(t.sem, 0)
            k = t.k
            if t.loop is self.loop:
                if seen["loop"] is None or k > seen["loop"]:
                    value = self.loop.i * m + (base + k)
                    self.engines[eng].wait_ge(self.sem(t.sem), value)
                    seen["loop"] = k
            else:
                v = base + (t.loop.n - 1) * m + k
                if v > seen["const"]:
                    self.engines[eng].wait_ge(self.sem(t.sem), v)
                    seen["const"] = v

    def repeat(self, n):
        return _Repeat(self, n)


class _Repeat:
    def __init__(self, sig, n):
        self.sig, self.n = sig, n

    def __enter__(self):
        s = self.sig
        s.loop = Loop(s.loops, self.n, dict(s.count))
        s.loops += 1
        for w in s.waited.values():
            w["loop"] = None
        self.fori = s.nc.Fori(0, self.n)
        s.loop.i = self.fori.__enter__()
        return s.loop.i

    def __exit__(self, *exc):
        s, loop = self.sig, self.sig.loop
        self.fori.__exit__(*exc)
        for name, m in loop.now.items():
            s.found["m", loop.number, name] = m
            s.count[name] = s.count.get(name, 0) + m * loop.n
        s.loop = None
        return False


def row_layout():
    at, rows = 0, {}
    for name, n in [("g", 8), ("down_s", D), ("bias1", E1), ("bq", D), ("bk", D), ("bv", D),
                    ("bdca", 2 * D), ("qn_w", 16), ("qn_b", 16), ("kn_w", 16), ("kn_b", 16),
                    ("kd_w", 16), ("kd_b", 16), ("bo", D), ("b2", D), ("b_r", 1), ("iota", P)]:
        rows[name] = (at, n)
        at += n
    return rows, at


ROWS, NROWS = row_layout()
COLS = {"gate_s": (0, 6), "up_s": (6, 6), "conv_w": (12, 8), "conv_b": (20, 2), "dt_b": (22, 2),
        "A_log": (24, 32), "Dp": (56, 2), "gq": (58, 1), "gk": (59, 1), "b1": (60, 8),
        "slot0": (68, 1)}
NCOLS = 69


class Core:

    def __init__(self, nc, ctx, io, plan):
        self.nc, self.io = nc, io
        self.s = Signals(nc, ctx, plan)

        def sb(name, shape, dt=F32):
            return ctx.enter_context(nc.sbuf_tensor(name, shape, dt))

        self.psum = ctx.enter_context(nc.psum_tensor("psum", [P, 8 * 512], F32))
        self.bank = [self.psum[:, b * 512:(b + 1) * 512] for b in range(8)]
        self.X = sb("X", [P, NT, D])
        self.xn = sb("xn", [P, NT, D])
        self.xT = sb("xT", [P, DC, T])
        self.cT = sb("cT", [P, T])
        self.ident = sb("ident", [P, P])
        self.rows = sb("rows", [P, NROWS])
        self.cols = sb("cols", [P, NCOLS])
        self.tg = sb("tg", [P, 8])
        self.stats = sb("stats", [P, NT, 6])
        self.mv = sb("mv", [P, NT, 2])
        self.rstd = sb("rstd", [P, NT])
        self.mhalf = sb("mhalf", [P, 128])
        self.phalf = sb("phalf", [P, 128])
        self.arena = sb("arena", [P, 34304])
        self.at = 0
        self.bank_free = [None] * 8

    def place(self, *shape, dt=F32):
        n = 1
        for d in shape:
            n *= d
        words = n if dt == F32 else (n + 1) // 2
        words += -words % 16
        v = self.arena[:, self.at:self.at + words]
        self.at += words
        assert self.at <= 34304, self.at
        if dt != F32:
            v = v.bitcast(dt)
        v = v[:, 0:n]
        if len(shape) == 2:
            v = v.rearrange("p (a b) -> p a b", a=shape[0])
        elif len(shape) == 3:
            v = v.rearrange("p (a b c) -> p a b c", a=shape[0], b=shape[1])
        elif len(shape) == 4:
            v = v.rearrange("p (a b c d) -> p a b c d", a=shape[0], b=shape[1], c=shape[2])
        return v

    def row(self, name):
        at, n = ROWS[name]
        return self.rows[:, at:at + n]

    def col(self, name, j=0):
        return self.cols[:, COLS[name][0] + j:COLS[name][0] + j + 1]

    def load_constants(self):
        nc, s, io = self.nc, self.s, self.io
        self.x_in = [s.loaded(f"x{h}", nc.sync.dma_start(
            self.X[:, 4 * h:4 * h + 4, :], io["x"][:, 4 * h:4 * h + 4, :])) for h in range(2)]
        self.ident_in = s.loaded("ident", nc.scalar.dma_start(self.ident[:, :], io["ident"]))
        self.rows_in = s.loaded("rows", nc.scalar.dma_start(
            self.rows[:, :], io["rows"].partition_broadcast(P)))
        self.cols_in = s.loaded("cols", nc.scalar.dma_start(self.cols[:, :], io["cols"]))
        self.ctx_in = s.loaded("cT", nc.sync.dma_start(self.cT[:, :], io["cT"]))
        nc.gpsimd.memset(self.mhalf[:, :], -0.5)
        self.halves = s.done("pool", nc.gpsimd.memset(self.phalf[:, :], 0.5))
        s.wait("act", self.rows_in)
        self.tg_done = s.done("act", nc.scalar.activation(self.tg[:, :], self.row("g"), ACT.Tanh))
        self.x_ready = list(self.x_in)
        s.wait("pe", self.ident_in)
        for e in ("dve", "pool"):
            s.wait(e, self.rows_in, self.cols_in, self.tg_done, self.halves)
        s.wait("act", self.cols_in)
        self.out = [None, None]

    def layernorm(self, readers=(), transpose=True):
        nc, s = self.nc, self.s
        s.wait("dve", *readers)
        s.wait("act", *readers)
        ready = []
        for h in range(2):
            tiles = range(4 * h, 4 * h + 4)
            s.wait("dve", self.x_ready[h])
            for t in tiles:
                st = s.done("dve", nc.vector.bn_stats(self.stats[:, t, :], self.X[:, t, :]))
            s.wait("dve", st)
            for t in tiles:
                ag = s.done("dve", nc.vector.bn_aggr(self.mv[:, t, :], self.stats[:, t, :]))
            s.wait("dve", ag)
            half = slice(4 * h, 4 * h + 4)
            ve = s.done("dve", nc.vector.tensor_scalar(self.rstd[:, half], self.mv[:, half, 1],
                                                       1e-5, None, ALU.add))
            s.wait("pool", ve)
            rs = s.done("pool", nc.gpsimd.tensor_tensor(self.rstd[:, half], self.rstd[:, half],
                                                        self.mhalf[:, 0:4], ALU.pow))
            s.wait("dve", rs)
            for j, t in enumerate(tiles):
                xn = s.done("dve", nc.vector.tensor_scalar(
                    self.xn[:, t, :], self.X[:, t, :], self.mv[:, t, 0:1], self.rstd[:, t:t + 1],
                    ALU.subtract, ALU.mult))
                if not transpose:
                    continue
                s.wait("pe", xn)
                for c in range(DC):
                    b = 2 * h + c
                    if j == 0:
                        s.wait("pe", self.bank_free[b])
                    tr = s.done("pe", nc.tensor.transpose(
                        self.bank[b][:, j * P:(j + 1) * P], self.xn[:, t, c * P:(c + 1) * P],
                        self.ident[:, :]))
            if not transpose:
                ready.append((xn,))
                continue
            s.wait("act", tr)
            s.wait("dve", tr)
            cols = slice(h * HALF, (h + 1) * HALF)
            a = s.done("act", nc.scalar.copy(self.xT[:, 0, cols], self.bank[2 * h][:, :]))
            v = s.done("dve", nc.vector.tensor_copy(self.xT[:, 1, cols], self.bank[2 * h + 1][:, :]))
            self.bank_free[2 * h], self.bank_free[2 * h + 1] = a, v
            ready.append((a, v))
        return ready

    def finish(self):
        nc, s = self.nc, self.s
        for h in range(2):
            s.wait("sp", self.x_ready[h])
            t = s.loaded("out", nc.sync.dma_start(self.io["out"][:, 4 * h:4 * h + 4, :],
                                                  self.X[:, 4 * h:4 * h + 4, :]))
        s.wait("sp", t)


def mamba(k, readers):
    nc, s = k.nc, k.s
    NI, NSTATE, RANK, W = 2, 16, 8, 4
    NBC = 2 * NSTATE
    k.at = 0
    Win = k.place(NI * P)
    Wx = k.place(NI, 3 * NBC + RANK)
    Wdt = k.place(NI * P)
    xp = k.place(NI, B, W - 1 + S)
    U, DT, DU, Y = k.place(NI, T), k.place(NI, T), k.place(NI, T), k.place(NI, T)
    V, E = k.place(NI, T), k.place(NI, T)
    A = k.place(NI, NSTATE)
    low = k.place(T)
    bcf = k.place(T)
    bc3 = k.place(T, dt=BF16)
    part = k.place(T, dt=BF16)
    sel = k.place(NBC, P, dt=BF16)
    row = k.place(NBC)
    gate = k.place(NT, S)
    dA, dBu = k.place(2, B, S), k.place(2, T)
    Hs, HC = k.place(2, T), k.place(2, T)
    bank = k.bank
    wi = s.loaded("mwi", nc.sync.dma_start(Win, k.io["in_proj"]))
    wx = s.loaded("mwx", nc.scalar.dma_start(Wx, k.io["x_proj"]))
    wd = s.loaded("mwd", nc.scalar.dma_start(Wdt[96:96 + RANK], k.io["dt_proj"]))
    nc.gpsimd.memset(dA[:, :, :, 0:1], 0.0)
    pads = s.done("pool", nc.gpsimd.memset(xp[:, :, :, 0:W - 1], 0.0))
    s.wait("pool", k.ident_in)
    ws = s.done("pool", nc.gpsimd.tensor_tensor(row, k.ident[:, 0:NBC], k.ident[:, NBC:2 * NBC], ALU.add))
    s.wait("pool", ws)
    ws = s.done("pool", nc.gpsimd.tensor_tensor(row, row, k.ident[:, 2 * NBC:3 * NBC], ALU.add))
    s.wait("pool", ws)
    ws = s.done("pool", nc.gpsimd.tensor_copy(sel, row.unsqueeze(2).broadcast_to([P, NBC, P])))
    s.wait("pe", k.ctx_in, wi)
    s.wait("act", pads)
    s.wait("dve", pads)
    for c in range(NI):
        for h in range(2):
            mm = nc.tensor.matmul(bank[2 * c + h], Win[:, c * P:(c + 1) * P],
                                  k.cT[:, h * HALF:(h + 1) * HALF], start=True, stop=True)
            pd = s.done("pe", mm)
            s.wait("act", pd)
            xi = s.done("act", nc.scalar.copy(xp[:, c, 2 * h:2 * h + 2, W - 1:],
                                              bank[2 * c + h].rearrange("p (b t) -> p b t", b=2)))
        s.wait("dve", xi)
        yv = Y[:, c, :].rearrange("p (b t) -> p b t", b=B)
        for w in range(W):
            tap, src = k.col("conv_w", c * W + w), xp[:, c, :, w:w + S]
            if w == 0:
                r = s.done("dve", nc.vector.tensor_scalar(yv, src, tap, None, ALU.mult))
            else:
                s.wait("dve", r)
                r = s.done("dve", nc.vector.scalar_tensor_tensor(yv, src, tap, yv, ALU.mult, ALU.add))
        s.wait("act", r)
        ui = s.done("act", nc.scalar.activation(U[:, c, :], Y[:, c, :], ACT.Silu, bias=k.col("conv_b", c)))
    z = k.layernorm(transpose=False)
    s.wait("act", *z[0], *z[1])
    gd = s.done("act", nc.scalar.activation(gate, k.xn[:, :, :], ACT.Silu))
    s.wait("pe", ui, wx)
    n96 = 3 * NBC
    for h in range(2):
        for c in range(NI):
            mm = nc.tensor.matmul(bank[4 + h][0:n96 + RANK, :], Wx[:, c, :],
                                  U[:, c, h * HALF:(h + 1) * HALF], start=c == 0, stop=c == NI - 1)
    xd = s.done("pe", mm)
    both = k.psum[:, 4 * 512:6 * 512]
    s.wait("act", xd)
    lo = s.done("act", nc.scalar.copy(low[96:96 + RANK], both[96:96 + RANK, :]))
    s.wait("dve", xd, lo)
    r = s.done("dve", nc.vector.tensor_copy(bc3[0:n96], both[0:n96, :]))
    s.wait("dve", r)
    r = s.done("dve", nc.vector.tensor_tensor(bcf[0:n96], both[0:n96, :], bc3[0:n96], ALU.subtract))
    s.wait("dve", r)
    r = s.done("dve", nc.vector.tensor_copy(part[0:n96], bcf[0:n96]))
    s.wait("dve", r)
    r1 = s.done("dve", nc.vector.tensor_copy(bc3[NBC:2 * NBC], part[NBC:2 * NBC]))
    r = s.done("dve", nc.vector.tensor_tensor(bcf[0:n96], bcf[0:n96], part[0:n96], ALU.subtract))
    s.wait("dve", r)
    split = s.done("dve", nc.vector.tensor_copy(bc3[2 * NBC:n96], bcf[2 * NBC:n96]))
    s.wait("pe", lo, wd)
    for c in range(NI):
        for h in range(2):
            mm = nc.tensor.matmul(bank[2 * c + h], Wdt[96:96 + RANK, c * P:(c + 1) * P],
                                  low[96:96 + RANK, h * HALF:(h + 1) * HALF], start=True, stop=True)
        vd = s.done("pe", mm)
        s.wait("act", vd)
        pv = k.psum[:, 2 * c * 512:(2 * c + 2) * 512]
        s.done("act", nc.scalar.activation(V[:, c, :], pv, ACT.Identity, bias=k.col("dt_b", c)))
        r = s.done("act", nc.scalar.activation(E[:, c, :], pv, ACT.Abs, bias=k.col("dt_b", c)))
        s.wait("act", r)
        e = s.done("act", nc.scalar.activation(E[:, c, :], E[:, c, :], ACT.Exp, scale=-1.0))
        s.wait("dve", e)
        w1 = s.done("dve", nc.vector.tensor_scalar(DT[:, c, :], E[:, c, :], 1.0, None, ALU.add))
        s.wait("act", w1)
        ln = s.done("act", nc.scalar.activation(DU[:, c, :], DT[:, c, :], ACT.Ln))
        s.wait("dve", ln)
        r = s.done("dve", nc.vector.tensor_scalar(DT[:, c, :], DT[:, c, :], -1.0, -1.0, ALU.add, ALU.mult))
        s.wait("dve", r)
        r = s.done("dve", nc.vector.tensor_tensor(E[:, c, :], E[:, c, :], DT[:, c, :], ALU.add))
        s.wait("dve", r)
        r = s.done("dve", nc.vector.tensor_tensor(E[:, c, :], E[:, c, :], DU[:, c, :], ALU.add))
        s.wait("dve", r)
        r = s.done("dve", nc.vector.scalar_tensor_tensor(DT[:, c, :], V[:, c, :], 0.0, E[:, c, :],
                                                         ALU.max, ALU.add))
        s.wait("dve", r, ui)
        r = s.done("dve", nc.vector.tensor_tensor(DU[:, c, :], DT[:, c, :], U[:, c, :], ALU.mult))
        s.wait("pool", ui, r)
        yd = s.done("pool", nc.gpsimd.tensor_scalar(Y[:, c, :], U[:, c, :], k.col("Dp", c), None, ALU.mult),
                    f"my{c}")
    al = COLS["A_log"][0]
    ex = s.done("act", nc.scalar.activation(A, k.cols[:, al:al + 32].rearrange("p (c n) -> p c n", c=2),
                                            ACT.Exp))
    s.wait("dve", ex)
    an = s.done("dve", nc.vector.tensor_scalar(A, A, -1.0, None, ALU.mult))
    s.wait("pe", split, ws, vd)
    s.wait("act", an, r)
    s.wait("dve", an)
    for e in ("pe", "act", "dve"):
        s.wait(e, yd, vd)

    def state(n, v):
        b0 = 4 * v
        s.wait("pe", *s.latest(f"mB{v}"))
        for row, b in ((n, b0), (n + NSTATE, b0 + 2)):
            if b == b0 + 2:
                s.wait("pe", *s.latest(f"mC{v}"))
            for h in range(2):
                mm = nc.tensor.matmul(bank[b + h], sel[0:n96, bass.ds(row, 1), :].rearrange("p a n -> p (a n)"),
                                      bc3[0:n96, h * HALF:(h + 1) * HALF], start=True, stop=True)
            rd = s.done("pe", mm)
        Bp, Cp = k.psum[:, b0 * 512:(b0 + 2) * 512], k.psum[:, (b0 + 2) * 512:(b0 + 4) * 512]
        for c in range(NI):
            s.wait("act", *s.latest(f"mscan{c}"))
            dtv = DT[:, c, :].rearrange("p (b t) -> p b t", b=B)
            ad = s.done("act", nc.scalar.activation(dA[:, c, :, 1:S], dtv[:, :, 1:S], ACT.Exp,
                                                    scale=A[:, c, bass.ds(n, 1)]))
            s.wait("dve", rd, *s.latest(f"mscan{c}"))
            r = s.done("dve", nc.vector.tensor_tensor(dBu[:, c, :], DU[:, c, :], Bp, ALU.mult), f"mB{v}")
            s.wait("dve", ad, r, *s.latest(f"mhc{c}"))
            r = s.done("dve", nc.vector.tensor_tensor_scan(
                Hs[:, c, :], dA[:, c].rearrange("p b t -> p (b t)"), dBu[:, c, :], 0.0, ALU.mult, ALU.add),
                f"mscan{c}")
            s.wait("dve", r, *s.latest(f"my{c}"))
            r = s.done("dve", nc.vector.tensor_tensor(HC[:, c, :], Hs[:, c, :], Cp, ALU.mult), f"mhc{c}")
            s.relabel(f"mC{v}", f"mhc{c}")
            s.wait("pool", r, *s.latest(f"my{c}"))
            s.done("pool", nc.gpsimd.tensor_tensor(Y[:, c, :], Y[:, c, :], HC[:, c, :], ALU.add), f"my{c}")

    with s.repeat(NSTATE // 2) as i:
        for v in range(2):
            state(i * 2 + v, v)
    tr = {}
    for c in range(NI):
        s.wait("dve", *s.latest(f"my{c}"), gd)
        g = s.done("dve", nc.vector.tensor_tensor(
            Y[:, c, :].rearrange("p (b t) -> p b t", b=B), Y[:, c, :].rearrange("p (b t) -> p b t", b=B),
            gate.rearrange("p (b c) t -> p b c t", c=NI)[:, :, c, :], ALU.mult))
        tr[c] = g
    s.wait("pe", *s.latest("mC0", "mC1"), tr[0], tr[1])
    for b in range(B):
        for j in range(2):
            for c in range(NI):
                mm = nc.tensor.transpose(bank[b][:, j * D + c * P:j * D + (c + 1) * P],
                                         Y[:, c, b * S + j * P:b * S + (j + 1) * P], k.ident[:, :])
        td = s.done("pe", mm)
        s.wait("dve", td)
        X2 = k.X[:, 2 * b:2 * b + 2, :]
        a = s.done("dve", nc.vector.scalar_tensor_tensor(
            X2, bank[b].rearrange("p (t d) -> p t d", t=2), k.tg[:, 0:1], X2, ALU.mult, ALU.add))
        k.bank_free[b] = a
        if b % 2:
            k.x_ready[b // 2] = a
    k.bank_free[4:] = [a] * 4
    return [td, a, *s.latest("my1"), gd]


def dense_ffn(k, readers):
    nc, s = k.nc, k.s
    k.at = 0
    nf = len(FB)
    gu = k.place(nf, 2, DC, P)
    down = k.place(nf, D)
    H = k.place(nf, T)
    G = k.place(2, HALF)
    Y = k.place(2, D)
    scale = k.place(D)
    s.wait("sp", *readers)
    w_in = [s.loaded("w0a", nc.sync.dma_start(gu[:, 0:1], k.io["gu0"][:, 0:1])),
            s.loaded("w0b", nc.sync.dma_start(gu[:, 1:nf], k.io["gu0"][:, 1:nf])),
            s.loaded("w0c", nc.sync.dma_start(down[:, :, :], k.io["down0"]))]
    ready = k.layernorm(readers)
    sc = s.done("dve", nc.vector.tensor_scalar(scale, k.row("down_s"), k.tg[:, 4:5], None, ALU.mult))
    free = k.bank_free
    n, muls, mul_done = 0, [], {}
    for h in range(2):
        cols = slice(h * HALF, (h + 1) * HALF)
        s.wait("pe", *ready[h], w_in[0])
        for f, (_, m) in enumerate(FB):
            if f == 1:
                s.wait("pe", w_in[1])
            g, u = 4 + n % 2 * 2, 5 + n % 2 * 2
            for b, which in ((g, 0), (u, 1)):
                s.wait("pe", free[b])
                for c in range(DC):
                    mm = nc.tensor.matmul(k.bank[b][0:m, :], gu[:, f, which, c, 0:m],
                                          k.xT[:, c, cols], start=c == 0, stop=c == DC - 1)
                if which == 0:
                    g_done = s.done("pe", mm)
            u_done = s.done("pe", mm)
            s.wait("act", g_done, muls[n - 2] if n >= 2 else None)
            si = s.done("act", nc.scalar.activation(G[0:m, n % 2, :], k.bank[g][0:m, :], ACT.Silu,
                                                    scale=k.col("gate_s", f)[0:m, :]))
            s.wait("dve", u_done, si)
            mu = s.done("dve", nc.vector.scalar_tensor_tensor(
                H[0:m, f, cols], k.bank[u][0:m, :], k.col("up_s", f)[0:m, :], G[0:m, n % 2, :],
                ALU.mult, ALU.mult))
            free[g], free[u] = si, mu
            muls.append(mu)
            n += 1
        mul_done[h] = muls[-1]
    s.wait("pe", w_in[2])
    added = []
    for t in range(NT):
        b = t % 4
        s.wait("pe", mul_done[t // 4], free[b])
        for f, (_, m) in enumerate(FB):
            mm = nc.tensor.matmul(k.bank[b][:, 0:D], H[0:m, f, t * P:(t + 1) * P], down[0:m, f, :],
                                  start=f == 0, stop=f == nf - 1)
        y_done = s.done("pe", mm)
        s.wait("dve", y_done, sc, added[t - 2] if t >= 2 else None)
        ys = s.done("dve", nc.vector.tensor_tensor(Y[:, t % 2, :], k.bank[b][:, 0:D], scale, ALU.mult))
        free[b] = ys
        s.wait("pool", ys)
        added.append(s.done("pool", nc.gpsimd.tensor_tensor(k.X[:, t, :], k.X[:, t, :],
                                                            Y[:, t % 2, :], ALU.add)))
    k.x_ready = [added[3], added[7]]
    return [y_done, added[-1]]


def top_mask(k, sel, ext, first, top, rep, mask, experts, keep):
    nc, s = k.nc, k.s
    s.wait("dve", first)
    for t in range(NT):
        mx = s.done("dve", nc.vector.max(top[:, t, :], ext[:, t, 0:experts]))
    s.wait("dve", mx)
    pads = s.done("dve", nc.vector.memset(top[:, :, keep:8], -BIG))
    s.wait("dve", pads)
    for t in range(NT):
        mr = s.done("dve", nc.vector.match_replace(rep[:, t, :], top[:, t, :], ext[:, t, :], BIG))
    s.wait("dve", mr)
    return s.done("dve", nc.vector.tensor_tensor(mask, rep[:, :, 0:experts], ext[:, :, 0:experts],
                                                 ALU.not_equal))


def moe(k, readers, tag, router, weights, experts, keep, gate, shared):
    nc, s = k.nc, k.s
    k.at = 0
    total = experts + shared
    W = k.place(2, 3, 256)
    wr = k.place(DC, experts)
    H = k.place(4, HALF)
    G = k.place(4, HALF)
    acc = k.place(NT, D)
    logits = k.place(NT, experts)
    score = k.place(NT, experts)
    ext = k.place(NT, experts + 8 - keep)
    rep = k.place(NT, experts + 8 - keep)
    top = k.place(NT, 8)
    ones = k.place(1)
    mask = k.place(NT, experts)
    cw = k.place(NT, experts)
    tot = k.place(NT)
    s.wait("sp", *readers)
    wr_in = s.loaded(tag + "wr", nc.sync.dma_start(wr[:, :, :], router))

    def load(slot, e):
        src = weights[bass.ds(e, 1)].rearrange("a p m n -> p (a m) n")
        return s.loaded(f"{tag}w{slot}", nc.sync.dma_start(W[:, slot, :, :], src), f"{tag}w{slot}")

    load(0, 0)
    load(1, 1)
    ready = k.layernorm(readers)
    s.wait("dve", *readers)
    s.wait("pool", *readers)
    cleared = s.done("pool", nc.gpsimd.memset(acc[:, :, :], 0.0))
    one = s.done("pool", nc.gpsimd.memset(ones, 1.0))
    padded = s.done("pool", nc.gpsimd.memset(ext[:, :, experts:experts + 8 - keep], -BIG))
    for h in range(2):
        s.wait("pe", *ready[h])
    s.wait("pe", wr_in, k.bank_free[7])
    for t in range(NT):
        for c in range(DC):
            mm = nc.tensor.matmul(k.bank[7][:, t * experts:(t + 1) * experts],
                                  k.xT[:, c, t * P:(t + 1) * P], wr[:, c, :],
                                  start=c == 0, stop=c == DC - 1)
    lg = s.done("pe", mm)
    lg_ps = k.bank[7][:, 0:NT * experts].rearrange("p (t e) -> p t e", t=NT)
    if tag == "m1":
        s.wait("act", lg)
        th = s.done("act", nc.scalar.activation(score[:, :, :], lg_ps, ACT.Tanh, scale=0.5))
        k.bank_free[7] = th
        s.wait("dve", th, padded)
        sg = s.done("dve", nc.vector.tensor_scalar(score, score, 0.5, 0.5, ALU.mult, ALU.add))
        s.wait("dve", sg)
        first = s.done("dve", nc.vector.tensor_tensor(
            ext[:, :, 0:experts], score, k.row("bias1").unsqueeze(1).broadcast_to([P, NT, experts]),
            ALU.add))
    else:
        s.wait("dve", lg, padded)
        first = s.done("dve", nc.vector.tensor_copy(ext[:, :, 0:experts], lg_ps))
        k.bank_free[7] = first
    mk = top_mask(k, None, ext, first, top, rep, mask, experts, keep)
    if tag == "m2":
        s.wait("dve", mk)
        d = s.done("dve", nc.vector.tensor_tensor(
            score, ext[:, :, 0:experts], top[:, :, 0:1].broadcast_to([P, NT, experts]), ALU.subtract))
        s.wait("act", d)
        ex = s.done("act", nc.scalar.activation(score[:, :, :], score[:, :, :], ACT.Exp))
        s.wait("dve", ex)
    s.wait("dve", mk)
    a = s.done("dve", nc.vector.tensor_tensor(cw, mask, score, ALU.mult))
    s.wait("dve", a)
    a = s.done("dve", nc.vector.tensor_reduce(tot, cw, AX, ALU.add))
    s.wait("dve", a)
    a = s.done("dve", nc.vector.reciprocal(tot, tot))
    s.wait("dve", a)
    a = s.done("dve", nc.vector.tensor_tensor(cw, cw, tot.unsqueeze(2).broadcast_to([P, NT, experts]),
                                              ALU.mult))
    s.wait("dve", a, cleared, one)

    def user(label, looped, same):
        if looped and not same:
            return s.before(label)
        return s.last.get(label)

    def gate_up(st, looped):
        r, slot, h = st % 4, st % 4 // 2, st % 2
        g, u, two = 2 * h, 2 * h + 1, (st + 2) % 4
        cols = slice(h * HALF, (h + 1) * HALF)
        s.wait("pe", user(f"{tag}w{slot}", looped, st == 4))
        s.wait("pe", user(f"{tag}silu{two}", looped, st >= 3))
        for c in range(DC):
            mm = nc.tensor.matmul(k.bank[g][:, :], W[:, slot, 0, c * P:(c + 1) * P], k.xT[:, c, cols],
                                  start=c == 0, stop=c == DC - 1)
        gd = s.done("pe", mm)
        s.wait("pe", user(f"{tag}mul{two}", looped, st >= 3))
        for c in range(DC):
            mm = nc.tensor.matmul(k.bank[u][:, :], W[:, slot, 1, c * P:(c + 1) * P], k.xT[:, c, cols],
                                  start=c == 0, stop=c == DC - 1)
        ud = s.done("pe", mm)
        s.wait("act", gd, user(f"{tag}mul{r}", looped, False))
        si = s.done("act", nc.scalar.activation(G[:, r, :], k.bank[g][:, :], ACT.Silu), f"{tag}silu{r}")
        s.wait("dve", ud, si, user(f"{tag}out{r}", looped, st == 4))
        s.done("dve", nc.vector.tensor_tensor(H[:, r, :], k.bank[u][:, :], G[:, r, :], ALU.mult),
               f"{tag}mul{r}")

    def down(st, looped, e):
        r, slot, h, two = st % 4, st % 4 // 2, st % 2, (st + 2) % 4
        s.wait("pe", user(f"{tag}mul{r}", looped, st >= 1))
        outs = []
        for j in range(4):
            b = 4 + 2 * h + j // 2
            if j % 2 == 0:
                s.wait("pe", user(f"{tag}acc{two}.{j + 1}", looped, st >= 2))
            mm = nc.tensor.matmul(k.bank[b][:, j % 2 * D:(j % 2 + 1) * D], H[:, r, j * P:(j + 1) * P],
                                  W[:, slot, 2, :], start=True, stop=True)
            if j % 2 == 1:
                outs.append(s.done("pe", mm, f"{tag}out{r}" if j == 3 else None))
        for j in range(4):
            t, b = 4 * h + j, 4 + 2 * h + j // 2
            w = ones if e is None else cw[:, t, bass.ds(e, 1)]
            s.wait("dve", outs[j // 2], user(f"{tag}acc{two}.{j}", looped, st >= 2))
            s.done("dve", nc.vector.scalar_tensor_tensor(
                acc[:, t, :], k.bank[b][:, j % 2 * D:(j % 2 + 1) * D], w, acc[:, t, :],
                ALU.mult, ALU.add), f"{tag}acc{r}.{j}")
        return outs[1]

    s.wait("pe", *[k.bank_free[b] for b in range(8)])
    s.wait("act", *[k.bank_free[b] for b in range(8)])
    pairs = total // 2 if shared else total // 2 - 1
    gate_up(0, False)
    s.wait("pe", s.last[f"{tag}mul0"])
    with s.repeat(pairs) as i:
        for st in range(4):
            gate_up(st + 1, True)
            od = down(st, True, i * 2 + st // 2)
            if st % 2 == 1:
                s.wait("sp", od)
                load(st // 2, i * 2 + 2 + st // 2)
    e = 2 * pairs
    if shared:
        gate_up(1, False)
        down(0, False, None)
        od = down(1, False, None)
    else:
        for st in range(4):
            if st < 3:
                gate_up(st + 1, False)
            od = down(st, False, e + st // 2)
    g = k.tg[:, gate:gate + 1]
    last = s.last[f"{tag}acc{1 if shared else 3}.3"]
    s.wait("dve", last)
    for t in range(NT):
        a = s.done("dve", nc.vector.scalar_tensor_tensor(k.X[:, t, :], acc[:, t, :], g, k.X[:, t, :],
                                                         ALU.mult, ALU.add))
        if t == 3:
            k.x_ready[0] = a
    k.x_ready[1] = a
    k.bank_free = [a] * 8
    return [od, a, s.last[f"{tag}silu{1 if shared else 3}"]] + [s.last[f"{tag}w{j}"] for j in range(2)]


def attention1(k, readers):
    nc, s = k.nc, k.s
    NH, HD = 16, P
    k.at = 0
    Wqkv = k.place(2, 512)
    Wo = k.place(2, D)
    Q, K = k.place(2, T), k.place(2, T)
    V, O = k.place(2, NT, HD), k.place(2, T)
    Kn = k.place(NT, HD)
    sq = k.place(2, NT, HD)
    ss = k.place(2, NT)
    rk = k.place(NT)
    rq = k.place(2, NT)
    Pr = k.place(2, 2, 2 * P)
    PT = k.place(2, 2, 2 * P)
    mx, nb, rs, ri = k.place(2, 2), k.place(2, 2), k.place(2, 2), k.place(2, 2)
    ones = k.place(1)
    s.wait("sp", *readers)
    bank = k.bank

    def load_qkv(slot, h):
        s.wait("sp", *s.latest(f"a1Quse{slot}"))
        s.loaded(f"a1qkv{slot}", nc.sync.dma_start(
            Wqkv[:, slot, :], k.io["qkv1"][bass.ds(h, 1)].rearrange("a p n -> p (a n)")), f"a1qkv{slot}")

    def load_o(slot, h):
        s.wait("sp", *s.latest("a1Ouse"))
        s.loaded(f"a1wo{slot}", nc.sync.dma_start(
            Wo[:, slot, :], k.io["wo1"][bass.ds(h, 1)].rearrange("a p n -> p (a n)")), f"a1wo{slot}")

    def keys_values(p):
        w = Wqkv[:, p, :]
        s.wait("pe", *s.latest(f"a1qkv{p}"))
        for half in range(2):
            b = 6 + half
            s.wait("pe", *s.latest(f"a1b{b}"))
            for j in range(4):
                mm = nc.tensor.matmul(bank[b][:, j * P:(j + 1) * P],
                                      k.cT[:, (4 * half + j) * P:(4 * half + j + 1) * P],
                                      w[:, 256:384], start=True, stop=True)
            kd = s.done("pe", mm)
            tl = slice(4 * half, 4 * half + 4)
            s.wait("act", kd, *s.latest("a1Kss"))
            a = s.done("act", nc.scalar.activation(sq[:, 0, tl, :], bank[b][:, :].rearrange("p (t d) -> p t d", t=4), ACT.Square))
            s.wait("dve", a, *s.latest("a1rk"))
            r = s.done("dve", nc.vector.tensor_reduce(ss[:, 0, tl], sq[:, 0, tl, :], AX, ALU.add))
            s.wait("dve", r)
            r = s.done("dve", nc.vector.tensor_scalar(ss[:, 0, tl], ss[:, 0, tl], 1.0 / HD, 1e-5,
                                                      ALU.mult, ALU.add), "a1Kss")
            s.wait("pool", r, *s.latest(f"a1Kn{half}"))
            r = s.done("pool", nc.gpsimd.tensor_tensor(rk[:, tl], ss[:, 0, tl], k.mhalf[:, 0:4], ALU.pow), "a1rk")
            s.wait("dve", r, *s.latest(f"a1Ktr{half}"))
            s.done("dve", nc.vector.tensor_tensor(
                Kn[:, tl, :], bank[b][:, :].rearrange("p (t d) -> p t d", t=4),
                rk[:, tl].unsqueeze(2).broadcast_to([P, 4, HD]), ALU.mult), f"a1Kn{half}")
            s.relabel(f"a1b{b}", f"a1Kn{half}")

    def values(p):
        w = Wqkv[:, p, :]
        for half in range(2):
            b = 6 + half
            s.wait("pe", *s.latest(f"a1b{b}"))
            for j in range(4):
                mm = nc.tensor.matmul(bank[b][:, j * P:(j + 1) * P],
                                      k.cT[:, (4 * half + j) * P:(4 * half + j + 1) * P],
                                      w[:, 384:512], start=True, stop=True)
            vd = s.done("pe", mm)
            s.wait("act", vd, *s.latest(f"a1V{p}"))
            s.done("act", nc.scalar.copy(V[:, p, 4 * half:4 * half + 4, :],
                                         bank[b][:, :].rearrange("p (t d) -> p t d", t=4)), f"a1b{b}")
            s.relabel(f"a1Vin{p}", f"a1b{b}")

    def queries(p, half):
        w = Wqkv[:, p, :]
        b = 6 + half
        cols = slice(half * HALF, (half + 1) * HALF)
        s.wait("pe", *s.latest(f"a1b{b}"))
        for c in range(DC):
            mm = nc.tensor.matmul(bank[b][:, :], w[:, c * P:(c + 1) * P], k.xT[:, c, cols],
                                  start=c == 0, stop=c == DC - 1)
        qd = s.done("pe", mm, f"a1Quse{p}")
        s.wait("act", qd, *s.latest("a1Qss", f"a1S{p}"))
        s.done("act", nc.scalar.activation(
            sq[:, 1, 4 * half:4 * half + 4, :], bank[b][:, :].rearrange("p (t d) -> p t d", t=4), ACT.Square), "a1Qsq")
        s.done("act", nc.scalar.activation(Q[:, p, cols], bank[b][:, :], ACT.Identity, scale=k.col("gq")),
               f"a1b{b}")
        s.relabel(f"a1Qin{p}", f"a1b{b}")

    def finish_projection(p):
        s.wait("pe", *s.latest("a1Qsq", "a1b6"))
        for t in range(NT):
            mm = nc.tensor.matmul(bank[6][:, t:t + 1], sq[:, 1, t, :], ones, start=True, stop=True)
        sd = s.done("pe", mm, "a1Qss")
        s.wait("dve", sd, *s.latest(f"a1Qrq"))
        r = s.done("dve", nc.vector.tensor_scalar(ss[:, 1, :], bank[6][:, 0:NT], HD * 1e-5, None,
                                                  ALU.add), "a1b6")
        s.wait("pool", r, *s.latest(f"a1E{p}"))
        r = s.done("pool", nc.gpsimd.tensor_tensor(rq[:, p, :], ss[:, 1, :], k.mhalf[:, 0:NT], ALU.pow), "a1Qrq")
        s.relabel(f"a1rq{p}", "a1Qrq")
        for half in (1, 0):
            b = 6 + half
            s.wait("pe", *s.latest(f"a1b{b}", f"a1Kn{half}"))
            for j in range(4):
                mm = nc.tensor.transpose(bank[b][:, j * P:(j + 1) * P], Kn[:, 4 * half + j, :], k.ident[:, :])
            td = s.done("pe", mm, f"a1Ktr{half}")
            s.wait("act", td, *s.latest(f"a1S{p}"))
            s.done("act", nc.scalar.activation(K[:, p, half * HALF:(half + 1) * HALF], bank[b][:, :],
                                               ACT.Identity, scale=k.col("gk")), f"a1b{b}")
            s.relabel(f"a1Kin{p}", f"a1b{b}")

    def scores(p, b):
        u = b % 2
        s.wait("pe", *s.latest(f"a1Kin{p}", f"a1Qin{p}", f"a1b{u}"))
        for j in range(2):
            mm = nc.tensor.matmul(bank[u][:, j * 256:(j + 1) * 256],
                                  Q[:, p, b * S + j * P:b * S + (j + 1) * P], K[:, p, b * S:(b + 1) * S],
                                  start=True, stop=True)
        sd = s.done("pe", mm, f"a1S{p}")
        s.wait("dve", sd, *s.latest(f"a1rq{p}", f"a1nb{u}", f"a1rs{u}"))
        r = s.done("dve", nc.vector.tensor_reduce(mx[:, u, :], bank[u][:, :].rearrange("p (t d) -> p t d", t=2),
                                                  AX, ALU.max))
        s.wait("dve", r)
        r = s.done("dve", nc.vector.scalar_tensor_tensor(nb[:, u, :], mx[:, u, :], -1.0,
                                                         rq[:, p, 2 * b:2 * b + 2], ALU.mult, ALU.mult))
        s.wait("act", r, *s.latest(f"a1T{u}"))
        for j in range(2):
            e = s.done("act", nc.scalar.activation(
                Pr[:, u, j, :], bank[u][:, j * 256:(j + 1) * 256], ACT.Exp, bias=nb[:, u, j:j + 1],
                scale=rq[:, p, 2 * b + j:2 * b + j + 1], accum_out=rs[:, u, j:j + 1]), f"a1b{u}")
        s.relabel(f"a1nb{u}", f"a1b{u}")
        s.relabel(f"a1E{p}", f"a1b{u}")
        s.wait("dve", e)
        r = s.done("dve", nc.vector.reciprocal(ri[:, u, :], rs[:, u, :]), f"a1rs{u}")
        s.wait("dve", r)
        for j in range(2):
            s.done("dve", nc.vector.tensor_scalar(Pr[:, u, j, :], Pr[:, u, j, :], ri[:, u, j:j + 1],
                                                  None, ALU.mult), f"a1Pn{u}")

    def transposed(p, b):
        u = b % 2
        s.wait("pe", *s.latest(f"a1Pn{u}", f"a1b{2 + u}"))
        for c in range(2):
            for j in range(2):
                mm = nc.tensor.transpose(bank[2 + u][:, c * 256 + j * P:c * 256 + (j + 1) * P],
                                         Pr[:, u, j, c * P:(c + 1) * P], k.ident[:, :])
        td = s.done("pe", mm, f"a1T{u}")
        eng, engine = ("dve", nc.vector.tensor_copy) if b % 2 else ("act", nc.scalar.copy)
        s.wait(eng, td, *s.latest(f"a1AV{u}"))
        s.done(eng, engine(PT[:, u, :, :], bank[2 + u][:, :].rearrange("p (t d) -> p t d", t=2)), f"a1b{2 + u}")

    def attend(p, b):
        u = b % 2
        s.wait("pe", *s.latest(f"a1b{2 + u}", f"a1Vin{p}", f"a1b{4 + u}"))
        for c in range(2):
            mm = nc.tensor.matmul(bank[4 + u][:, 0:S], V[:, p, 2 * b + c, :], PT[:, u, c, :],
                                  start=c == 0, stop=c == 1)
        od = s.done("pe", mm, f"a1AV{u}")
        s.relabel(f"a1V{p}", f"a1AV{u}")
        eng, engine = ("act", nc.scalar.copy) if b % 2 else ("dve", nc.vector.tensor_copy)
        s.wait(eng, od, *s.latest("a1Ouse"))
        s.done(eng, engine(O[:, p, b * S:(b + 1) * S], bank[4 + u][:, 0:S]), f"a1b{4 + u}")

    def project_out():
        for t2 in range(NT // 2):
            u = t2 % 2
            s.wait("pe", *s.latest("a1b4", "a1b5", "a1wo0", "a1wo1"))
            for j in range(2):
                t = 2 * t2 + j
                for p in range(2):
                    mm = nc.tensor.matmul(bank[4 + u][:, j * D:(j + 1) * D], O[:, p, t * P:(t + 1) * P],
                                          Wo[:, p, :], start=p == 0, stop=p == 1)
            md = s.done("pe", mm, "a1Ouse")
            s.wait("dve", md, *s.latest(f"a1X{t2}"))
            s.done("dve", nc.vector.scalar_tensor_tensor(
                k.X[:, 2 * t2:2 * t2 + 2, :], bank[4 + u][:, :].rearrange("p (t d) -> p t d", t=2),
                k.tg[:, 1:2], k.X[:, 2 * t2:2 * t2 + 2, :], ALU.mult, ALU.add), f"a1b{4 + u}")
            s.relabel(f"a1X{t2}", f"a1b{4 + u}")

    def head(p, follow):
        n = 1 - p
        scores(p, 0)
        scores(p, 1)
        if follow:
            keys_values(n)
        transposed(p, 0)
        scores(p, 2)
        if follow:
            values(n)
        attend(p, 0)
        transposed(p, 1)
        scores(p, 3)
        if follow:
            queries(n, 0)
        attend(p, 1)
        transposed(p, 2)
        if follow:
            queries(n, 1)
        attend(p, 2)
        transposed(p, 3)
        if follow:
            finish_projection(n)
        attend(p, 3)

    load_qkv(0, 0)
    load_qkv(1, 1)
    load_o(0, 0)
    load_o(1, 1)
    s.wait("pool", *readers)
    one = s.done("pool", nc.gpsimd.memset(ones, 1.0))
    ready = k.layernorm(readers)
    s.wait("pe", one, k.ctx_in, *ready[0], *ready[1], *k.bank_free)
    s.wait("act", *readers)
    s.wait("dve", *readers)
    keys_values(0)
    values(0)
    queries(0, 0)
    queries(0, 1)
    finish_projection(0)
    for e in ("pe", "act", "dve"):
        s.wait(e, *s.latest("a1Kin0", "a1Vin0", "a1Qin0", "a1rq0", "a1b6", "a1b7"))
    s.wait("pool", *s.latest("a1Kn1", "a1b6"))
    s.wait("sp", *s.latest("a1Quse0"))
    with s.repeat(NH // 2 - 1) as i:
        load_qkv(0, i * 2 + 2)
        head(0, True)
        load_qkv(1, i * 2 + 3)
        head(1, True)
        project_out()
        load_o(0, i * 2 + 2)
        load_o(1, i * 2 + 3)
    head(0, True)
    head(1, False)
    project_out()
    k.x_ready = [s.last["a1X1"], s.last["a1X3"]]
    k.bank_free = [s.last[f"a1b{b}"] for b in range(8)]
    return [s.last[n] for n in ("a1Ouse", "a1X3", "a1b0", "a1b1", "a1b4", "a1b5", "a1b6", "a1b7", "a1rq1")]


def attention2(k, readers):
    nc, s = k.nc, k.s
    NH, HD, KM = 16, 16, S - 16
    SCALE = HD ** -0.5
    k.at = 0
    Wq, Wo = k.place(DC, D), k.place(DC, D)
    Wkv = k.place(4, D)
    bias = k.place(6, D)
    ind = k.place(3, P)
    sets = k.place(2, T)
    Kn, Qn = k.place(NT, NH, 32), k.place(NT, NH, 32)
    V = k.place(NT, NH, 32)
    KT, QT = k.place(4, T), k.place(4, T)
    xc, sq = k.place(2, 2 * NH, HD), k.place(2, 2 * NH, HD)
    su, va, rt = k.place(2, 2 * NH), k.place(2, 2 * NH), k.place(2, 2 * NH)
    aff = k.place(6)
    s.wait("sp", *readers)
    l1 = s.loaded("a2w", nc.sync.dma_start(Wkv, k.io["wkv2"]))
    l2 = s.loaded("a2b", nc.sync.dma_start(bias[0:2], k.io["bias2"]))
    l3 = s.loaded("a2i", nc.sync.dma_start(ind[0:2], k.io["ind2"]))
    l4 = s.loaded("a2q", nc.sync.dma_start(Wq, k.io["wq2"]))
    l5 = s.loaded("a2o", nc.sync.dma_start(Wo, k.io["wo2"]))
    l6 = s.loaded("a2a", nc.sync.dma_start(aff, k.io["aff2"]))
    s.wait("pool", *readers, k.ctx_in)
    zero = s.done("pool", nc.gpsimd.memset(sets[:, :, :], 0.0))
    nc.gpsimd.memset(Kn, 0.0)
    nc.gpsimd.memset(Qn, 0.0)
    zeros = s.done("pool", nc.gpsimd.memset(V, 0.0))
    s.wait("pool", zero)
    by_batch = k.cT[:, :].rearrange("p (b t) -> p b t", b=B)
    for n, keys in ((0, slice(0, KM)), (1, slice(KM, S))):
        split = s.done("pool", nc.gpsimd.tensor_copy(
            sets[:, n, :].rearrange("p (b t) -> p b t", b=B)[:, :, keys], by_batch[:, :, keys]))
    ready = k.layernorm(readers)
    s.wait("pe", split, l1, l2, l3, *k.bank_free)
    s.wait("act", zeros, l6, *readers, *k.bank_free)
    s.wait("dve", zeros, *readers, *k.bank_free)

    def project(out, terms):
        for n, (l, r) in enumerate(terms):
            mm = nc.tensor.matmul(out, l, r, start=n == 0, stop=n == len(terms) - 1)
        return mm

    def norm_heads(b, tiles, out, n):
        u = n % 2
        v = k.bank[b].rearrange("p (h d) -> p h d", d=HD)
        xv, sv = xc[:, u], sq[:, u]
        s.wait("dve", *s.latest(f"a2va{u}", f"a2rt{u}"))
        r = s.done("dve", nc.vector.tensor_reduce(su[:, u, :], v, AX, ALU.add))
        s.wait("dve", r)
        r = s.done("dve", nc.vector.tensor_scalar(su[:, u, :], su[:, u, :], 1.0 / HD, None, ALU.mult))
        s.wait("dve", r)
        r = s.done("dve", nc.vector.tensor_tensor(
            xv, v, su[:, u, :].unsqueeze(2).broadcast_to([P, 2 * NH, HD]), ALU.subtract), f"a2b{b}")
        s.wait("act", r)
        q = s.done("act", nc.scalar.activation(sv, xv, ACT.Square))
        s.wait("dve", q)
        r = s.done("dve", nc.vector.tensor_reduce(va[:, u, :], sv, AX, ALU.add))
        s.wait("dve", r)
        r = s.done("dve", nc.vector.tensor_scalar(va[:, u, :], va[:, u, :], 1.0 / HD, 1e-6,
                                                  ALU.mult, ALU.add))
        s.wait("pool", r)
        r = s.done("pool", nc.gpsimd.tensor_tensor(rt[:, u, :], va[:, u, :], k.mhalf[:, 0:2 * NH],
                                                   ALU.pow), f"a2va{u}")
        s.wait("dve", r)
        return s.done("dve", nc.vector.tensor_tensor(
            out[:, tiles, :, 0:HD].rearrange("p t h d -> p (t h) d"), xv,
            rt[:, u, :].unsqueeze(2).broadcast_to([P, 2 * NH, HD]), ALU.mult), f"a2rt{u}")

    def affine(dst, src, n):
        return nc.scalar.activation(dst, src, ACT.Identity, scale=aff[:, n:n + 1],
                                    bias=aff[:, n + 1:n + 2])

    n, kn, qn, vin = 0, [], [], None
    for b in range(B):
        bk, bv = 4 * (b % 2), 4 * (b % 2) + 1
        s.wait("pe", *s.latest(f"a2b{bk}", f"a2b{bv}", f"a2b{bv + 1}"))
        for j in range(2):
            t = 2 * b + j
            c = slice(t * P, (t + 1) * P)
            o = slice(j * D, (j + 1) * D)
            main = [(sets[:, 0, c], Wkv[:, 0, :]), (ind[0:2, j, :], bias[0:2, 0, :])]
            mm = project(k.bank[bk][:, o], main + [(sets[:, 1, c], Wkv[:, 2, :])] * j)
        kd = s.done("pe", mm)
        for j in range(2):
            t = 2 * b + j
            c = slice(t * P, (t + 1) * P)
            o = slice(j * D, (j + 1) * D)
            mm = project(k.bank[bv][:, o], [(sets[:, 0, c], Wkv[:, 1, :]),
                                            (ind[0:2, j, :], bias[0:2, 1, :])])
        mm = project(k.bank[bv + 1][:, 0:D], [(sets[:, 1, c], Wkv[:, 3, :]),
                                              (ind[0:2, 1, :], bias[0:2, 2, :])])
        vd = s.done("pe", mm)
        s.wait("act", vd)
        s.done("act", nc.scalar.copy(
            V[:, 2 * b:2 * b + 2, :, 0:HD].rearrange("p t h d -> p (t h) d"),
            k.bank[bv].rearrange("p (h d) -> p h d", d=HD)), f"a2b{bv}")
        vin = s.done("act", nc.scalar.copy(
            V[:, 2 * b + 1, :, HD:32], k.bank[bv + 1][:, 0:D].rearrange("p (h d) -> p h d", d=HD)),
            f"a2b{bv + 1}")
        s.wait("dve", kd)
        kn.append(norm_heads(bk, slice(2 * b, 2 * b + 2), Kn, n))
        n += 1
    s.wait("pe", l4, *ready[0], *ready[1])
    for b in range(B):
        bq = 3 if b % 2 == 0 else 7
        s.wait("pe", *s.latest(f"a2b{bq}"))
        for j in range(2):
            t = 2 * b + j
            mm = project(k.bank[bq][:, j * D:(j + 1) * D],
                         [(k.xT[:, c, t * P:(t + 1) * P], Wq[:, c, :]) for c in range(DC)]
                         + [(ind[0:1, 2, :], bias[0:1, 3, :])])
        qd = s.done("pe", mm)
        s.wait("dve", qd)
        qn.append(norm_heads(bq, slice(2 * b, 2 * b + 2), Qn, n))
        n += 1
    m = 0
    for src, dst, done in ((Kn, KT, kn), (Qn, QT, qn)):
        for half in range(2):
            for g in range(4):
                bb = (0, 1, 2, 4)[m % 4]
                m += 1
                s.wait("pe", done[2 * half + 1], *s.latest(f"a2b{bb}"))
                for j in range(4):
                    mm = nc.tensor.transpose(k.bank[bb][:, j * P:(j + 1) * P],
                                             src[:, 4 * half + j, 4 * g:4 * g + 4, :].rearrange(
                                                 "p h d -> p (h d)"), k.ident[:, :])
                td = s.done("pe", mm)
                s.wait("act", td)
                cols = slice(half * HALF, (half + 1) * HALF)
                if src is Qn:
                    s.done("act", affine(dst[:, g, cols], k.bank[bb], 0), f"a2b{bb}")
                else:
                    dv = dst[:, g, cols].rearrange("p (b t) -> p b t", b=2)
                    bv = k.bank[bb].rearrange("p (b t) -> p b t", b=2)
                    s.done("act", affine(dv[:, :, 0:KM], bv[:, :, 0:KM], 2), f"a2b{bb}")
                    s.done("act", affine(dv[:, :, KM:S], bv[:, :, KM:S], 4), f"a2b{bb}")
    made = s.last[f"a2b{bb}"]

    Qb = Kn[:, 0:2].rearrange("p t h d -> p (t h d)").rearrange("p (g t) -> p g t", g=4)
    Kb = Qn[:, 0:2].rearrange("p t h d -> p (t h d)").rearrange("p (g t) -> p g t", g=4)
    Pr = k.place(2, 4, S)
    PT = k.place(2, 2, S)
    mx, nb = k.place(2, 4), k.place(2, 4)
    mxd = k.place(2, 4)
    sums = k.place(2, NH, 2)
    inv = k.place(2, NH, 2)
    Ob = k.place(2, NH, HD)
    Od = k.place(2, NH, HD)
    OT = k.place(DC, S)
    s.wait("pe", made, vin, l5)
    s.wait("dve", made, vin)
    s.wait("pool", made)
    s.wait("act", made, *s.latest("a2b3", "a2b7"))
    for b in range(8):
        s.last.pop(f"a2b{b}", None)

    def scores(g2):
        u, h0 = g2 % 2, 2 * g2
        s.wait("pe", *s.latest(f"a2E{u}", "a2Qb"))
        for h in (h0, h0 + 1):
            g, r = h // 4, h % 4 * 32
            for j in range(2):
                mm = nc.tensor.matmul(
                    k.bank[2 * u + h % 2][:, j * S:(j + 1) * S], Qb[r:r + HD, g, j * P:(j + 1) * P],
                    Kb[r:r + HD, g, :], start=True, stop=True)
        sd = s.done("pe", mm, "a2Qbuse")
        v = k.psum[:, 2 * u * 512:(2 * u + 2) * 512].rearrange("p (a t) -> p a t", t=S)
        pr = Pr[:, u]
        s.wait("dve", sd, *s.latest(f"a2T{u}", f"a2E{u}"))
        r1 = s.done("dve", nc.vector.tensor_reduce(mxd[:, u, :], v[:, :, KM:S], AX, ALU.max))
        r = s.done("dve", nc.vector.tensor_reduce(mx[:, u, :], v[:, :, 0:KM], AX, ALU.max))
        s.wait("dve", r1)
        r2 = s.done("dve", nc.vector.tensor_tensor(
            pr[:, :, KM:S], v[:, :, KM:S], mxd[:, u, :].unsqueeze(2).broadcast_to([P, 4, S - KM]),
            ALU.subtract))
        s.wait("dve", r)
        r = s.done("dve", nc.vector.tensor_scalar(nb[:, u, :], mx[:, u, :], -SCALE, None, ALU.mult))
        s.wait("act", r, *s.latest("a2inv"))
        for a in range(4):
            s.done("act", nc.scalar.activation(pr[:, a, 0:KM], v[:, a, 0:KM], ACT.Exp, bias=nb[:, u, a:a + 1],
                                               scale=SCALE, accum_out=sums[:, a % 2, h0 + a // 2, 0:1]))
        e = s.done("act", nc.scalar.activation(pr[:, :, KM:S], pr[:, :, KM:S], ACT.Exp, scale=SCALE),
                   f"a2E{u}")
        s.wait("dve", e)
        s.done("dve", nc.vector.tensor_reduce(
            sums[:, :, h0:h0 + 2, 1].rearrange("p j h -> p h j"),
            pr[:, :, KM:S].rearrange("p (h j) t -> p h j t", h=2), AX, ALU.add), "a2sum")

    def transposed(h):
        u, w = h // 2 % 2, h % 2
        s.wait("pe", *s.latest(f"a2E{u}", f"a2PT{w}"))
        for c in range(2):
            for j in range(2):
                mm = nc.tensor.transpose(k.bank[4 + w][:, c * S + j * P:c * S + (j + 1) * P],
                                         Pr[:, u, 2 * w + j, c * P:(c + 1) * P], k.ident[:, :])
        td = s.done("pe", mm, f"a2T{u}")
        eng, engine = ("dve", nc.vector.tensor_copy) if w else ("act", nc.scalar.copy)
        s.wait(eng, td, *s.latest(f"a2AV{w}"))
        s.done(eng, engine(PT[:, w, :, :], k.bank[4 + w].rearrange("p (t d) -> p t d", t=2)), f"a2PT{w}")

    def attend(h):
        w = h % 2
        s.wait("pe", *s.latest(f"a2PT{w}", "a2O"))
        for j in range(2):
            for c in range(2):
                mm = nc.tensor.matmul(
                    k.bank[6 + j][:, h * 32:(h + 1) * 32], PT[:, w, c, j * P:(j + 1) * P],
                    V[:, bass.ds(it * 2 + c, 1), h, :].rearrange("p a d -> p (a d)"),
                    start=c == 0, stop=c == 1)
        return s.done("pe", mm, f"a2AV{w}")

    with s.repeat(B) as it:
        s.wait("pool", *s.latest("a2Qbuse"))
        nc.gpsimd.tensor_copy(Kb, KT[:, :, bass.ds(it * S, S)])
        s.done("pool", nc.gpsimd.tensor_copy(Qb, QT[:, :, bass.ds(it * S, S)]), "a2Qb")
        for g2 in range(NH // 2 + 1):
            if g2 < NH // 2:
                scores(g2)
            if g2 >= 1:
                h = 2 * (g2 - 1)
                transposed(h)
                transposed(h + 1)
                attend(h)
                ad = attend(h + 1)
        s.wait("dve", *s.latest("a2sum", "a2OTr"))
        r = s.done("dve", nc.vector.reciprocal(inv, sums), "a2inv")
        s.wait("dve", r, ad)
        o = k.psum[:, 6 * 512:8 * 512].rearrange("p (h e d) -> p h e d", e=2, d=HD)
        iv = inv.rearrange("p j h e -> p (j h) e")
        full = [P, 2 * NH, HD]
        for e, dst in ((0, Ob), (1, Od)):
            r = s.done("dve", nc.vector.tensor_tensor(
                dst.rearrange("p j h d -> p (j h) d"), o[:, :, e, :],
                iv[:, :, e].unsqueeze(2).broadcast_to(full), ALU.mult), "a2O")
        s.wait("dve", r)
        r = s.done("dve", nc.vector.tensor_tensor(Ob, Ob, Od, ALU.add))
        s.wait("pe", r, *s.latest("a2PT0", "a2PT1"))
        for c in range(DC):
            for j in range(2):
                mm = nc.tensor.transpose(
                    k.bank[4][:, c * S + j * P:c * S + (j + 1) * P],
                    Ob[:, j].rearrange("p h d -> p (h d)")[:, c * P:(c + 1) * P], k.ident[:, :])
        td = s.done("pe", mm, "a2OTr")
        s.wait("act", td)
        oc = s.done("act", nc.scalar.copy(OT, k.bank[4].rearrange("p (c t) -> p c t", c=DC)), "a2PT0")
        s.wait("pe", oc)
        for j in range(2):
            mm = project(k.bank[5][:, j * D:(j + 1) * D],
                         [(OT[:, c, j * P:(j + 1) * P], Wo[:, c, :]) for c in range(DC)]
                         + [(ind[0:1, 2, :], bias[0:1, 4, :])])
        yd = s.done("pe", mm)
        s.wait("dve", yd)
        X2 = k.X[:, bass.ds(it * 2, 2), :]
        s.done("dve", nc.vector.scalar_tensor_tensor(
            X2, k.bank[5].rearrange("p (t d) -> p t d", t=2), k.tg[:, 2:3], X2, ALU.mult, ALU.add), "a2PT1")
    k.x_ready = [s.last["a2PT1"]] * 2
    k.bank_free = [s.last["a2PT1"]] * 8
    return [yd, s.last["a2PT1"], s.last["a2E0"], s.last["a2E1"], s.last["a2PT0"], s.last["a2Qb"]]


def quantised_layer(k, readers):
    nc, s = k.nc, k.s
    EPS, QMAX, MAGIC = 1e-6, 127.0, 1.5 * 2.0 ** 23
    k.at = 0
    bank = k.bank
    w1 = k.place(NT, D)
    w1T = k.place(DC, T)
    w2 = k.place(NT, C)
    XS, WS = k.place(NT, D), k.place(NT, D)
    XQ, WQ = k.place(NT, D, dt=BF16), k.place(NT, D, dt=BF16)
    XQT, WQT = k.place(DC, T, dt=BF16), k.place(DC, T, dt=BF16)
    diag = k.place(8, P)
    sB = k.place(NT, P)
    hid, act = k.place(NT, D), k.place(NT, P)
    ones = k.place(P)
    identb = k.place(P, dt=BF16)
    small = k.place(16, 8)
    s.wait("sp", *readers)
    lw = [s.loaded("q1", nc.sync.dma_start(w1, k.io["fside"])),
          s.loaded("q1T", nc.sync.dma_start(w1T, k.io["fsideT"])),
          s.loaded("q2", nc.sync.dma_start(w2, k.io["ctok"]))]
    s.wait("pool", *readers)
    ready = k.layernorm(readers)
    s.wait("pool", k.ident_in)
    nc.gpsimd.memset(ones, 1.0)
    cst = s.done("pool", nc.gpsimd.tensor_copy(identb, k.ident[:, :]))
    for e in ("dve", "act", "pe", "pool"):
        s.wait(e, *readers, *lw, cst, *ready[0], *ready[1], *k.bank_free)

    def dve(ins):
        t = s.done("dve", ins)
        s.wait("dve", t)
        return t

    def rows_of(cols, b0):
        t = dve(nc.vector.tensor_tensor(diag, k.ident[:, :].unsqueeze(1).broadcast_to([P, 8, P]),
                                        cols.unsqueeze(2).broadcast_to([P, 8, P]), ALU.mult))
        s.wait("pe", t)
        dv = diag.rearrange("p a b -> p (a b)")
        for h in range(2):
            mm = nc.tensor.matmul(bank[b0 + h], ones, dv[:, h * 512:(h + 1) * 512], start=True, stop=True)
        t = s.done("pe", mm)
        s.wait("dve", t)
        s.wait("act", t)
        return k.psum[:, b0 * 512:(b0 + 2) * 512]

    def quantise(v, q, scale, inv, n):
        dve(nc.vector.tensor_reduce(scale, v, AX, ALU.max, apply_absolute_value=True))
        dve(nc.vector.tensor_scalar(scale, scale, EPS, 1.0 / QMAX, ALU.max, ALU.mult))
        dve(nc.vector.reciprocal(inv, scale))
        for t in range(NT):
            d = s.done("dve", nc.vector.tensor_scalar(v[:, t, :], v[:, t, :], inv[:, t:t + 1], MAGIC,
                                                      ALU.mult, ALU.add))
        s.wait("dve", d)
        dve(nc.vector.tensor_scalar(v, v, MAGIC + QMAX, MAGIC - QMAX, ALU.min, ALU.max))
        return dve(nc.vector.tensor_scalar(q, v, MAGIC, None, ALU.subtract))

    def linear(x_tok, x_feat, w_rows, w_feat, nd, evacuate):
        ax, aw, sm, rs = (small[:, j, 0:nd * B] for j in range(4))
        xsc, wsc, xin, win = (small[:, j, :] for j in range(4, 8))
        F = nd * P
        dve(nc.vector.tensor_reduce(ax, x_feat, AX, ALU.max, apply_absolute_value=True))
        dve(nc.vector.tensor_reduce(aw, w_feat, AX, ALU.max, apply_absolute_value=True))
        dve(nc.vector.tensor_scalar(ax, ax, EPS, None, ALU.max))
        dve(nc.vector.tensor_scalar(aw, aw, EPS, None, ALU.max))
        dve(nc.vector.reciprocal(aw, aw))
        t = dve(nc.vector.tensor_tensor(sm, ax, aw, ALU.mult))
        s.wait("pool", t)
        t = s.done("pool", nc.gpsimd.tensor_tensor(sm, sm, k.phalf[:, 0:nd * B], ALU.pow))
        s.wait("dve", t)
        dve(nc.vector.tensor_scalar(sm, sm, EPS, None, ALU.max))
        dve(nc.vector.reciprocal(rs, sm))

        def scaled(dst, src, cols, b0):
            if nd == 2:
                both = small[:, 8 + b0 // 2, :].rearrange("p (b c) -> p b c", c=nd)
                dve(nc.vector.tensor_copy(both, cols.rearrange("p (c b) -> p b c", c=nd)))
                cols = small[:, 8 + b0 // 2, :]
            else:
                both = small[:, 8 + b0 // 2, :]
                dve(nc.vector.memset(both, 0.0))
                dve(nc.vector.tensor_copy(both[:, 0:B], cols))
                cols = both
            r = rows_of(cols, b0)[:, 0:B * F].rearrange("p (b f) -> p b f", b=B)
            return dve(nc.vector.tensor_tensor(
                dst.rearrange("p (b j) f -> p b j f", b=B), src.rearrange("p (b j) f -> p b j f", b=B),
                r.unsqueeze(2).broadcast_to([P, B, 2, F]), ALU.mult))

        xs, ws = XS[:, :, 0:F], WS[:, :, 0:F]
        xq, wq = XQ[:, :, 0:F], WQ[:, :, 0:F]
        scaled(xs, x_tok, rs, 0)
        tq = quantise(xs, xq, xsc, xin, F)
        scaled(ws, w_rows, sm, 2)
        tw = quantise(ws, wq, wsc, win, F)
        n = 0
        for src, dst, ready_q in ((xq, XQT, tq), (wq, WQT, tw)):
            s.wait("pe", ready_q)
            for c in range(nd):
                bb = 4 + n % 2
                n += 1
                s.wait("pe", s.last.get(f"qb{bb}"))
                half = bank[bb].bitcast(BF16)
                for t in range(NT):
                    mm = nc.tensor.transpose(half[:, t * P:(t + 1) * P], src[:, t, c * P:(c + 1) * P],
                                             identb)
                td = s.done("pe", mm)
                s.wait("act", td)
                s.done("act", nc.scalar.copy(dst[:, c, :], half), f"qb{bb}")
        wr = rows_of(wsc, 0)
        tr = dve(nc.vector.tensor_copy(sB.rearrange("p t d -> p (t d)"), wr))
        s.wait("pe", s.last["qb4"], s.last["qb5"])
        for b in range(B):
            for j in range(2):
                t, bb = 2 * b + j, 4 + b % 4
                if j == 0:
                    s.wait("pe", s.last.get(f"qo{bb}"))
                for c in range(nd):
                    mm = nc.tensor.matmul(bank[bb][:, j * D:(j + 1) * D], XQT[:, c, t * P:(t + 1) * P],
                                          WQT[:, c, b * D:(b + 1) * D], start=c == 0, stop=c == nd - 1)
            td = s.done("pe", mm)
            s.wait("dve", td)
            for j in range(2):
                t = 2 * b + j
                r = s.done("dve", nc.vector.scalar_tensor_tensor(
                    hid[:, t, :], bank[bb][:, j * D:(j + 1) * D], xsc[:, t:t + 1],
                    sB[:, 2 * b:2 * b + 2, :].rearrange("p t d -> p (t d)"), ALU.mult, ALU.mult),
                    f"qo{bb}")
            evacuate(b, r)

    def gated(b, r):
        s.wait("act", r)
        tiles = slice(2 * b, 2 * b + 2)
        g = s.done("act", nc.scalar.activation(act[:, tiles, :], hid[:, tiles, 0:P], ACT.Silu))
        s.wait("dve", g)
        s.done("dve", nc.vector.tensor_tensor(act[:, tiles, :], act[:, tiles, :], hid[:, tiles, P:D],
                                              ALU.mult), "qact")

    linear(k.xn[:, :, :], k.xT[:, :, :].rearrange("p c (b t) -> p (c b) t", b=B), w1,
           w1T.rearrange("p c (b t) -> p (c b) t", b=B), DC, gated)
    s.wait("pe", s.last["qact"], s.last["qo6"], s.last["qo7"])
    for t in range(NT):
        mm = nc.tensor.transpose(bank[6 + t // 4][:, t % 4 * P:(t % 4 + 1) * P], act[:, t, :],
                                 k.ident[:, :])
    td = s.done("pe", mm)
    s.wait("dve", td, s.last["qact"])
    s.wait("pe", s.last["qo4"], s.last["qo5"])

    def added(b, r):
        s.wait("dve", r)
        X2 = k.X[:, 2 * b:2 * b + 2, :]
        s.done("dve", nc.vector.scalar_tensor_tensor(
            X2, hid[:, 2 * b:2 * b + 2, :], k.tg[:, 3:4], X2, ALU.mult, ALU.add), f"qx{b // 2}")

    linear(act, k.psum[:, 6 * 512:8 * 512].rearrange("p (b t) -> p b t", b=B), w2,
           k.cT[:, :].rearrange("p (b t) -> p b t", b=B), 1, added)
    k.x_ready = [s.last["qx0"], s.last["qx1"]]
    k.bank_free = [s.last["qx1"]] * 8
    return [s.last["qx1"], s.last["qb4"], s.last["qb5"], td]


def chosen_ffn(k, readers):
    nc, s = k.nc, k.s
    KEEP, NF = KEEP3, 8
    k.at = 0
    bank = k.bank
    W1, W2 = k.place(DC, NF, P), k.place(NF, D)
    wr = k.place(DC, B, B)
    w4, left, top, mask = k.place(S), k.place(S), k.place(8), k.place(S)
    pos, zero = k.place(S), k.place(S)
    R = k.place(S)
    RT = k.place(2, 96)
    sel = k.place(NT, P)
    selT = k.place(NT, P)
    xg = k.place(DC, 2 * P)
    H = k.place(NF, 2 * P)
    blk = k.place(2, D)
    s.wait("sp", *readers)
    l0 = s.loaded("cr", nc.sync.dma_start(wr, k.io["router3"]))
    l1 = s.loaded("c1", nc.sync.dma_start(W1, k.io["w31"]))
    l2 = s.loaded("c2", nc.sync.dma_start(W2, k.io["w32"]))
    s.wait("pool", *readers)
    nc.gpsimd.memset(zero, 0.0)
    cleared = s.done("pool", nc.gpsimd.memset(R, 0.0))
    ready = k.layernorm(readers)
    for e in ("dve", "act", "pe"):
        s.wait(e, *readers, cleared, *ready[0], *ready[1], *k.bank_free)

    def dve(ins):
        t = s.done("dve", ins)
        s.wait("dve", t)
        return t

    s.wait("pe", l0)
    for b in range(B):
        for c in range(DC):
            mm = nc.tensor.matmul(bank[0][0:B, 0:S], wr[:, c, b, :], k.xT[:, c, b * S:(b + 1) * S],
                                  start=b == 0 and c == 0, stop=b == B - 1 and c == DC - 1)
    t = s.done("pe", mm)
    s.wait("dve", t)
    r4 = slice(0, B)
    dve(nc.vector.tensor_scalar(w4[r4], bank[0][r4, 0:S], k.row("b_r")[r4], None, ALU.add))
    dve(nc.vector.tensor_copy(left[r4], w4[r4]))
    for n in range(KEEP // 8):
        dve(nc.vector.max(top[r4], left[r4]))
        if n < KEEP // 8 - 1:
            dve(nc.vector.match_replace(left[r4], top[r4], left[r4], -BIG))
    dve(nc.vector.tensor_scalar(mask[r4], w4[r4], top[r4, 7:8], None, ALU.is_gt))
    dve(nc.vector.tensor_tensor_scan(pos[r4], mask[r4], zero[r4], 0.0, ALU.add, ALU.add))
    dve(nc.vector.scalar_tensor_tensor(R[r4], pos[r4], k.col("slot0")[r4], mask[r4], ALU.add, ALU.mult))
    dve(nc.vector.tensor_scalar(R[r4], R[r4], 1.0, None, ALU.subtract))
    dve(nc.vector.tensor_tensor(R[32:32 + B], w4[r4], mask[r4], ALU.mult))
    t = dve(nc.vector.tensor_scalar(R[64:64 + B], mask[r4], -1.0, 1.0, ALU.mult, ALU.add))
    s.wait("pe", t)
    for j in range(2):
        mm = nc.tensor.transpose(bank[1][:, j * P:j * P + 96], R[0:96, j * P:(j + 1) * P],
                                 k.ident[0:96, 0:96])
    t = s.done("pe", mm)
    s.wait("dve", t)
    b1v = bank[1][:, 0:2 * P].rearrange("p (j n) -> p j n", j=2)
    dve(nc.vector.tensor_copy(RT[:, :, 0:32], b1v[:, :, 0:32]))
    rt = dve(nc.vector.tensor_scalar(RT[:, :, 32:96], b1v[:, :, 32:96], k.tg[:, 7:8], None, ALU.mult))
    for t8 in range(NT):
        b, j = t8 // 2, t8 % 2
        t = s.done("dve", nc.vector.tensor_scalar(sel[:, t8, :], k.row("iota"), RT[:, j, b:b + 1], None,
                                                  ALU.is_equal))
    s.wait("pe", t)
    for c in range(DC):
        for t8 in range(NT):
            g = t8 // 4
            mm = nc.tensor.matmul(bank[2][:, (2 * c + g) * P:(2 * c + g + 1) * P],
                                  k.xn[:, t8, c * P:(c + 1) * P], sel[:, t8, :],
                                  start=t8 % 4 == 0, stop=t8 % 4 == 3)
    t = s.done("pe", mm)
    s.wait("act", t)
    xgd = s.done("act", nc.scalar.copy(xg, bank[2].rearrange("p (c n) -> p c n", c=DC)))
    for t8 in range(NT):
        mm = nc.tensor.transpose(bank[6 + t8 // 4][:, t8 % 4 * P:(t8 % 4 + 1) * P], sel[:, t8, :],
                                 k.ident[:, :])
    t = s.done("pe", mm)
    s.wait("dve", t)
    stt = s.done("dve", nc.vector.tensor_copy(selT.rearrange("p t n -> p (t n)"),
                                              k.psum[:, 6 * 512:8 * 512]))
    for t8 in range(NT):
        b, j = t8 // 2, t8 % 2
        ps = s.done("dve", nc.vector.scalar_tensor_tensor(
            k.X[:, t8, :], k.xn[:, t8, :], RT[:, j, 64 + b:65 + b], k.X[:, t8, :], ALU.mult, ALU.add))
    s.wait("pe", xgd, l1)
    for f in range(NF):
        bb = 3 + f % 2
        s.wait("pe", s.last.get(f"cb{bb}"))
        for c in range(DC):
            mm = nc.tensor.matmul(bank[bb][:, 0:2 * P], W1[:, c, f, :], xg[:, c, :], start=c == 0,
                                  stop=c == DC - 1)
        t = s.done("pe", mm)
        s.wait("act", t)
        hd = s.done("act", nc.scalar.activation(H[:, f, :], bank[bb][:, 0:2 * P], ACT.Gelu_apprx_tanh,
                                                bias=k.col("b1", f)), f"cb{bb}")
    s.wait("pe", hd, l2)
    for g in range(2):
        for f in range(NF):
            mm = nc.tensor.matmul(bank[5][:, g * D:(g + 1) * D], H[:, f, g * P:(g + 1) * P], W2[:, f, :],
                                  start=f == 0, stop=f == NF - 1)
    t = s.done("pe", mm)
    s.wait("dve", t)
    t = dve(nc.vector.tensor_tensor(
        blk, bank[5].rearrange("p (g n) -> p g n", g=2),
        k.row("b2").unsqueeze(1).broadcast_to([P, 2, D]), ALU.add))
    s.wait("pe", t, stt, hd, xgd)
    s.wait("dve", ps)
    for t8 in range(NT):
        b, j = t8 // 2, t8 % 2
        bb = t8
        if t8 >= 6:
            s.wait("pe", stt)
        mm = nc.tensor.matmul(bank[bb][:, 0:D], selT[:, t8, :], blk[:, t8 // 4, :], start=True, stop=True)
        t = s.done("pe", mm)
        s.wait("dve", t)
        a = s.done("dve", nc.vector.scalar_tensor_tensor(
            k.X[:, t8, :], bank[bb][:, 0:D], RT[:, j, 32 + b:33 + b], k.X[:, t8, :], ALU.mult, ALU.add))
        k.x_ready[t8 // 4] = a
    k.bank_free = [a] * 8
    return [a, t, hd]


def program(nc, io, plan, ctx):
    k = Core(nc, ctx, io, plan)
    k.load_constants()
    readers = []
    for layer in LAYERS:
        if layer == 0:
            readers = mamba(k, readers)
        elif layer == 1:
            readers = dense_ffn(k, readers)
        elif layer == 2:
            readers = attention1(k, readers)
        elif layer == 4:
            readers = attention2(k, readers)
        elif layer == 6:
            readers = quantised_layer(k, readers)
        elif layer == 7:
            readers = chosen_ffn(k, readers)
        elif layer == 3:
            readers = moe(k, readers, "m1", io["router1"], io["moe1"], E1, E1K, 5, 1)
        elif layer == 5:
            readers = moe(k, readers, "m2", io["router2"], io["moe2"], E2, E2K, 6, 0)
    k.finish()
    return k.s.found


def layout(inputs):
    import numpy as np

    a = {n: np.asarray(v) for n, v in inputs.items()}

    def tiles(v):
        return v.reshape(-1, P, *v.shape[1:]).swapaxes(0, 1)

    def chunks(v, n):
        z = np.zeros((n * P,), v.dtype)
        z[:v.size] = v
        return z.reshape(n, P).T

    out = {}
    out["x"] = tiles(a["x"].reshape(T, D))
    out["cT"] = a["ctx_1024"].reshape(T, C).T
    out["ident"] = np.eye(P, dtype=np.float32)
    g = np.concatenate([a["g_xattn"], a["g_ffn"]])
    rows = {"g": g, "down_s": a["L0_ffn_down_s"], "bias1": a["L1_ffn_expert_bias"],
            "bq": a["L2_xattn_bq"], "bk": a["L2_xattn_bk"], "bv": a["L2_xattn_bv"],
            "bdca": a["L2_xattn_bkv_dca"], "qn_w": a["L2_xattn_qn_w"], "qn_b": a["L2_xattn_qn_b"],
            "kn_w": a["L2_xattn_kn_w"], "kn_b": a["L2_xattn_kn_b"],
            "kd_w": a["L2_xattn_kn_dca_w"], "kd_b": a["L2_xattn_kn_dca_b"],
            "bo": a["L2_xattn_bo"], "b2": a["L3_ffn_b2"], "b_r": a["L3_ffn_b_r"],
            "iota": np.arange(P, dtype=np.float32)}
    out["rows"] = np.concatenate([rows[n].reshape(-1) for n in ROWS])
    cw = a["L0_xattn_conv_w"].reshape(2, P, 4).transpose(1, 0, 2).reshape(P, 8)
    al = a["L0_xattn_A_log"].reshape(2, P, 16).transpose(1, 0, 2).reshape(P, 32)
    out["cols"] = np.concatenate(
        [chunks(a["L0_ffn_gate_s"], 6), chunks(a["L0_ffn_up_s"], 6), cw,
         chunks(a["L0_xattn_conv_b"], 2), chunks(a["L0_xattn_dt_proj_b"], 2), al,
         chunks(a["L0_xattn_D"], 2), chunks(a["L1_xattn_gq"], 1), chunks(a["L1_xattn_gk"], 1),
         chunks(a["L3_ffn_b1"], 8), (KEEP3 * np.arange(P) % P).astype(np.float32)[:, None]], axis=1)
    nf = len(FB)
    gu = np.zeros((2, nf * P, D), np.float32)
    gu[0, :F0], gu[1, :F0] = a["L0_ffn_gate_w"], a["L0_ffn_up_w"]
    out["gu0"] = gu.reshape(2, nf, P, DC, P).transpose(4, 1, 0, 3, 2)
    dn = np.zeros((nf * P, D), np.float32)
    dn[:F0] = a["L0_ffn_down_w"].T
    out["down0"] = tiles(dn)
    def expert(wg, wu, wd):
        n = wg.shape[0]
        gu = [w.reshape(n, DC, P, P).transpose(0, 2, 1, 3).reshape(n, P, 256) for w in (wg, wu)]
        return np.stack([gu[0], gu[1], wd], axis=2)
    m1 = [np.concatenate([a["L1_ffn_w_" + n], a["L1_ffn_sw_" + n][None],
                          a["L1_ffn_sw_" + n][None]]) for n in ("gate", "up", "down")]
    out["moe1"] = expert(*[m.transpose(0, 2, 1) for m in m1])
    out["moe2"] = expert(a["L2_ffn_w1"], a["L2_ffn_w2"], a["L2_ffn_w3"])
    w = a["fside_BxS2xS2_0"]
    out["fside"] = tiles(w.reshape(B * D, D))
    out["fsideT"] = tiles(w.transpose(2, 0, 1).reshape(D, B * D))
    out["ctok"] = tiles(a["ctx_1024"].reshape(T, C))
    rw = np.zeros((DC, P, B, B), np.float32)
    rw[:, :, np.arange(B), np.arange(B)] = a["L3_ffn_W_r"].reshape(DC, P, 1)
    out["router3"] = rw.transpose(1, 0, 2, 3)
    out["w31"] = a["L3_ffn_W1"].reshape(DC, P, 8, P).transpose(1, 0, 2, 3)
    out["w32"] = tiles(a["L3_ffn_W2"])
    out["in_proj"] = a["L0_xattn_in_proj_w"].T
    xw = a["L0_xattn_x_proj_w"]
    out["x_proj"] = tiles(np.concatenate([xw[8:], xw[8:], xw[8:], xw[:8]]).T)
    out["dt_proj"] = a["L0_xattn_dt_proj_w"].T
    def joined(wk, wv):
        w = np.concatenate([wk, wv], axis=-1).reshape(-1, 16, 2, 16)
        return w[:, :, 0].reshape(-1, D), w[:, :, 1].reshape(-1, D)
    wd, bd = a["L2_xattn_Wkv_dca"], a["L2_xattn_bkv_dca"]
    wk, wv = joined(a["L2_xattn_Wk"], a["L2_xattn_Wv"])
    bk, bv = joined(a["L2_xattn_bk"], a["L2_xattn_bv"])
    out["wkv2"] = np.stack([wk, wv, wd[:, :D], wd[:, D:]], axis=1)
    bias = np.zeros((2, 6, D), np.float32)
    bias[0, 0], bias[1, 0], bias[0, 1], bias[1, 2] = bk[0], bd[:D], bv[0], bd[D:]
    bias[0, 3], bias[0, 4] = a["L2_xattn_bq"], a["L2_xattn_bo"]
    out["bias2"] = bias
    ind = np.zeros((2, 3, P), np.float32)
    ind[0, 0], ind[0, 1, :P - 16], ind[1, 1, P - 16:], ind[0, 2] = 1, 1, 1, 1
    out["ind2"] = ind
    out["wq2"], out["wo2"] = tiles(a["L2_xattn_Wq"]), tiles(a["L2_xattn_Wo"])
    aff = np.zeros((4, 32, 6), np.float32)
    for j, n in enumerate(["qn_w", "qn_b", "kn_w", "kn_b", "kn_dca_w", "kn_dca_b"]):
        aff[:, :16, j] = a["L2_xattn_" + n]
    out["aff2"] = aff.reshape(P, 6)
    def heads(w):
        n = w.shape[0] // P
        return w.reshape(n, P, 16, P).transpose(2, 1, 0, 3).reshape(16, P, n * P)
    out["qkv1"] = np.concatenate([heads(a["L1_xattn_W" + n]) for n in "qkv"], axis=2)
    out["wo1"] = a["L1_xattn_Wo"].reshape(16, P, D)
    out["router1"] = tiles(a["L1_ffn_gate_w"].T)
    out["router2"] = tiles(a["L2_ffn_router_w"].T)
    return {n: np.ascontiguousarray(v) for n, v in out.items()}


def kernel(**inputs):
    import numpy as np
    import concourse.bacc as bacc
    from concourse.bass_utils import run_bass_kernel_spmd as run

    arrays = layout(inputs)

    def build(plan):
        nc = bacc.Bacc("TRN2", target_bir_lowering=False, num_devices=1)
        io = {n: nc.dram_tensor("in_" + n, v.shape, mybir.dt.from_np(v.dtype),
                                kind="ExternalInput").ap() for n, v in arrays.items()}
        io["out"] = nc.dram_tensor("out", (P, NT, D), F32, kind="ExternalOutput").ap()
        with ExitStack() as ctx:
            found = program(nc, io, plan, ctx)
        return nc, found

    _, plan = build({})
    nc, _ = build(plan)
    r = run(nc, [{"in_" + n: v for n, v in arrays.items()}], core_ids=[0])
    got = np.asarray(r.results[0]["out"])
    return np.ascontiguousarray(got.transpose(1, 0, 2).reshape(B, S, D))
```

```python
from contextlib import ExitStack

import concourse.bass as bass
from concourse import mybir
from concourse.alu_op_type import AluOpType as ALU

F32 = mybir.dt.float32
BF16 = mybir.dt.bfloat16
ACT = mybir.ActivationFunctionType
AX = mybir.AxisListType.X

P = 128
B, S, D = 4, 256, 256
T = B * S
NT = T // P
DC = D // P
C = 128
HALF = T // 2
F0 = 704
FB = [(f, min(P, F0 - f)) for f in range(0, F0, P)]
E1, E1K = 16, 4
E2, E2K = 8, 2
SET2 = 16
KEEP3 = 64
BIG = 3.0e38
LAYERS = range(8)


class Token:

    def __init__(self, sem, k, loop=None):
        self.sem, self.k, self.loop = sem, k, loop


class Loop:
    def __init__(self, number, n, base):
        self.number, self.n, self.base, self.i, self.now = number, n, base, None, {}


class Signals:

    START = 2048

    def __init__(self, nc, ctx, plan):
        self.nc, self.ctx, self.plan, self.found = nc, ctx, plan, {}
        self.sems, self.count, self.waited, self.last = {}, {}, {}, {}
        self.loop, self.loops = None, 0
        self.engines = {"pe": nc.tensor, "act": nc.scalar, "dve": nc.vector,
                        "pool": nc.gpsimd, "sp": nc.sync}
        for e in ("pe", "act", "dve", "pool"):
            self.sem(e)
            self.engines[e].sem_inc(self.sems[e], self.START)
            self.count[e] = self.START

    def sem(self, name):
        if name not in self.sems:
            self.sems[name] = self.ctx.enter_context(self.nc.semaphore("s_" + name))
            self.count[name] = 0
        return self.sems[name]

    def done(self, name, ins, label=None, by=1):
        ins.then_inc(self.sem(name), by)
        if self.loop is None:
            self.count[name] += by
            t = Token(name, self.count[name])
        else:
            now = self.loop.now
            now[name] = now.get(name, 0) + by
            t = Token(name, now[name], self.loop)
            if label:
                self.found["k", self.loop.number, label] = (name, now[name])
        if label:
            self.last[label] = t
        return t

    def relabel(self, label, other):
        t = self.last[label] = self.last[other]
        if self.loop is not None:
            self.found["k", self.loop.number, label] = (t.sem, t.k)
        return t

    def loaded(self, name, ins, label=None):
        return self.done("d_" + name, ins, label, 16)

    def before(self, label):
        found = self.plan.get(("k", self.loop.number, label))
        if found is None:
            assert not self.plan, label
            return None
        name, k = found
        return Token(name, k - self.gain(self.loop, name), self.loop)

    def latest(self, *labels):
        got = []
        for label in labels:
            t = self.last.get(label)
            if self.loop is not None and (t is None or t.loop is not self.loop) and (
                    not self.plan or ("k", self.loop.number, label) in self.plan):
                t = self.before(label)
            got.append(t)
        return got

    def settle(self, prefix, engines=("pe", "act", "dve", "pool", "sp")):
        for e in engines:
            self.wait(e, *[t for label, t in self.last.items() if label.startswith(prefix)])

    def gain(self, loop, name):
        return self.plan.get(("m", loop.number, name), 1)

    def wait(self, eng, *tokens):
        for t in tokens:
            if t is None:
                continue
            seen = self.waited.setdefault((eng, t.sem), {"const": 0, "loop": None})
            if t.loop is None:
                if t.k > seen["const"]:
                    self.engines[eng].wait_ge(self.sem(t.sem), t.k)
                    seen["const"] = t.k
                continue
            m, base = self.gain(t.loop, t.sem), t.loop.base.get(t.sem, 0)
            k = t.k
            if t.loop is self.loop:
                if seen["loop"] is None or k > seen["loop"]:
                    value = self.loop.i * m + (base + k)
                    self.engines[eng].wait_ge(self.sem(t.sem), value)
                    seen["loop"] = k
            else:
                v = base + (t.loop.n - 1) * m + k
                if v > seen["const"]:
                    self.engines[eng].wait_ge(self.sem(t.sem), v)
                    seen["const"] = v

    def repeat(self, n):
        return _Repeat(self, n)


class _Repeat:
    def __init__(self, sig, n):
        self.sig, self.n = sig, n

    def __enter__(self):
        s = self.sig
        s.loop = Loop(s.loops, self.n, dict(s.count))
        s.loops += 1
        for w in s.waited.values():
            w["loop"] = None
        self.fori = s.nc.Fori(0, self.n)
        s.loop.i = self.fori.__enter__()
        return s.loop.i

    def __exit__(self, *exc):
        s, loop = self.sig, self.sig.loop
        self.fori.__exit__(*exc)
        for name, m in loop.now.items():
            s.found["m", loop.number, name] = m
            s.count[name] = s.count.get(name, 0) + m * loop.n
        s.loop = None
        return False


def row_layout():
    at, rows = 0, {}
    for name, n in [("g", 8), ("down_s", D), ("bias1", E1), ("bq", D), ("bv", D),
                    ("bvd", D), ("bo", D), ("b2", D), ("b_r", 1), ("iota", P)]:
        rows[name] = (at, n)
        at += n
    return rows, at


ROWS, NROWS = row_layout()
COLS = {"gate_s": (0, 6), "up_s": (6, 6), "conv_w": (12, 8), "conv_b": (20, 2), "dt_b": (22, 2),
        "A_log": (24, 32), "Dp": (56, 2), "gq": (58, 1), "gk": (59, 1), "b1": (60, 8),
        "slot0": (68, 1)}
NCOLS = 69


class Core:

    def __init__(self, nc, ctx, io, plan):
        self.nc, self.io = nc, io
        self.s = Signals(nc, ctx, plan)

        def sb(name, shape, dt=F32):
            return ctx.enter_context(nc.sbuf_tensor(name, shape, dt))

        self.psum = ctx.enter_context(nc.psum_tensor("psum", [P, 8 * 512], F32))
        self.bank = [self.psum[:, b * 512:(b + 1) * 512] for b in range(8)]
        self.X = sb("X", [P, NT, D])
        self.xn = sb("xn", [P, NT, D])
        self.xT = sb("xT", [P, DC, T])
        self.cT = sb("cT", [P, T])
        self.sets = sb("sets", [P, 2, B, P])
        self.ident = sb("ident", [P, P])
        self.rows = sb("rows", [P, NROWS])
        self.cols = sb("cols", [P, NCOLS])
        self.tg = sb("tg", [P, 8])
        self.stats = sb("stats", [P, NT, 6])
        self.mv = sb("mv", [P, NT, 2])
        self.rstd = sb("rstd", [P, NT])
        self.mhalf = sb("mhalf", [P, 128])
        self.phalf = sb("phalf", [P, 128])
        self.arena = sb("arena", [P, 34304])
        self.at = 0
        self.bank_free = [None] * 8

    def place(self, *shape, dt=F32):
        n = 1
        for d in shape:
            n *= d
        words = n if dt == F32 else (n + 1) // 2
        words += -words % 16
        v = self.arena[:, self.at:self.at + words]
        self.at += words
        assert self.at <= 34304, self.at
        if dt != F32:
            v = v.bitcast(dt)
        v = v[:, 0:n]
        if len(shape) == 2:
            v = v.rearrange("p (a b) -> p a b", a=shape[0])
        elif len(shape) == 3:
            v = v.rearrange("p (a b c) -> p a b c", a=shape[0], b=shape[1])
        elif len(shape) == 4:
            v = v.rearrange("p (a b c d) -> p a b c d", a=shape[0], b=shape[1], c=shape[2])
        return v

    def row(self, name):
        at, n = ROWS[name]
        return self.rows[:, at:at + n]

    def col(self, name, j=0):
        return self.cols[:, COLS[name][0] + j:COLS[name][0] + j + 1]

    def load_constants(self):
        nc, s, io = self.nc, self.s, self.io
        self.x_in = [s.loaded(f"x{h}", nc.sync.dma_start(
            self.X[:, 4 * h:4 * h + 4, :], io["x"][:, 4 * h:4 * h + 4, :])) for h in range(2)]
        self.ident_in = s.loaded("ident", nc.scalar.dma_start(self.ident[:, :], io["ident"]))
        self.rows_in = s.loaded("rows", nc.scalar.dma_start(
            self.rows[:, :], io["rows"].partition_broadcast(P)))
        self.cols_in = s.loaded("cols", nc.scalar.dma_start(self.cols[:, :], io["cols"]))
        self.ctx_in = s.loaded("cT", nc.sync.dma_start(self.cT[:, :], io["cT"]))
        nc.gpsimd.memset(self.mhalf[:, :], -0.5)
        self.halves = s.done("pool", nc.gpsimd.memset(self.phalf[:, :], 0.5))
        cleared = s.done("pool", nc.gpsimd.memset(self.sets[:, :, :, :], 0.0))
        s.wait("pool", cleared, self.ctx_in)
        second = self.cT[:, :].rearrange("p (b j t) -> p b j t", b=B, j=2)[:, :, 1, :]
        main = P - SET2
        nc.gpsimd.tensor_copy(self.sets[:, 0, :, 0:main], second[:, :, 0:main])
        self.sets_in = s.done("pool", nc.gpsimd.tensor_copy(self.sets[:, 1, :, main:], second[:, :, main:]))
        s.wait("act", self.rows_in)
        self.tg_done = s.done("act", nc.scalar.activation(self.tg[:, :], self.row("g"), ACT.Tanh))
        self.x_ready = list(self.x_in)
        s.wait("pe", self.ident_in)
        for e in ("dve", "pool"):
            s.wait(e, self.rows_in, self.cols_in, self.tg_done, self.halves)
        s.wait("act", self.cols_in)
        self.out = [None, None]

    def layernorm(self, readers=(), transpose=True):
        nc, s = self.nc, self.s
        s.wait("dve", *readers)
        s.wait("act", *readers)
        ready = []
        for h in range(2):
            tiles = range(4 * h, 4 * h + 4)
            s.wait("dve", self.x_ready[h])
            for t in tiles:
                st = s.done("dve", nc.vector.bn_stats(self.stats[:, t, :], self.X[:, t, :]))
            s.wait("dve", st)
            for t in tiles:
                ag = s.done("dve", nc.vector.bn_aggr(self.mv[:, t, :], self.stats[:, t, :]))
            s.wait("dve", ag)
            half = slice(4 * h, 4 * h + 4)
            ve = s.done("dve", nc.vector.tensor_scalar(self.rstd[:, half], self.mv[:, half, 1],
                                                       1e-5, None, ALU.add))
            s.wait("pool", ve)
            rs = s.done("pool", nc.gpsimd.tensor_tensor(self.rstd[:, half], self.rstd[:, half],
                                                        self.mhalf[:, 0:4], ALU.pow))
            s.wait("dve", rs)
            for j, t in enumerate(tiles):
                xn = s.done("dve", nc.vector.tensor_scalar(
                    self.xn[:, t, :], self.X[:, t, :], self.mv[:, t, 0:1], self.rstd[:, t:t + 1],
                    ALU.subtract, ALU.mult))
                if not transpose:
                    continue
                s.wait("pe", xn)
                for c in range(DC):
                    b = 2 * h + c
                    if j == 0:
                        s.wait("pe", self.bank_free[b])
                    tr = s.done("pe", nc.tensor.transpose(
                        self.bank[b][:, j * P:(j + 1) * P], self.xn[:, t, c * P:(c + 1) * P],
                        self.ident[:, :]))
            if not transpose:
                ready.append((xn,))
                continue
            s.wait("act", tr)
            s.wait("dve", tr)
            cols = slice(h * HALF, (h + 1) * HALF)
            a = s.done("act", nc.scalar.copy(self.xT[:, 0, cols], self.bank[2 * h][:, :]))
            v = s.done("dve", nc.vector.tensor_copy(self.xT[:, 1, cols], self.bank[2 * h + 1][:, :]))
            self.bank_free[2 * h], self.bank_free[2 * h + 1] = a, v
            ready.append((a, v))
        return ready

    def finish(self):
        nc, s = self.nc, self.s
        for h in range(2):
            s.wait("sp", self.x_ready[h])
            t = s.loaded("out", nc.sync.dma_start(self.io["out"][:, 4 * h:4 * h + 4, :],
                                                  self.X[:, 4 * h:4 * h + 4, :]))
        s.wait("sp", t)


def mamba(k, readers):
    nc, s = k.nc, k.s
    NI, NSTATE, RANK, W = 2, 16, 8, 4
    NBC = 2 * NSTATE
    k.at = 0
    Win = k.place(NI * P)
    Wx = k.place(NI, 3 * NBC + RANK)
    Wdt = k.place(NI * P)
    xp = k.place(NI, B, W - 1 + S)
    U, DT, DU, Y = k.place(NI, T), k.place(NI, T), k.place(NI, T), k.place(NI, T)
    V, E = k.place(NI, T), k.place(NI, T)
    A = k.place(NI, NSTATE)
    low = k.place(T)
    bcf = k.place(T)
    bc3 = k.place(T, dt=BF16)
    part = k.place(T, dt=BF16)
    sel = k.place(NBC, P, dt=BF16)
    row = k.place(NBC)
    gate = k.place(NT, S)
    dA, dBu = k.place(2, B, S), k.place(2, T)
    Hs, HC = k.place(2, T), k.place(2, T)
    bank = k.bank
    wi = s.loaded("mwi", nc.sync.dma_start(Win, k.io["in_proj"]))
    wx = s.loaded("mwx", nc.scalar.dma_start(Wx, k.io["x_proj"]))
    wd = s.loaded("mwd", nc.scalar.dma_start(Wdt[96:96 + RANK], k.io["dt_proj"]))
    nc.gpsimd.memset(dA[:, :, :, 0:1], 0.0)
    pads = s.done("pool", nc.gpsimd.memset(xp[:, :, :, 0:W - 1], 0.0))
    s.wait("pool", k.ident_in)
    ws = s.done("pool", nc.gpsimd.tensor_tensor(row, k.ident[:, 0:NBC], k.ident[:, NBC:2 * NBC], ALU.add))
    s.wait("pool", ws)
    ws = s.done("pool", nc.gpsimd.tensor_tensor(row, row, k.ident[:, 2 * NBC:3 * NBC], ALU.add))
    s.wait("pool", ws)
    ws = s.done("pool", nc.gpsimd.tensor_copy(sel, row.unsqueeze(2).broadcast_to([P, NBC, P])))
    s.wait("pe", k.ctx_in, wi)
    s.wait("act", pads)
    s.wait("dve", pads)
    for c in range(NI):
        for h in range(2):
            mm = nc.tensor.matmul(bank[2 * c + h], Win[:, c * P:(c + 1) * P],
                                  k.cT[:, h * HALF:(h + 1) * HALF], start=True, stop=True)
            pd = s.done("pe", mm)
            s.wait("act", pd)
            xi = s.done("act", nc.scalar.copy(xp[:, c, 2 * h:2 * h + 2, W - 1:],
                                              bank[2 * c + h].rearrange("p (b t) -> p b t", b=2)))
        s.wait("dve", xi)
        yv = Y[:, c, :].rearrange("p (b t) -> p b t", b=B)
        for w in range(W):
            tap, src = k.col("conv_w", c * W + w), xp[:, c, :, w:w + S]
            if w == 0:
                r = s.done("dve", nc.vector.tensor_scalar(yv, src, tap, None, ALU.mult))
            else:
                s.wait("dve", r)
                r = s.done("dve", nc.vector.scalar_tensor_tensor(yv, src, tap, yv, ALU.mult, ALU.add))
        s.wait("act", r)
        ui = s.done("act", nc.scalar.activation(U[:, c, :], Y[:, c, :], ACT.Silu, bias=k.col("conv_b", c)))
    z = k.layernorm(transpose=False)
    s.wait("act", *z[0], *z[1])
    gd = s.done("act", nc.scalar.activation(gate, k.xn[:, :, :], ACT.Silu))
    s.wait("pe", ui, wx)
    n96 = 3 * NBC
    for h in range(2):
        for c in range(NI):
            mm = nc.tensor.matmul(bank[4 + h][0:n96 + RANK, :], Wx[:, c, :],
                                  U[:, c, h * HALF:(h + 1) * HALF], start=c == 0, stop=c == NI - 1)
    xd = s.done("pe", mm)
    both = k.psum[:, 4 * 512:6 * 512]
    s.wait("act", xd)
    lo = s.done("act", nc.scalar.copy(low[96:96 + RANK], both[96:96 + RANK, :]))
    s.wait("dve", xd, lo)
    r = s.done("dve", nc.vector.tensor_copy(bc3[0:n96], both[0:n96, :]))
    s.wait("dve", r)
    r = s.done("dve", nc.vector.tensor_tensor(bcf[0:n96], both[0:n96, :], bc3[0:n96], ALU.subtract))
    s.wait("dve", r)
    r = s.done("dve", nc.vector.tensor_copy(part[0:n96], bcf[0:n96]))
    s.wait("dve", r)
    r1 = s.done("dve", nc.vector.tensor_copy(bc3[NBC:2 * NBC], part[NBC:2 * NBC]))
    r = s.done("dve", nc.vector.tensor_tensor(bcf[0:n96], bcf[0:n96], part[0:n96], ALU.subtract))
    s.wait("dve", r)
    split = s.done("dve", nc.vector.tensor_copy(bc3[2 * NBC:n96], bcf[2 * NBC:n96]))
    s.wait("pe", lo, wd)
    for c in range(NI):
        for h in range(2):
            mm = nc.tensor.matmul(bank[2 * c + h], Wdt[96:96 + RANK, c * P:(c + 1) * P],
                                  low[96:96 + RANK, h * HALF:(h + 1) * HALF], start=True, stop=True)
        vd = s.done("pe", mm)
        s.wait("act", vd)
        pv = k.psum[:, 2 * c * 512:(2 * c + 2) * 512]
        s.done("act", nc.scalar.activation(V[:, c, :], pv, ACT.Identity, bias=k.col("dt_b", c)))
        r = s.done("act", nc.scalar.activation(E[:, c, :], pv, ACT.Abs, bias=k.col("dt_b", c)))
        s.wait("act", r)
        e = s.done("act", nc.scalar.activation(E[:, c, :], E[:, c, :], ACT.Exp, scale=-1.0))
        s.wait("dve", e)
        w1 = s.done("dve", nc.vector.tensor_scalar(DT[:, c, :], E[:, c, :], 1.0, None, ALU.add))
        s.wait("act", w1)
        ln = s.done("act", nc.scalar.activation(DU[:, c, :], DT[:, c, :], ACT.Ln))
        s.wait("dve", ln)
        r = s.done("dve", nc.vector.tensor_scalar(DT[:, c, :], DT[:, c, :], -1.0, -1.0, ALU.add, ALU.mult))
        s.wait("dve", r)
        r = s.done("dve", nc.vector.tensor_tensor(E[:, c, :], E[:, c, :], DT[:, c, :], ALU.add))
        s.wait("dve", r)
        r = s.done("dve", nc.vector.tensor_tensor(E[:, c, :], E[:, c, :], DU[:, c, :], ALU.add))
        s.wait("dve", r)
        r = s.done("dve", nc.vector.scalar_tensor_tensor(DT[:, c, :], V[:, c, :], 0.0, E[:, c, :],
                                                         ALU.max, ALU.add))
        s.wait("dve", r, ui)
        r = s.done("dve", nc.vector.tensor_tensor(DU[:, c, :], DT[:, c, :], U[:, c, :], ALU.mult))
        s.wait("pool", ui, r)
        yd = s.done("pool", nc.gpsimd.tensor_scalar(Y[:, c, :], U[:, c, :], k.col("Dp", c), None, ALU.mult),
                    f"my{c}")
    al = COLS["A_log"][0]
    ex = s.done("act", nc.scalar.activation(A, k.cols[:, al:al + 32].rearrange("p (c n) -> p c n", c=2),
                                            ACT.Exp))
    s.wait("dve", ex)
    an = s.done("dve", nc.vector.tensor_scalar(A, A, -1.0, None, ALU.mult))
    s.wait("pe", split, ws, vd)
    s.wait("act", an, r)
    s.wait("dve", an)
    for e in ("pe", "act", "dve"):
        s.wait(e, yd, vd)

    def state(n, v):
        b0 = 4 * v
        s.wait("pe", *s.latest(f"mB{v}"))
        for row, b in ((n, b0), (n + NSTATE, b0 + 2)):
            if b == b0 + 2:
                s.wait("pe", *s.latest(f"mC{v}"))
            for h in range(2):
                mm = nc.tensor.matmul(bank[b + h], sel[0:n96, bass.ds(row, 1), :].rearrange("p a n -> p (a n)"),
                                      bc3[0:n96, h * HALF:(h + 1) * HALF], start=True, stop=True)
            rd = s.done("pe", mm)
        Bp, Cp = k.psum[:, b0 * 512:(b0 + 2) * 512], k.psum[:, (b0 + 2) * 512:(b0 + 4) * 512]
        for c in range(NI):
            s.wait("act", *s.latest(f"mscan{c}"))
            dtv = DT[:, c, :].rearrange("p (b t) -> p b t", b=B)
            ad = s.done("act", nc.scalar.activation(dA[:, c, :, 1:S], dtv[:, :, 1:S], ACT.Exp,
                                                    scale=A[:, c, bass.ds(n, 1)]))
            s.wait("dve", rd, *s.latest(f"mscan{c}"))
            r = s.done("dve", nc.vector.tensor_tensor(dBu[:, c, :], DU[:, c, :], Bp, ALU.mult), f"mB{v}")
            s.wait("dve", ad, r, *s.latest(f"mhc{c}"))
            r = s.done("dve", nc.vector.tensor_tensor_scan(
                Hs[:, c, :], dA[:, c].rearrange("p b t -> p (b t)"), dBu[:, c, :], 0.0, ALU.mult, ALU.add),
                f"mscan{c}")
            s.wait("dve", r, *s.latest(f"my{c}"))
            r = s.done("dve", nc.vector.tensor_tensor(HC[:, c, :], Hs[:, c, :], Cp, ALU.mult), f"mhc{c}")
            s.relabel(f"mC{v}", f"mhc{c}")
            s.wait("pool", r, *s.latest(f"my{c}"))
            s.done("pool", nc.gpsimd.tensor_tensor(Y[:, c, :], Y[:, c, :], HC[:, c, :], ALU.add), f"my{c}")

    with s.repeat(NSTATE // 2) as i:
        for v in range(2):
            state(i * 2 + v, v)
    tr = {}
    for c in range(NI):
        s.wait("dve", *s.latest(f"my{c}"), gd)
        g = s.done("dve", nc.vector.tensor_tensor(
            Y[:, c, :].rearrange("p (b t) -> p b t", b=B), Y[:, c, :].rearrange("p (b t) -> p b t", b=B),
            gate.rearrange("p (b c) t -> p b c t", c=NI)[:, :, c, :], ALU.mult))
        tr[c] = g
    s.wait("pe", *s.latest("mC0", "mC1"), tr[0], tr[1])
    for b in range(B):
        for j in range(2):
            for c in range(NI):
                mm = nc.tensor.transpose(bank[b][:, j * D + c * P:j * D + (c + 1) * P],
                                         Y[:, c, b * S + j * P:b * S + (j + 1) * P], k.ident[:, :])
        td = s.done("pe", mm)
        s.wait("dve", td)
        X2 = k.X[:, 2 * b:2 * b + 2, :]
        a = s.done("dve", nc.vector.scalar_tensor_tensor(
            X2, bank[b].rearrange("p (t d) -> p t d", t=2), k.tg[:, 0:1], X2, ALU.mult, ALU.add))
        k.bank_free[b] = a
        if b % 2:
            k.x_ready[b // 2] = a
    k.bank_free[4:] = [a] * 4
    return [td, a, *s.latest("my1"), gd]


def dense_ffn(k, readers):
    nc, s = k.nc, k.s
    k.at = 0
    nf = len(FB)
    gu = k.place(nf, 2, DC, P)
    down = k.place(nf, D)
    H = k.place(nf, T)
    G = k.place(2, HALF)
    Y = k.place(2, D)
    scale = k.place(D)
    s.wait("sp", *readers)
    w_in = [s.loaded("w0a", nc.sync.dma_start(gu[:, 0:1], k.io["gu0"][:, 0:1])),
            s.loaded("w0b", nc.sync.dma_start(gu[:, 1:nf], k.io["gu0"][:, 1:nf])),
            s.loaded("w0c", nc.sync.dma_start(down[:, :, :], k.io["down0"]))]
    ready = k.layernorm(readers)
    sc = s.done("dve", nc.vector.tensor_scalar(scale, k.row("down_s"), k.tg[:, 4:5], None, ALU.mult))
    free = k.bank_free
    n, muls, mul_done = 0, [], {}
    for h in range(2):
        cols = slice(h * HALF, (h + 1) * HALF)
        s.wait("pe", *ready[h], w_in[0])
        for f, (_, m) in enumerate(FB):
            if f == 1:
                s.wait("pe", w_in[1])
            g, u = 4 + n % 2 * 2, 5 + n % 2 * 2
            for b, which in ((g, 0), (u, 1)):
                s.wait("pe", free[b])
                for c in range(DC):
                    mm = nc.tensor.matmul(k.bank[b][0:m, :], gu[:, f, which, c, 0:m],
                                          k.xT[:, c, cols], start=c == 0, stop=c == DC - 1)
                if which == 0:
                    g_done = s.done("pe", mm)
            u_done = s.done("pe", mm)
            s.wait("act", g_done, muls[n - 2] if n >= 2 else None)
            si = s.done("act", nc.scalar.activation(G[0:m, n % 2, :], k.bank[g][0:m, :], ACT.Silu,
                                                    scale=k.col("gate_s", f)[0:m, :]))
            s.wait("dve", u_done, si)
            mu = s.done("dve", nc.vector.scalar_tensor_tensor(
                H[0:m, f, cols], k.bank[u][0:m, :], k.col("up_s", f)[0:m, :], G[0:m, n % 2, :],
                ALU.mult, ALU.mult))
            free[g], free[u] = si, mu
            muls.append(mu)
            n += 1
        mul_done[h] = muls[-1]
    s.wait("pe", w_in[2])
    added = []
    for t in range(NT):
        b = t % 4
        s.wait("pe", mul_done[t // 4], free[b])
        for f, (_, m) in enumerate(FB):
            mm = nc.tensor.matmul(k.bank[b][:, 0:D], H[0:m, f, t * P:(t + 1) * P], down[0:m, f, :],
                                  start=f == 0, stop=f == nf - 1)
        y_done = s.done("pe", mm)
        s.wait("dve", y_done, sc, added[t - 2] if t >= 2 else None)
        ys = s.done("dve", nc.vector.tensor_tensor(Y[:, t % 2, :], k.bank[b][:, 0:D], scale, ALU.mult))
        free[b] = ys
        s.wait("pool", ys)
        added.append(s.done("pool", nc.gpsimd.tensor_tensor(k.X[:, t, :], k.X[:, t, :],
                                                            Y[:, t % 2, :], ALU.add)))
    k.x_ready = [added[3], added[7]]
    return [y_done, added[-1]]


def top_mask(k, sel, ext, first, top, rep, mask, experts, keep):
    nc, s = k.nc, k.s
    s.wait("dve", first)
    for t in range(NT):
        mx = s.done("dve", nc.vector.max(top[:, t, :], ext[:, t, 0:experts]))
    s.wait("dve", mx)
    pads = s.done("dve", nc.vector.memset(top[:, :, keep:8], -BIG))
    s.wait("dve", pads)
    for t in range(NT):
        mr = s.done("dve", nc.vector.match_replace(rep[:, t, :], top[:, t, :], ext[:, t, :], BIG))
    s.wait("dve", mr)
    return s.done("dve", nc.vector.tensor_tensor(mask, rep[:, :, 0:experts], ext[:, :, 0:experts],
                                                 ALU.not_equal))


def moe(k, readers, tag, router, weights, experts, keep, gate, shared):
    nc, s = k.nc, k.s
    k.at = 0
    total = experts + shared
    W = k.place(2, 3, 256)
    wr = k.place(DC, experts)
    H = k.place(4, HALF)
    G = k.place(4, HALF)
    acc = k.place(NT, D)
    logits = k.place(NT, experts)
    score = k.place(NT, experts)
    ext = k.place(NT, experts + 8 - keep)
    rep = k.place(NT, experts + 8 - keep)
    top = k.place(NT, 8)
    ones = k.place(1)
    mask = k.place(NT, experts)
    cw = k.place(NT, experts)
    tot = k.place(NT)
    s.wait("sp", *readers)
    wr_in = s.loaded(tag + "wr", nc.sync.dma_start(wr[:, :, :], router))

    def load(slot, e):
        src = weights[bass.ds(e, 1)].rearrange("a p m n -> p (a m) n")
        return s.loaded(f"{tag}w{slot}", nc.sync.dma_start(W[:, slot, :, :], src), f"{tag}w{slot}")

    load(0, 0)
    load(1, 1)
    ready = k.layernorm(readers)
    s.wait("dve", *readers)
    s.wait("pool", *readers)
    cleared = s.done("pool", nc.gpsimd.memset(acc[:, :, :], 0.0))
    one = s.done("pool", nc.gpsimd.memset(ones, 1.0))
    padded = s.done("pool", nc.gpsimd.memset(ext[:, :, experts:experts + 8 - keep], -BIG))
    for h in range(2):
        s.wait("pe", *ready[h])
    s.wait("pe", wr_in, k.bank_free[7])
    for t in range(NT):
        for c in range(DC):
            mm = nc.tensor.matmul(k.bank[7][:, t * experts:(t + 1) * experts],
                                  k.xT[:, c, t * P:(t + 1) * P], wr[:, c, :],
                                  start=c == 0, stop=c == DC - 1)
    lg = s.done("pe", mm)
    lg_ps = k.bank[7][:, 0:NT * experts].rearrange("p (t e) -> p t e", t=NT)
    if tag == "m1":
        s.wait("act", lg)
        th = s.done("act", nc.scalar.activation(score[:, :, :], lg_ps, ACT.Tanh, scale=0.5))
        k.bank_free[7] = th
        s.wait("dve", th, padded)
        sg = s.done("dve", nc.vector.tensor_scalar(score, score, 0.5, 0.5, ALU.mult, ALU.add))
        s.wait("dve", sg)
        first = s.done("dve", nc.vector.tensor_tensor(
            ext[:, :, 0:experts], score, k.row("bias1").unsqueeze(1).broadcast_to([P, NT, experts]),
            ALU.add))
    else:
        s.wait("dve", lg, padded)
        first = s.done("dve", nc.vector.tensor_copy(ext[:, :, 0:experts], lg_ps))
        k.bank_free[7] = first
    mk = top_mask(k, None, ext, first, top, rep, mask, experts, keep)
    if tag == "m2":
        s.wait("dve", mk)
        d = s.done("dve", nc.vector.tensor_tensor(
            score, ext[:, :, 0:experts], top[:, :, 0:1].broadcast_to([P, NT, experts]), ALU.subtract))
        s.wait("act", d)
        ex = s.done("act", nc.scalar.activation(score[:, :, :], score[:, :, :], ACT.Exp))
        s.wait("dve", ex)
    s.wait("dve", mk)
    a = s.done("dve", nc.vector.tensor_tensor(cw, mask, score, ALU.mult))
    s.wait("dve", a)
    a = s.done("dve", nc.vector.tensor_reduce(tot, cw, AX, ALU.add))
    s.wait("dve", a)
    a = s.done("dve", nc.vector.reciprocal(tot, tot))
    s.wait("dve", a)
    a = s.done("dve", nc.vector.tensor_tensor(cw, cw, tot.unsqueeze(2).broadcast_to([P, NT, experts]),
                                              ALU.mult))
    s.wait("dve", a, cleared, one)

    def user(label, looped, same):
        if looped and not same:
            return s.before(label)
        return s.last.get(label)

    def gate_up(st, looped):
        r, slot, h = st % 4, st % 4 // 2, st % 2
        g, u, two = 2 * h, 2 * h + 1, (st + 2) % 4
        cols = slice(h * HALF, (h + 1) * HALF)
        s.wait("pe", user(f"{tag}w{slot}", looped, st == 4))
        s.wait("pe", user(f"{tag}silu{two}", looped, st >= 3))
        for c in range(DC):
            mm = nc.tensor.matmul(k.bank[g][:, :], W[:, slot, 0, c * P:(c + 1) * P], k.xT[:, c, cols],
                                  start=c == 0, stop=c == DC - 1)
        gd = s.done("pe", mm)
        s.wait("pe", user(f"{tag}mul{two}", looped, st >= 3))
        for c in range(DC):
            mm = nc.tensor.matmul(k.bank[u][:, :], W[:, slot, 1, c * P:(c + 1) * P], k.xT[:, c, cols],
                                  start=c == 0, stop=c == DC - 1)
        ud = s.done("pe", mm)
        s.wait("act", gd, user(f"{tag}mul{r}", looped, False))
        si = s.done("act", nc.scalar.activation(G[:, r, :], k.bank[g][:, :], ACT.Silu), f"{tag}silu{r}")
        s.wait("dve", ud, si, user(f"{tag}out{r}", looped, st == 4))
        s.done("dve", nc.vector.tensor_tensor(H[:, r, :], k.bank[u][:, :], G[:, r, :], ALU.mult),
               f"{tag}mul{r}")

    def down(st, looped, e):
        r, slot, h, two = st % 4, st % 4 // 2, st % 2, (st + 2) % 4
        s.wait("pe", user(f"{tag}mul{r}", looped, st >= 1))
        outs = []
        for j in range(4):
            b = 4 + 2 * h + j // 2
            if j % 2 == 0:
                s.wait("pe", user(f"{tag}acc{two}.{j + 1}", looped, st >= 2))
            mm = nc.tensor.matmul(k.bank[b][:, j % 2 * D:(j % 2 + 1) * D], H[:, r, j * P:(j + 1) * P],
                                  W[:, slot, 2, :], start=True, stop=True)
            if j % 2 == 1:
                outs.append(s.done("pe", mm, f"{tag}out{r}" if j == 3 else None))
        for j in range(4):
            t, b = 4 * h + j, 4 + 2 * h + j // 2
            w = ones if e is None else cw[:, t, bass.ds(e, 1)]
            s.wait("dve", outs[j // 2], user(f"{tag}acc{two}.{j}", looped, st >= 2))
            s.done("dve", nc.vector.scalar_tensor_tensor(
                acc[:, t, :], k.bank[b][:, j % 2 * D:(j % 2 + 1) * D], w, acc[:, t, :],
                ALU.mult, ALU.add), f"{tag}acc{r}.{j}")
        return outs[1]

    s.wait("pe", *[k.bank_free[b] for b in range(8)])
    s.wait("act", *[k.bank_free[b] for b in range(8)])
    pairs = total // 2 if shared else total // 2 - 1
    gate_up(0, False)
    s.wait("pe", s.last[f"{tag}mul0"])
    with s.repeat(pairs) as i:
        for st in range(4):
            gate_up(st + 1, True)
            od = down(st, True, i * 2 + st // 2)
            if st % 2 == 1:
                s.wait("sp", od)
                load(st // 2, i * 2 + 2 + st // 2)
    e = 2 * pairs
    if shared:
        gate_up(1, False)
        down(0, False, None)
        od = down(1, False, None)
    else:
        for st in range(4):
            if st < 3:
                gate_up(st + 1, False)
            od = down(st, False, e + st // 2)
    g = k.tg[:, gate:gate + 1]
    last = s.last[f"{tag}acc{1 if shared else 3}.3"]
    s.wait("dve", last)
    for t in range(NT):
        a = s.done("dve", nc.vector.scalar_tensor_tensor(k.X[:, t, :], acc[:, t, :], g, k.X[:, t, :],
                                                         ALU.mult, ALU.add))
        if t == 3:
            k.x_ready[0] = a
    k.x_ready[1] = a
    k.bank_free = [a] * 8
    return [od, a, s.last[f"{tag}silu{1 if shared else 3}"]] + [s.last[f"{tag}w{j}"] for j in range(2)]


def attention1(k, readers):
    nc, s = k.nc, k.s
    NH, HD = 16, P
    k.at = 0
    Wqkv = k.place(2, 512)
    Wo = k.place(2, D)
    Q, K = k.place(2, T), k.place(2, T)
    V, O = k.place(2, NT, HD), k.place(2, T)
    Kr, Kn = k.place(NT, HD), k.place(NT, HD)
    sq = k.place(2, NT, HD)
    ss = k.place(2, NT)
    rk = k.place(NT)
    rq = k.place(2, NT)
    Pr = k.place(2, 2, 2 * P)
    PT = k.place(2, 2, 2 * P)
    mx, nb, rs, ri = k.place(2, 2), k.place(2, 2), k.place(2, 2), k.place(2, 2)
    ones = k.place(1)
    s.wait("sp", *readers)
    bank = k.bank

    def load_qkv(slot, h):
        s.wait("sp", *s.latest(f"a1Quse{slot}"))
        s.loaded(f"a1qkv{slot}", nc.sync.dma_start(
            Wqkv[:, slot, :], k.io["qkv1"][bass.ds(h, 1)].rearrange("a p n -> p (a n)")), f"a1qkv{slot}")

    def load_o(slot, h):
        s.wait("sp", *s.latest("a1Ouse"))
        s.loaded(f"a1wo{slot}", nc.sync.dma_start(
            Wo[:, slot, :], k.io["wo1"][bass.ds(h, 1)].rearrange("a p n -> p (a n)")), f"a1wo{slot}")

    def keys(p):
        w = Wqkv[:, p, :]
        s.wait("pe", *s.latest(f"a1qkv{p}"))
        for half in range(2):
            b = 6 + half
            s.wait("pe", *s.latest(f"a1b{b}"))
            for j in range(4):
                mm = nc.tensor.matmul(bank[b][:, j * P:(j + 1) * P],
                                      k.cT[:, (4 * half + j) * P:(4 * half + j + 1) * P],
                                      w[:, 256:384], start=True, stop=True)
            kd = s.done("pe", mm)
            s.wait("act", kd, *s.latest("a1Kss", "a1Kn"))
            tl = slice(4 * half, 4 * half + 4)
            kv = bank[b].rearrange("p (t d) -> p t d", t=4)
            s.done("act", nc.scalar.activation(sq[:, 0, tl, :], kv, ACT.Square))
            s.done("act", nc.scalar.copy(Kr[:, tl, :], kv), f"a1b{b}")

    def key_norms():
        s.wait("dve", *s.latest("a1b7", "a1rk"))
        r = s.done("dve", nc.vector.tensor_reduce(ss[:, 0, :], sq[:, 0, :, :], AX, ALU.add), "a1Kss")
        s.wait("dve", r)
        r = s.done("dve", nc.vector.tensor_scalar(ss[:, 0, :], ss[:, 0, :], 1.0 / HD, 1e-5,
                                                  ALU.mult, ALU.add))
        s.wait("pool", r, *s.latest("a1Kn"))
        s.done("pool", nc.gpsimd.tensor_tensor(rk, ss[:, 0, :], k.mhalf[:, 0:NT], ALU.pow), "a1rk")

    def normalise_keys():
        s.wait("dve", *s.latest("a1rk", "a1Ktr"))
        s.done("dve", nc.vector.tensor_tensor(Kn, Kr, rk.unsqueeze(2).broadcast_to([P, NT, HD]),
                                              ALU.mult), "a1Kn")

    def values(p):
        w = Wqkv[:, p, :]
        for half in (1, 0):
            b = 6 + half
            s.wait("pe", *s.latest(f"a1b{b}"))
            for j in range(4):
                mm = nc.tensor.matmul(bank[b][:, j * P:(j + 1) * P],
                                      k.cT[:, (4 * half + j) * P:(4 * half + j + 1) * P],
                                      w[:, 384:512], start=True, stop=True)
            vd = s.done("pe", mm, f"a1Quse{p}")
            s.wait("act", vd, *s.latest(f"a1V{p}"))
            s.done("act", nc.scalar.copy(V[:, p, 4 * half:4 * half + 4, :],
                                         bank[b][:, :].rearrange("p (t d) -> p t d", t=4)), f"a1b{b}")
            s.relabel(f"a1Vin{p}", f"a1b{b}")

    def queries(p, half):
        w = Wqkv[:, p, :]
        b = 6 + half
        cols = slice(half * HALF, (half + 1) * HALF)
        s.wait("pe", *s.latest(f"a1b{b}"))
        for c in range(DC):
            mm = nc.tensor.matmul(bank[b][:, :], w[:, c * P:(c + 1) * P], k.xT[:, c, cols],
                                  start=c == 0, stop=c == DC - 1)
        qd = s.done("pe", mm)
        s.wait("act", qd, *s.latest("a1Qss", f"a1S{p}"))
        s.done("act", nc.scalar.activation(
            sq[:, 1, 4 * half:4 * half + 4, :], bank[b][:, :].rearrange("p (t d) -> p t d", t=4), ACT.Square), "a1Qsq")
        s.done("act", nc.scalar.activation(Q[:, p, cols], bank[b][:, :], ACT.Identity, scale=k.col("gq")),
               f"a1b{b}")
        s.relabel(f"a1Qin{p}", f"a1b{b}")

    def query_norms(p):
        s.wait("pe", *s.latest("a1Qsq", "a1b4"))
        for t in range(NT):
            mm = nc.tensor.matmul(bank[4][:, t:t + 1], sq[:, 1, t, :], ones, start=True, stop=True)
        sd = s.done("pe", mm, "a1Qss")
        s.wait("dve", sd, *s.latest(f"a1Qrq"))
        r = s.done("dve", nc.vector.tensor_scalar(ss[:, 1, :], bank[4][:, 0:NT], HD * 1e-5, None,
                                                  ALU.add), "a1b4")
        s.wait("pool", r, *s.latest(f"a1E{p}"))
        r = s.done("pool", nc.gpsimd.tensor_tensor(rq[:, p, :], ss[:, 1, :], k.mhalf[:, 0:NT], ALU.pow), "a1Qrq")
        s.relabel(f"a1rq{p}", "a1Qrq")

    def turn_keys(p, half):
        b = 6 + half
        s.wait("pe", *s.latest(f"a1b{b}", "a1Kn"))
        for j in range(4):
            mm = nc.tensor.transpose(bank[b][:, j * P:(j + 1) * P], Kn[:, 4 * half + j, :], k.ident[:, :])
        td = s.done("pe", mm, "a1Ktr")
        s.wait("act", td, *s.latest(f"a1S{p}"))
        s.done("act", nc.scalar.activation(K[:, p, half * HALF:(half + 1) * HALF], bank[b][:, :],
                                           ACT.Identity, scale=k.col("gk")), f"a1b{b}")
        s.relabel(f"a1Kin{p}", f"a1b{b}")

    def scores(p, b):
        u = b % 2
        s.wait("pe", *s.latest(f"a1Kin{p}", f"a1Qin{p}", f"a1b{u}"))
        for j in range(2):
            mm = nc.tensor.matmul(bank[u][:, j * 256:(j + 1) * 256],
                                  Q[:, p, b * S + j * P:b * S + (j + 1) * P], K[:, p, b * S:(b + 1) * S],
                                  start=True, stop=True)
        sd = s.done("pe", mm, f"a1S{p}")
        s.wait("dve", sd, *s.latest(f"a1rq{p}", f"a1nb{u}", f"a1rs{u}"))
        r = s.done("dve", nc.vector.tensor_reduce(mx[:, u, :], bank[u][:, :].rearrange("p (t d) -> p t d", t=2),
                                                  AX, ALU.max))
        s.wait("dve", r)
        r = s.done("dve", nc.vector.scalar_tensor_tensor(nb[:, u, :], mx[:, u, :], -1.0,
                                                         rq[:, p, 2 * b:2 * b + 2], ALU.mult, ALU.mult))
        s.wait("act", r, *s.latest(f"a1T{u}", f"a1rs{u}"))
        for j in range(2):
            s.done("act", nc.scalar.activation(
                Pr[:, u, j, :], bank[u][:, j * 256:(j + 1) * 256], ACT.Exp, bias=nb[:, u, j:j + 1],
                scale=rq[:, p, 2 * b + j:2 * b + j + 1], accum_out=rs[:, u, j:j + 1]), f"a1b{u}")
        s.relabel(f"a1nb{u}", f"a1b{u}")
        s.relabel(f"a1E{p}", f"a1b{u}")

    def normalise(b):
        u = b % 2
        s.wait("dve", *s.latest(f"a1nb{u}"))
        r = s.done("dve", nc.vector.reciprocal(ri[:, u, :], rs[:, u, :]), f"a1rs{u}")
        s.wait("dve", r)
        for j in range(2):
            s.done("dve", nc.vector.tensor_scalar(Pr[:, u, j, :], Pr[:, u, j, :], ri[:, u, j:j + 1],
                                                  None, ALU.mult), f"a1Pn{u}")

    def transposed(p, b):
        u = b % 2
        s.wait("pe", *s.latest(f"a1Pn{u}", f"a1b{2 + u}"))
        for c in range(2):
            for j in range(2):
                mm = nc.tensor.transpose(bank[2 + u][:, c * 256 + j * P:c * 256 + (j + 1) * P],
                                         Pr[:, u, j, c * P:(c + 1) * P], k.ident[:, :])
        td = s.done("pe", mm, f"a1T{u}")
        eng, engine = ("dve", nc.vector.tensor_copy) if b % 2 else ("act", nc.scalar.copy)
        s.wait(eng, td, *s.latest(f"a1AV{u}"))
        s.done(eng, engine(PT[:, u, :, :], bank[2 + u][:, :].rearrange("p (t d) -> p t d", t=2)), f"a1b{2 + u}")

    def attend(p, b):
        u = b % 2
        s.wait("pe", *s.latest(f"a1b{2 + u}", f"a1Vin{p}", f"a1b{4 + u}"))
        for c in range(2):
            mm = nc.tensor.matmul(bank[4 + u][:, 0:S], V[:, p, 2 * b + c, :], PT[:, u, c, :],
                                  start=c == 0, stop=c == 1)
        od = s.done("pe", mm, f"a1AV{u}")
        s.relabel(f"a1V{p}", f"a1AV{u}")
        eng, engine = ("act", nc.scalar.copy) if b % 2 else ("dve", nc.vector.tensor_copy)
        s.wait(eng, od, *s.latest("a1Ouse"))
        s.done(eng, engine(O[:, p, b * S:(b + 1) * S], bank[4 + u][:, 0:S]), f"a1b{4 + u}")

    def project_out():
        for t2 in range(NT // 2):
            u = t2 % 2
            s.wait("pe", *s.latest(f"a1b{4 + u}", "a1wo0", "a1wo1"))
            for j in range(2):
                t = 2 * t2 + j
                for p in range(2):
                    mm = nc.tensor.matmul(bank[4 + u][:, j * D:(j + 1) * D], O[:, p, t * P:(t + 1) * P],
                                          Wo[:, p, :], start=p == 0, stop=p == 1)
            md = s.done("pe", mm, "a1Ouse")
            s.wait("dve", md, *s.latest(f"a1X{t2}"))
            s.done("dve", nc.vector.scalar_tensor_tensor(
                k.X[:, 2 * t2:2 * t2 + 2, :], bank[4 + u][:, :].rearrange("p (t d) -> p t d", t=2),
                k.tg[:, 1:2], k.X[:, 2 * t2:2 * t2 + 2, :], ALU.mult, ALU.add), f"a1b{4 + u}")
            s.relabel(f"a1X{t2}", f"a1b{4 + u}")

    def head(p, follow):
        n = 1 - p
        scores(p, 1)
        normalise(0)
        if follow:
            keys(n)
        transposed(p, 0)
        normalise(1)
        scores(p, 2)
        if follow:
            key_norms()
            queries(n, 0)
        attend(p, 0)
        transposed(p, 1)
        normalise(2)
        scores(p, 3)
        if follow:
            normalise_keys()
            queries(n, 1)
        attend(p, 1)
        transposed(p, 2)
        normalise(3)
        if follow:
            turn_keys(n, 1)
            query_norms(n)
            turn_keys(n, 0)
            values(n)
        attend(p, 2)
        transposed(p, 3)
        if follow:
            scores(n, 0)
        attend(p, 3)

    load_qkv(0, 0)
    load_qkv(1, 1)
    load_o(0, 0)
    load_o(1, 1)
    s.wait("pool", *readers)
    one = s.done("pool", nc.gpsimd.memset(ones, 1.0))
    ready = k.layernorm(readers)
    s.wait("pe", one, k.ctx_in, *ready[0], *ready[1], *k.bank_free)
    s.wait("act", *readers)
    s.wait("dve", *readers)
    keys(0)
    key_norms()
    normalise_keys()
    queries(0, 0)
    queries(0, 1)
    query_norms(0)
    turn_keys(0, 1)
    turn_keys(0, 0)
    values(0)
    scores(0, 0)
    s.settle("a1")
    with s.repeat(NH // 2 - 1) as i:
        load_qkv(0, i * 2 + 2)
        head(0, True)
        load_qkv(1, i * 2 + 3)
        head(1, True)
        project_out()
        load_o(0, i * 2 + 2)
        load_o(1, i * 2 + 3)
    head(0, True)
    head(1, False)
    project_out()
    k.x_ready = [s.last["a1X1"], s.last["a1X3"]]
    k.bank_free = [s.last[f"a1b{b}"] for b in range(8)]
    return [s.last[n] for n in ("a1Ouse", "a1X3", "a1b0", "a1b1", "a1b4", "a1b5", "a1b6", "a1b7", "a1rq1")]


def attention2(k, readers):
    nc, s = k.nc, k.s
    NH, HD, KM = 16, 16, S - SET2
    SCALE = HD ** -0.5
    k.at = 0
    bank = k.bank
    W = k.place(6, D)
    Wo = k.place(DC, D)
    bias = k.place(2, D)
    ind = k.place(2, P)
    bK, bQ = k.place(2, D), k.place(D)
    bO, bV = k.place(D), k.place(D)
    mean = k.place(4 * NH)
    N = k.place(NT, 2, D)
    V = k.place(NT, NH, 32)
    KT = k.place(DC, T)
    QT = k.place(DC, T)
    xc, sq = k.place(4, 2 * NH, HD), k.place(2, 2 * NH, HD)
    va, rt = k.place(4, 2 * NH), k.place(4, 2 * NH)
    aff = k.place(10)
    s.wait("sp", *readers)
    l1 = s.loaded("a2w", nc.sync.dma_start(W, k.io["w2"]))
    s.wait("act", *readers)
    l2 = s.loaded("a2b", nc.scalar.dma_start(bias[0:2], k.io["bias2"]))
    l3 = s.loaded("a2i", nc.scalar.dma_start(ind[0:2], k.io["ind2"]))
    l6 = s.loaded("a2a", nc.scalar.dma_start(aff, k.io["aff2"]))
    l5 = s.loaded("a2o", nc.sync.dma_start(Wo, k.io["wo2"]))
    s.wait("pool", *readers)
    for b in range(B):
        nc.gpsimd.memset(V[:, 2 * b, :, HD:32], 0.0)
    bv = s.done("pool", nc.gpsimd.tensor_tensor(bV, k.row("bv"), k.row("bvd"), ALU.add))
    bo = s.done("pool", nc.gpsimd.tensor_scalar(bO, k.row("bo"), k.tg[:, 2:3], None, ALU.mult))

    def centre(dst, v, n):
        r = s.done("dve", nc.vector.tensor_reduce(mean[:, 0:n], v, AX, ALU.add))
        s.wait("dve", r)
        r = s.done("dve", nc.vector.tensor_scalar(mean[:, 0:n], mean[:, 0:n], 1.0 / HD, None, ALU.mult))
        s.wait("dve", r)
        r = s.done("dve", nc.vector.tensor_tensor(
            dst, v, mean[:, 0:n].unsqueeze(2).broadcast_to([P, n, HD]), ALU.subtract))
        s.wait("dve", r)
        return r

    def heads(v):
        return v.rearrange("p (h d) -> p h d", d=HD)

    s.wait("pe", l2, l3, *readers, *k.bank_free)
    for j in range(2):
        mm = nc.tensor.matmul(bank[7][:, j * D:(j + 1) * D], ind[0:2, j, :], bias[0:2, 0, :],
                              start=True, stop=True)
    bd = s.done("pe", mm)
    s.wait("dve", l1, *readers)
    wv = heads(W[:, 0:4, :].rearrange("p a n -> p (a n)"))
    wc = centre(wv, wv, 4 * NH)
    centre(heads(bQ), heads(k.row("bq")), NH)
    s.wait("dve", bd)
    bc = centre(heads(bK.rearrange("p j n -> p (j n)")), heads(bank[7]), 2 * NH)
    s.last["a2p7"] = bc
    ready = k.layernorm(readers)
    s.wait("act", bv, bo, l6)
    s.wait("pool", *ready[1], *ready[0])
    for h in range(2):
        xb = s.done("pool", nc.gpsimd.tensor_tensor(
            k.X[:, 4 * h:4 * h + 4, :], k.X[:, 4 * h:4 * h + 4, :],
            bO.unsqueeze(1).broadcast_to([P, 4, D]), ALU.add))
    ring = [0]

    def next_bank():
        b = 4 + ring[0] % 4
        ring[0] += 1
        s.wait("pe", s.last.get(f"a2p{b}"))
        return b

    def biased(n, b, biases):
        s.wait("dve", s.last.get(f"a2n{n - 4}"))
        r = s.done("dve", nc.vector.tensor_tensor(xc[:, n % 4].rearrange("p h d -> p (h d)"), bank[b],
                                                  biases, ALU.add), f"a2p{b}")
        s.wait("act", r, s.last.get(f"a2v{n - 2}"))
        s.done("act", nc.scalar.activation(sq[:, n % 2], xc[:, n % 4], ACT.Square), f"a2s{n}")

    def variance(n):
        s.wait("dve", s.last[f"a2s{n}"])
        r = s.done("dve", nc.vector.tensor_reduce(va[:, n % 4, :], sq[:, n % 2], AX, ALU.add), f"a2v{n}")
        s.wait("dve", r)
        r = s.done("dve", nc.vector.tensor_scalar(va[:, n % 4, :], va[:, n % 4, :], 1.0 / HD, 1e-6,
                                                  ALU.mult, ALU.add))
        s.wait("dve", r)
        r = s.done("dve", nc.vector.reciprocal(va[:, n % 4, :], va[:, n % 4, :]))
        s.wait("act", r)
        s.done("act", nc.scalar.activation(rt[:, n % 4, :], va[:, n % 4, :], ACT.Sqrt), f"a2r{n}")

    def scaled(n):
        s.wait("dve", s.last[f"a2r{n}"])
        b, q = n % 4, n // 4
        s.done("dve", nc.vector.tensor_tensor(
            N[:, 2 * b:2 * b + 2, q, :].rearrange("p t (h d) -> p t h d", d=HD),
            xc[:, n % 4].rearrange("p (t h) d -> p t h d", t=2),
            rt[:, n % 4, :].rearrange("p (t h) -> p t h", t=2).unsqueeze(3).broadcast_to([P, 2, NH, HD]),
            ALU.mult), f"a2n{n}")

    def advance(n):
        if n - 1 >= 0:
            variance(n - 1)
        if n - 2 >= 0:
            scaled(n - 2)

    s.wait("pe", wc, bc, k.sets_in)
    for b in range(B):
        first, sets = k.cT[:, 2 * b * P:(2 * b + 1) * P], [k.sets[:, n, b, :] for n in range(2)]
        kb = next_bank()
        nc.tensor.matmul(bank[kb][:, 0:D], first, W[:, 2, :], start=True, stop=True)
        nc.tensor.matmul(bank[kb][:, D:], sets[0], W[:, 2, :], start=True, stop=False)
        kd = s.done("pe", nc.tensor.matmul(bank[kb][:, D:], sets[1], W[:, 3, :], start=False, stop=True))
        vb = next_bank()
        nc.tensor.matmul(bank[vb][:, 0:D], first, W[:, 4, :], start=True, stop=True)
        vd = s.done("pe", nc.tensor.matmul(bank[vb][:, D:], sets[0], W[:, 4, :], start=True, stop=True))
        v2 = next_bank()
        v2d = s.done("pe", nc.tensor.matmul(bank[v2][:, 0:D], sets[1], W[:, 5, :], start=True, stop=True))
        s.wait("dve", kd)
        biased(b, kb, bK.rearrange("p j n -> p (j n)"))
        s.wait("act", vd)
        s.done("act", nc.scalar.copy(
            V[:, 2 * b:2 * b + 2, :, 0:HD].rearrange("p t h d -> p (t h) d"), heads(bank[vb])), f"a2p{vb}")
        s.wait("act", v2d)
        vin = s.done("act", nc.scalar.copy(V[:, 2 * b + 1, :, HD:32], heads(bank[v2][:, 0:D])), f"a2p{v2}")
        advance(b)
    for b in range(B):
        qb = next_bank()
        for j in range(2):
            for c in range(DC):
                t = 2 * b + j
                mm = nc.tensor.matmul(bank[qb][:, j * D:(j + 1) * D], k.xT[:, c, t * P:(t + 1) * P],
                                      W[:, c, :], start=c == 0, stop=c == DC - 1)
        qd = s.done("pe", mm)
        s.wait("dve", qd)
        s.wait("dve", s.last.get(f"a2n{b}"))
        s.done("dve", nc.vector.tensor_tensor(
            xc[:, b].rearrange("p (t h) d -> p t (h d)", t=2), bank[qb].rearrange("p (t n) -> p t n", t=2),
            bQ.unsqueeze(1).broadcast_to([P, 2, D]), ALU.add), f"a2p{qb}")
        s.wait("act", s.last[f"a2p{qb}"], s.last[f"a2v{b + 2}"])
        s.done("act", nc.scalar.activation(sq[:, b % 2], xc[:, b], ACT.Square), f"a2s{b + 4}")
        advance(b + 4)
    advance(2 * B)
    scaled(2 * B - 1)
    def affine(dst, src, n):
        return nc.scalar.activation(dst, src, ACT.Identity, scale=aff[:, n:n + 1],
                                    bias=aff[:, n + 1:n + 2])

    for q in range(2):
        for half in range(2):
            for c in range(DC):
                b = (2 * half + c) % 4
                s.wait("pe", s.last[f"a2n{4 * q + 2 * half + 1}"], s.last.get(f"a2q{b}"))
                for j in range(4):
                    mm = nc.tensor.transpose(bank[b][:, j * P:(j + 1) * P],
                                             N[:, 4 * half + j, q, c * P:(c + 1) * P], k.ident[:, :])
                td = s.done("pe", mm)
                s.wait("act", td)
                cols = slice(half * HALF, (half + 1) * HALF)
                if q:
                    made = s.done("act", affine(QT[:, c, cols], bank[b], 0), f"a2q{b}")
                else:
                    dv = KT[:, c, cols].rearrange("p (b t) -> p b t", b=2)
                    sv = bank[b].rearrange("p (b t) -> p b t", b=2)
                    s.done("act", affine(dv[:, :, 0:KM], sv[:, :, 0:KM], 2))
                    s.done("act", affine(dv[:, :, KM:S], sv[:, :, KM:S], 4), f"a2q{b}")

    Kb = k.place(DC, S)
    Qb = k.place(4, DC, S)
    Vb = k.place(2, NH, 32)
    OS = k.place(4, S)
    Pr = k.place(2, 4, S)
    PT = k.place(4, 2, S)
    mx, nb, mxd = k.place(2, 4), k.place(2, 4), k.place(2, 4)
    sums, inv = k.place(2, NH, 2), k.place(2, NH, 2)
    Ob, Od = k.place(2, NH, HD), k.place(2, NH, HD)
    obv = Ob.rearrange("p j h d -> p j (h d)")
    OT = k.place(DC, S)
    for e in ("pe", "dve", "act", "pool"):
        s.wait(e, made, vin, l5, xb, s.last["a2p4"], s.last["a2p5"], s.last["a2p6"], s.last["a2p7"])

    def fetch(b):
        cols = bass.ds(b * S, S)
        s.wait("dve", *s.latest("a2S"))
        s.wait("pool", *s.latest("a2S"))
        s.done("dve", nc.vector.tensor_scalar(Qb[:, 0], QT[:, :, cols], aff[:, 6:7], None, ALU.mult))
        s.done("dve", nc.vector.tensor_copy(Kb, KT[:, :, cols]))
        s.done("dve", nc.vector.tensor_scalar(Qb[:, 1], QT[:, :, cols], aff[:, 7:8], None, ALU.mult), "a2Qb")
        for v in (2, 3):
            s.done("pool", nc.gpsimd.tensor_tensor(
                Qb[:, v], QT[:, :, cols], aff[:, 6 + v:7 + v].unsqueeze(2).broadcast_to([P, DC, S]),
                ALU.mult), "a2Qc")

    def fetch_values(b, half):
        s.wait("pool", *s.latest("a2AV1"))
        hs = slice(half * 8, half * 8 + 8)
        s.done("pool", nc.gpsimd.tensor_copy(Vb[:, :, hs, :], V[:, bass.ds(b * 2, 2), hs, :]), f"a2Vb{half}")

    def scores(g):
        u, h0 = g % 2, 2 * g
        s.wait("pe", *s.latest(f"a2E{u}", f"a2sub{u}", "a2Qb"))
        if g % 2:
            s.wait("pe", *s.latest("a2Qc"))
        for h in (h0, h0 + 1):
            c, r, e = h // 8, h % 8 // 4 * 64, h % 2
            for j in range(2):
                mm = nc.tensor.matmul(
                    bank[2 * u + e][:, j * S:(j + 1) * S], Qb[r:r + 64, h % 4, c, j * P:(j + 1) * P],
                    Kb[r:r + 64, c, :], start=True, stop=True)
        sd = s.done("pe", mm, "a2S")
        v = k.psum[:, 2 * u * 512:(2 * u + 2) * 512].rearrange("p (a t) -> p a t", t=S)
        pr = Pr[:, u]
        s.wait("dve", sd, *s.latest(f"a2T{u}", f"a2E{u}", f"a2sub{u}"))
        r1 = s.done("dve", nc.vector.tensor_reduce(mxd[:, u, :], v[:, :, KM:S], AX, ALU.max))
        r = s.done("dve", nc.vector.tensor_reduce(mx[:, u, :], v[:, :, 0:KM], AX, ALU.max))
        s.wait("dve", r1)
        s.done("dve", nc.vector.tensor_tensor(
            pr[:, :, KM:S], v[:, :, KM:S], mxd[:, u, :].unsqueeze(2).broadcast_to([P, 4, S - KM]),
            ALU.subtract), f"a2sub{u}")
        s.wait("dve", r)
        s.done("dve", nc.vector.tensor_scalar(nb[:, u, :], mx[:, u, :], -SCALE, None, ALU.mult), f"a2nb{u}")

    def exponentials(g):
        u, h0 = g % 2, 2 * g
        v, pr = k.psum[:, 2 * u * 512:(2 * u + 2) * 512].rearrange("p (a t) -> p a t", t=S), Pr[:, u]
        s.wait("act", *s.latest(f"a2nb{u}", f"a2inv{g}", f"a2T{u}"))
        for a in range(4):
            s.done("act", nc.scalar.activation(pr[:, a, 0:KM], v[:, a, 0:KM], ACT.Exp, bias=nb[:, u, a:a + 1],
                                               scale=SCALE, accum_out=sums[:, a % 2, h0 + a // 2, 0:1]))
        s.done("act", nc.scalar.activation(pr[:, :, KM:S], pr[:, :, KM:S], ACT.Exp, scale=SCALE),
               f"a2E{u}")

    def second_sums(g):
        u = g % 2
        s.wait("dve", *s.latest(f"a2E{u}"))
        s.done("dve", nc.vector.tensor_reduce(
            sums[:, :, 2 * g:2 * g + 2, 1].rearrange("p j h -> p h j"),
            Pr[:, u, :, KM:S].rearrange("p (h j) t -> p h j t", h=2), AX, ALU.add), f"a2sum{u}")

    def inverse(g):
        s.wait("dve", *s.latest(f"a2sum{g % 2}", "a2O"))
        s.done("dve", nc.vector.reciprocal(inv[:, :, 2 * g:2 * g + 2, :], sums[:, :, 2 * g:2 * g + 2, :]),
               f"a2inv{g}")

    def transposed(g):
        u = g % 2
        s.wait("pe", *s.latest(f"a2E{u}"))
        for w in range(2):
            s.wait("pe", *s.latest(f"a2t{w}"))
            for c in range(2):
                for j in range(2):
                    mm = nc.tensor.transpose(bank[4 + w][:, c * S + j * P:c * S + (j + 1) * P],
                                             Pr[:, u, 2 * w + j, c * P:(c + 1) * P], k.ident[:, :])
            td = s.done("pe", mm, f"a2T{u}")
            eng, engine = ("dve", nc.vector.tensor_copy) if w else ("act", nc.scalar.copy)
            s.wait(eng, td, *s.latest(f"a2AV{u}"))
            s.done(eng, engine(PT[:, 2 * u + w, :, :], bank[4 + w].rearrange("p (t d) -> p t d", t=2)),
                   f"a2t{w}")
            s.relabel(f"a2PT{u}{w}", f"a2t{w}")

    def attend(g):
        u = g % 2
        s.wait("pe", *s.latest("a2OSa", "a2OS", "a2O", f"a2Vb{g // 4}"))
        for w in range(2):
            h = 2 * g + w
            s.wait("pe", *s.latest(f"a2PT{u}{w}"))
            at = 6 * 512 + h // 4 * S
            for c in range(2):
                mm = nc.tensor.matmul(
                    k.psum[h % 4 * 32:(h % 4 + 1) * 32, at:at + S], Vb[:, c, h, :],
                    PT[:, 2 * u + w, c, :], start=c == 0, stop=c == 1)
        return s.done("pe", mm, f"a2AV{u}")

    def turned():
        s.wait("pe", *s.latest("a2OSa", "a2OS"))
        for j in range(2):
            for q in range(4):
                mm = nc.tensor.transpose(bank[6 + j][:, q * P:(q + 1) * P], OS[:, q, j * P:(j + 1) * P],
                                         k.ident[:, :])
        s.done("pe", mm, "a2OSr")

    def normalised():
        s.wait("dve", *s.latest("a2OSr", "a2inv7", "a2OTr"))
        o = k.psum[:, 6 * 512:8 * 512].rearrange("p (h e d) -> p h e d", e=2, d=HD)
        iv = inv.rearrange("p j h e -> p (j h) e")
        for e, dst in ((0, Ob), (1, Od)):
            r = s.done("dve", nc.vector.tensor_tensor(
                dst.rearrange("p j h d -> p (j h) d"), o[:, :, e, :],
                iv[:, :, e].unsqueeze(2).broadcast_to([P, 2 * NH, HD]), ALU.mult), "a2O")
        s.wait("pool", r)
        r = s.done("pool", nc.gpsimd.tensor_tensor(Ob, Ob, Od, ALU.add))
        s.wait("pool", r)
        s.done("pool", nc.gpsimd.tensor_tensor(obv, obv, bV.unsqueeze(1).broadcast_to([P, 2, D]), ALU.add),
               "a2Ob")

    def out_transposed():
        s.wait("pe", *s.latest("a2Ob", "a2t0"))
        for c in range(DC):
            for j in range(2):
                mm = nc.tensor.transpose(bank[4][:, c * S + j * P:c * S + (j + 1) * P],
                                         obv[:, j, c * P:(c + 1) * P], k.ident[:, :])
        td = s.done("pe", mm, "a2OTr")
        s.wait("act", td, *s.latest("a2Y"))
        s.done("act", nc.scalar.copy(OT, bank[4].rearrange("p (c t) -> p c t", c=DC)), "a2OT")
        s.relabel("a2t0", "a2OT")

    def project(b):
        s.wait("pe", *s.latest("a2OT", "a2t1"))
        for j in range(2):
            for c in range(DC):
                mm = nc.tensor.matmul(bank[5][:, j * D:(j + 1) * D], OT[:, c, j * P:(j + 1) * P],
                                      Wo[:, c, :], start=c == 0, stop=c == DC - 1)
        yd = s.done("pe", mm, "a2Y")
        s.wait("dve", yd)
        X2 = k.X[:, bass.ds(b * 2, 2), :]
        s.done("dve", nc.vector.scalar_tensor_tensor(
            X2, bank[5].rearrange("p (t d) -> p t d", t=2), k.tg[:, 2:3], X2, ALU.mult, ALU.add), "a2t1")
        return yd

    def batch(b, prior, follow):
        steps = NH // 2
        for g in range(steps):
            if g + 1 < steps:
                scores(g + 1)
            elif follow:
                scores(0)
            second_sums(g)
            transposed(g)
            if g + 1 < steps or follow:
                exponentials((g + 1) % steps)
            if prior is not None:
                if g == 0:
                    turned()
                    normalised()
                elif g == 2:
                    out_transposed()
                elif g == 3:
                    project(prior)
            inverse(g)
            if g == 0:
                fetch_values(b, 1)
            if g == steps - 2 and follow:
                fetch(b + 1)
                fetch_values(b + 1, 0)
            if g >= 1:
                attend(g - 1)
        ad = attend(steps - 1)
        s.wait("act", ad, *s.latest("a2OSr"))
        s.wait("dve", ad, *s.latest("a2OSr"))
        s.done("act", nc.scalar.copy(OS[:, 0:2, :], bank[6].rearrange("p (q t) -> p q t", q=2)), "a2OSa")
        s.done("dve", nc.vector.tensor_copy(OS[:, 2:4, :], bank[7].rearrange("p (q t) -> p q t", q=2)),
               "a2OS")

    fetch(0)
    fetch_values(0, 0)
    scores(0)
    exponentials(0)
    batch(0, None, True)
    s.settle("a2")
    with s.repeat(B - 2) as it:
        batch(it + 1, it, True)
    batch(B - 1, B - 2, False)
    turned()
    normalised()
    out_transposed()
    yd = project(B - 1)
    k.x_ready = [s.last["a2t1"]] * 2
    k.bank_free = [s.last["a2t1"]] * 8
    return [yd, s.last["a2t1"], s.last["a2E0"], s.last["a2E1"], s.last["a2t0"]]


def quantised_layer(k, readers):
    nc, s = k.nc, k.s
    EPS, QMAX, MAGIC = 1e-6, 127.0, 1.5 * 2.0 ** 23
    k.at = 0
    bank = k.bank
    w1 = k.place(NT, D)
    w1T = k.place(DC, T)
    w2 = k.place(NT, C)
    XS, WS = k.place(NT, D), k.place(NT, D)
    XQ, WQ = k.place(NT, D, dt=BF16), k.place(NT, D, dt=BF16)
    XQT, WQT = k.place(DC, T, dt=BF16), k.place(DC, T, dt=BF16)
    diag = k.place(8, P)
    sB = k.place(NT, P)
    hid, act = k.place(NT, D), k.place(NT, P)
    ones = k.place(P)
    identb = k.place(P, dt=BF16)
    small = k.place(16, 8)
    s.wait("sp", *readers)
    lw = [s.loaded("q1", nc.sync.dma_start(w1, k.io["fside"])),
          s.loaded("q1T", nc.sync.dma_start(w1T, k.io["fsideT"])),
          s.loaded("q2", nc.sync.dma_start(w2, k.io["ctok"]))]
    s.wait("pool", *readers)
    ready = k.layernorm(readers)
    s.wait("pool", k.ident_in)
    nc.gpsimd.memset(ones, 1.0)
    cst = s.done("pool", nc.gpsimd.tensor_copy(identb, k.ident[:, :]))
    for e in ("dve", "act", "pe", "pool"):
        s.wait(e, *readers, *lw, cst, *ready[0], *ready[1], *k.bank_free)

    def dve(ins):
        t = s.done("dve", ins)
        s.wait("dve", t)
        return t

    def rows_of(cols, b0):
        t = dve(nc.vector.tensor_tensor(diag, k.ident[:, :].unsqueeze(1).broadcast_to([P, 8, P]),
                                        cols.unsqueeze(2).broadcast_to([P, 8, P]), ALU.mult))
        s.wait("pe", t)
        dv = diag.rearrange("p a b -> p (a b)")
        for h in range(2):
            mm = nc.tensor.matmul(bank[b0 + h], ones, dv[:, h * 512:(h + 1) * 512], start=True, stop=True)
        t = s.done("pe", mm)
        s.wait("dve", t)
        s.wait("act", t)
        return k.psum[:, b0 * 512:(b0 + 2) * 512]

    def quantise(v, q, scale, inv, n):
        dve(nc.vector.tensor_reduce(scale, v, AX, ALU.max, apply_absolute_value=True))
        dve(nc.vector.tensor_scalar(scale, scale, EPS, 1.0 / QMAX, ALU.max, ALU.mult))
        dve(nc.vector.reciprocal(inv, scale))
        for t in range(NT):
            d = s.done("dve", nc.vector.tensor_scalar(v[:, t, :], v[:, t, :], inv[:, t:t + 1], MAGIC,
                                                      ALU.mult, ALU.add))
        s.wait("dve", d)
        dve(nc.vector.tensor_scalar(v, v, MAGIC + QMAX, MAGIC - QMAX, ALU.min, ALU.max))
        return dve(nc.vector.tensor_scalar(q, v, MAGIC, None, ALU.subtract))

    def linear(x_tok, x_feat, w_rows, w_feat, nd, evacuate):
        ax, aw, sm, rs = (small[:, j, 0:nd * B] for j in range(4))
        xsc, wsc, xin, win = (small[:, j, :] for j in range(4, 8))
        F = nd * P
        dve(nc.vector.tensor_reduce(ax, x_feat, AX, ALU.max, apply_absolute_value=True))
        dve(nc.vector.tensor_reduce(aw, w_feat, AX, ALU.max, apply_absolute_value=True))
        dve(nc.vector.tensor_scalar(ax, ax, EPS, None, ALU.max))
        dve(nc.vector.tensor_scalar(aw, aw, EPS, None, ALU.max))
        dve(nc.vector.reciprocal(aw, aw))
        t = dve(nc.vector.tensor_tensor(sm, ax, aw, ALU.mult))
        s.wait("pool", t)
        t = s.done("pool", nc.gpsimd.tensor_tensor(sm, sm, k.phalf[:, 0:nd * B], ALU.pow))
        s.wait("dve", t)
        dve(nc.vector.tensor_scalar(sm, sm, EPS, None, ALU.max))
        dve(nc.vector.reciprocal(rs, sm))

        def scaled(dst, src, cols, b0):
            if nd == 2:
                both = small[:, 8 + b0 // 2, :].rearrange("p (b c) -> p b c", c=nd)
                dve(nc.vector.tensor_copy(both, cols.rearrange("p (c b) -> p b c", c=nd)))
                cols = small[:, 8 + b0 // 2, :]
            else:
                both = small[:, 8 + b0 // 2, :]
                dve(nc.vector.memset(both, 0.0))
                dve(nc.vector.tensor_copy(both[:, 0:B], cols))
                cols = both
            r = rows_of(cols, b0)[:, 0:B * F].rearrange("p (b f) -> p b f", b=B)
            return dve(nc.vector.tensor_tensor(
                dst.rearrange("p (b j) f -> p b j f", b=B), src.rearrange("p (b j) f -> p b j f", b=B),
                r.unsqueeze(2).broadcast_to([P, B, 2, F]), ALU.mult))

        xs, ws = XS[:, :, 0:F], WS[:, :, 0:F]
        xq, wq = XQ[:, :, 0:F], WQ[:, :, 0:F]
        scaled(xs, x_tok, rs, 0)
        tq = quantise(xs, xq, xsc, xin, F)
        scaled(ws, w_rows, sm, 2)
        tw = quantise(ws, wq, wsc, win, F)
        n = 0
        for src, dst, ready_q in ((xq, XQT, tq), (wq, WQT, tw)):
            s.wait("pe", ready_q)
            for c in range(nd):
                bb = 4 + n % 2
                n += 1
                s.wait("pe", s.last.get(f"qb{bb}"))
                half = bank[bb].bitcast(BF16)
                for t in range(NT):
                    mm = nc.tensor.transpose(half[:, t * P:(t + 1) * P], src[:, t, c * P:(c + 1) * P],
                                             identb)
                td = s.done("pe", mm)
                s.wait("act", td)
                s.done("act", nc.scalar.copy(dst[:, c, :], half), f"qb{bb}")
        wr = rows_of(wsc, 0)
        tr = dve(nc.vector.tensor_copy(sB.rearrange("p t d -> p (t d)"), wr))
        s.wait("pe", s.last["qb4"], s.last["qb5"])
        for b in range(B):
            for j in range(2):
                t, bb = 2 * b + j, 4 + b % 4
                if j == 0:
                    s.wait("pe", s.last.get(f"qo{bb}"))
                for c in range(nd):
                    mm = nc.tensor.matmul(bank[bb][:, j * D:(j + 1) * D], XQT[:, c, t * P:(t + 1) * P],
                                          WQT[:, c, b * D:(b + 1) * D], start=c == 0, stop=c == nd - 1)
            td = s.done("pe", mm)
            s.wait("dve", td)
            for j in range(2):
                t = 2 * b + j
                r = s.done("dve", nc.vector.scalar_tensor_tensor(
                    hid[:, t, :], bank[bb][:, j * D:(j + 1) * D], xsc[:, t:t + 1],
                    sB[:, 2 * b:2 * b + 2, :].rearrange("p t d -> p (t d)"), ALU.mult, ALU.mult),
                    f"qo{bb}")
            evacuate(b, r)

    def gated(b, r):
        s.wait("act", r)
        tiles = slice(2 * b, 2 * b + 2)
        g = s.done("act", nc.scalar.activation(act[:, tiles, :], hid[:, tiles, 0:P], ACT.Silu))
        s.wait("dve", g)
        s.done("dve", nc.vector.tensor_tensor(act[:, tiles, :], act[:, tiles, :], hid[:, tiles, P:D],
                                              ALU.mult), "qact")

    linear(k.xn[:, :, :], k.xT[:, :, :].rearrange("p c (b t) -> p (c b) t", b=B), w1,
           w1T.rearrange("p c (b t) -> p (c b) t", b=B), DC, gated)
    s.wait("pe", s.last["qact"], s.last["qo6"], s.last["qo7"])
    for t in range(NT):
        mm = nc.tensor.transpose(bank[6 + t // 4][:, t % 4 * P:(t % 4 + 1) * P], act[:, t, :],
                                 k.ident[:, :])
    td = s.done("pe", mm)
    s.wait("dve", td, s.last["qact"])
    s.wait("pe", s.last["qo4"], s.last["qo5"])

    def added(b, r):
        s.wait("dve", r)
        X2 = k.X[:, 2 * b:2 * b + 2, :]
        s.done("dve", nc.vector.scalar_tensor_tensor(
            X2, hid[:, 2 * b:2 * b + 2, :], k.tg[:, 3:4], X2, ALU.mult, ALU.add), f"qx{b // 2}")

    linear(act, k.psum[:, 6 * 512:8 * 512].rearrange("p (b t) -> p b t", b=B), w2,
           k.cT[:, :].rearrange("p (b t) -> p b t", b=B), 1, added)
    k.x_ready = [s.last["qx0"], s.last["qx1"]]
    k.bank_free = [s.last["qx1"]] * 8
    return [s.last["qx1"], s.last["qb4"], s.last["qb5"], td]


def chosen_ffn(k, readers):
    nc, s = k.nc, k.s
    KEEP, NF = KEEP3, 8
    k.at = 0
    bank = k.bank
    W1, W2 = k.place(DC, NF, P), k.place(NF, D)
    wr = k.place(DC, B, B)
    w4, left, top, mask = k.place(S), k.place(S), k.place(8), k.place(S)
    pos, zero = k.place(S), k.place(S)
    R = k.place(S)
    RT = k.place(2, 96)
    sel = k.place(NT, P)
    selT = k.place(NT, P)
    xg = k.place(DC, 2 * P)
    H = k.place(NF, 2 * P)
    blk = k.place(2, D)
    s.wait("sp", *readers)
    l0 = s.loaded("cr", nc.sync.dma_start(wr, k.io["router3"]))
    l1 = s.loaded("c1", nc.sync.dma_start(W1, k.io["w31"]))
    l2 = s.loaded("c2", nc.sync.dma_start(W2, k.io["w32"]))
    s.wait("pool", *readers)
    nc.gpsimd.memset(zero, 0.0)
    cleared = s.done("pool", nc.gpsimd.memset(R, 0.0))
    ready = k.layernorm(readers)
    for e in ("dve", "act", "pe"):
        s.wait(e, *readers, cleared, *ready[0], *ready[1], *k.bank_free)

    def dve(ins):
        t = s.done("dve", ins)
        s.wait("dve", t)
        return t

    s.wait("pe", l0)
    for b in range(B):
        for c in range(DC):
            mm = nc.tensor.matmul(bank[0][0:B, 0:S], wr[:, c, b, :], k.xT[:, c, b * S:(b + 1) * S],
                                  start=b == 0 and c == 0, stop=b == B - 1 and c == DC - 1)
    t = s.done("pe", mm)
    s.wait("dve", t)
    r4 = slice(0, B)
    dve(nc.vector.tensor_scalar(w4[r4], bank[0][r4, 0:S], k.row("b_r")[r4], None, ALU.add))
    dve(nc.vector.tensor_copy(left[r4], w4[r4]))
    for n in range(KEEP // 8):
        dve(nc.vector.max(top[r4], left[r4]))
        if n < KEEP // 8 - 1:
            dve(nc.vector.match_replace(left[r4], top[r4], left[r4], -BIG))
    dve(nc.vector.tensor_scalar(mask[r4], w4[r4], top[r4, 7:8], None, ALU.is_gt))
    dve(nc.vector.tensor_tensor_scan(pos[r4], mask[r4], zero[r4], 0.0, ALU.add, ALU.add))
    dve(nc.vector.scalar_tensor_tensor(R[r4], pos[r4], k.col("slot0")[r4], mask[r4], ALU.add, ALU.mult))
    dve(nc.vector.tensor_scalar(R[r4], R[r4], 1.0, None, ALU.subtract))
    dve(nc.vector.tensor_tensor(R[32:32 + B], w4[r4], mask[r4], ALU.mult))
    t = dve(nc.vector.tensor_scalar(R[64:64 + B], mask[r4], -1.0, 1.0, ALU.mult, ALU.add))
    s.wait("pe", t)
    for j in range(2):
        mm = nc.tensor.transpose(bank[1][:, j * P:j * P + 96], R[0:96, j * P:(j + 1) * P],
                                 k.ident[0:96, 0:96])
    t = s.done("pe", mm)
    s.wait("dve", t)
    b1v = bank[1][:, 0:2 * P].rearrange("p (j n) -> p j n", j=2)
    dve(nc.vector.tensor_copy(RT[:, :, 0:32], b1v[:, :, 0:32]))
    rt = dve(nc.vector.tensor_scalar(RT[:, :, 32:96], b1v[:, :, 32:96], k.tg[:, 7:8], None, ALU.mult))
    for t8 in range(NT):
        b, j = t8 // 2, t8 % 2
        t = s.done("dve", nc.vector.tensor_scalar(sel[:, t8, :], k.row("iota"), RT[:, j, b:b + 1], None,
                                                  ALU.is_equal))
    s.wait("pe", t)
    for c in range(DC):
        for t8 in range(NT):
            g = t8 // 4
            mm = nc.tensor.matmul(bank[2][:, (2 * c + g) * P:(2 * c + g + 1) * P],
                                  k.xn[:, t8, c * P:(c + 1) * P], sel[:, t8, :],
                                  start=t8 % 4 == 0, stop=t8 % 4 == 3)
    t = s.done("pe", mm)
    s.wait("act", t)
    xgd = s.done("act", nc.scalar.copy(xg, bank[2].rearrange("p (c n) -> p c n", c=DC)))
    for t8 in range(NT):
        mm = nc.tensor.transpose(bank[6 + t8 // 4][:, t8 % 4 * P:(t8 % 4 + 1) * P], sel[:, t8, :],
                                 k.ident[:, :])
    t = s.done("pe", mm)
    s.wait("dve", t)
    stt = s.done("dve", nc.vector.tensor_copy(selT.rearrange("p t n -> p (t n)"),
                                              k.psum[:, 6 * 512:8 * 512]))
    for t8 in range(NT):
        b, j = t8 // 2, t8 % 2
        ps = s.done("dve", nc.vector.scalar_tensor_tensor(
            k.X[:, t8, :], k.xn[:, t8, :], RT[:, j, 64 + b:65 + b], k.X[:, t8, :], ALU.mult, ALU.add))
    s.wait("pe", xgd, l1)
    for f in range(NF):
        bb = 3 + f % 2
        s.wait("pe", s.last.get(f"cb{bb}"))
        for c in range(DC):
            mm = nc.tensor.matmul(bank[bb][:, 0:2 * P], W1[:, c, f, :], xg[:, c, :], start=c == 0,
                                  stop=c == DC - 1)
        t = s.done("pe", mm)
        s.wait("act", t)
        hd = s.done("act", nc.scalar.activation(H[:, f, :], bank[bb][:, 0:2 * P], ACT.Gelu_apprx_tanh,
                                                bias=k.col("b1", f)), f"cb{bb}")
    s.wait("pe", hd, l2)
    for g in range(2):
        for f in range(NF):
            mm = nc.tensor.matmul(bank[5][:, g * D:(g + 1) * D], H[:, f, g * P:(g + 1) * P], W2[:, f, :],
                                  start=f == 0, stop=f == NF - 1)
    t = s.done("pe", mm)
    s.wait("dve", t)
    t = dve(nc.vector.tensor_tensor(
        blk, bank[5].rearrange("p (g n) -> p g n", g=2),
        k.row("b2").unsqueeze(1).broadcast_to([P, 2, D]), ALU.add))
    s.wait("pe", t, stt, hd, xgd)
    s.wait("dve", ps)
    for t8 in range(NT):
        b, j = t8 // 2, t8 % 2
        bb = t8
        if t8 >= 6:
            s.wait("pe", stt)
        mm = nc.tensor.matmul(bank[bb][:, 0:D], selT[:, t8, :], blk[:, t8 // 4, :], start=True, stop=True)
        t = s.done("pe", mm)
        s.wait("dve", t)
        a = s.done("dve", nc.vector.scalar_tensor_tensor(
            k.X[:, t8, :], bank[bb][:, 0:D], RT[:, j, 32 + b:33 + b], k.X[:, t8, :], ALU.mult, ALU.add))
        k.x_ready[t8 // 4] = a
    k.bank_free = [a] * 8
    return [a, t, hd]


def program(nc, io, plan, ctx):
    k = Core(nc, ctx, io, plan)
    k.load_constants()
    readers = []
    for layer in LAYERS:
        if layer == 0:
            readers = mamba(k, readers)
        elif layer == 1:
            readers = dense_ffn(k, readers)
        elif layer == 2:
            readers = attention1(k, readers)
        elif layer == 4:
            readers = attention2(k, readers)
        elif layer == 6:
            readers = quantised_layer(k, readers)
        elif layer == 7:
            readers = chosen_ffn(k, readers)
        elif layer == 3:
            readers = moe(k, readers, "m1", io["router1"], io["moe1"], E1, E1K, 5, 1)
        elif layer == 5:
            readers = moe(k, readers, "m2", io["router2"], io["moe2"], E2, E2K, 6, 0)
    k.finish()
    return k.s.found


def layout(inputs):
    import numpy as np

    a = {n: np.asarray(v) for n, v in inputs.items()}

    def tiles(v):
        return v.reshape(-1, P, *v.shape[1:]).swapaxes(0, 1)

    def chunks(v, n):
        z = np.zeros((n * P,), v.dtype)
        z[:v.size] = v
        return z.reshape(n, P).T

    def joined(wk, wv):
        w = np.concatenate([wk, wv], axis=-1).reshape(-1, 16, 2, 16)
        return w[:, :, 0].reshape(-1, D), w[:, :, 1].reshape(-1, D)

    wk2, wv2 = joined(a["L2_xattn_Wk"], a["L2_xattn_Wv"])
    bk2, bv2 = (v.reshape(-1) for v in joined(a["L2_xattn_bk"], a["L2_xattn_bv"]))
    out = {}
    out["x"] = tiles(a["x"].reshape(T, D))
    out["cT"] = a["ctx_1024"].reshape(T, C).T
    out["ident"] = np.eye(P, dtype=np.float32)
    g = np.concatenate([a["g_xattn"], a["g_ffn"]])
    rows = {"g": g, "down_s": a["L0_ffn_down_s"], "bias1": a["L1_ffn_expert_bias"],
            "bq": a["L2_xattn_bq"], "bv": bv2, "bvd": a["L2_xattn_bkv_dca"][D:],
            "bo": a["L2_xattn_bo"], "b2": a["L3_ffn_b2"], "b_r": a["L3_ffn_b_r"],
            "iota": np.arange(P, dtype=np.float32)}
    out["rows"] = np.concatenate([rows[n].reshape(-1) for n in ROWS])
    cw = a["L0_xattn_conv_w"].reshape(2, P, 4).transpose(1, 0, 2).reshape(P, 8)
    al = a["L0_xattn_A_log"].reshape(2, P, 16).transpose(1, 0, 2).reshape(P, 32)
    out["cols"] = np.concatenate(
        [chunks(a["L0_ffn_gate_s"], 6), chunks(a["L0_ffn_up_s"], 6), cw,
         chunks(a["L0_xattn_conv_b"], 2), chunks(a["L0_xattn_dt_proj_b"], 2), al,
         chunks(a["L0_xattn_D"], 2), chunks(a["L1_xattn_gq"], 1), chunks(a["L1_xattn_gk"], 1),
         chunks(a["L3_ffn_b1"], 8), (KEEP3 * np.arange(P) % P).astype(np.float32)[:, None]], axis=1)
    nf = len(FB)
    gu = np.zeros((2, nf * P, D), np.float32)
    gu[0, :F0], gu[1, :F0] = a["L0_ffn_gate_w"], a["L0_ffn_up_w"]
    out["gu0"] = gu.reshape(2, nf, P, DC, P).transpose(4, 1, 0, 3, 2)
    dn = np.zeros((nf * P, D), np.float32)
    dn[:F0] = a["L0_ffn_down_w"].T
    out["down0"] = tiles(dn)
    def expert(wg, wu, wd):
        n = wg.shape[0]
        gu = [w.reshape(n, DC, P, P).transpose(0, 2, 1, 3).reshape(n, P, 256) for w in (wg, wu)]
        return np.stack([gu[0], gu[1], wd], axis=2)
    m1 = [np.concatenate([a["L1_ffn_w_" + n], a["L1_ffn_sw_" + n][None],
                          a["L1_ffn_sw_" + n][None]]) for n in ("gate", "up", "down")]
    out["moe1"] = expert(*[m.transpose(0, 2, 1) for m in m1])
    out["moe2"] = expert(a["L2_ffn_w1"], a["L2_ffn_w2"], a["L2_ffn_w3"])
    w = a["fside_BxS2xS2_0"]
    out["fside"] = tiles(w.reshape(B * D, D))
    out["fsideT"] = tiles(w.transpose(2, 0, 1).reshape(D, B * D))
    out["ctok"] = tiles(a["ctx_1024"].reshape(T, C))
    rw = np.zeros((DC, P, B, B), np.float32)
    rw[:, :, np.arange(B), np.arange(B)] = a["L3_ffn_W_r"].reshape(DC, P, 1)
    out["router3"] = rw.transpose(1, 0, 2, 3)
    out["w31"] = a["L3_ffn_W1"].reshape(DC, P, 8, P).transpose(1, 0, 2, 3)
    out["w32"] = tiles(a["L3_ffn_W2"])
    out["in_proj"] = a["L0_xattn_in_proj_w"].T
    xw = a["L0_xattn_x_proj_w"]
    out["x_proj"] = tiles(np.concatenate([xw[8:], xw[8:], xw[8:], xw[:8]]).T)
    out["dt_proj"] = a["L0_xattn_dt_proj_w"].T
    wd = a["L2_xattn_Wkv_dca"]
    out["w2"] = np.stack([a["L2_xattn_Wq"][:P], a["L2_xattn_Wq"][P:], wk2, wd[:, :D], wv2, wd[:, D:]], axis=1)
    out["bias2"] = np.stack([bk2, a["L2_xattn_bkv_dca"][:D]])[:, None].repeat(2, axis=1)
    ind = np.zeros((2, 2, P), np.float32)
    ind[0, 0], ind[0, 1, :P - SET2], ind[1, 1, P - SET2:] = 1, 1, 1
    out["ind2"] = ind
    out["wo2"] = tiles(a["L2_xattn_Wo"])
    aff = np.zeros((2, 4, 16, 10), np.float32)
    for j, n in enumerate(["qn_w", "qn_b", "kn_w", "kn_b", "kn_dca_w", "kn_dca_b"]):
        aff[..., j] = a["L2_xattn_" + n]
    for j in range(4):
        aff[:, j, :, 6 + j] = 1
    out["aff2"] = aff.reshape(P, 10)
    def heads(w):
        n = w.shape[0] // P
        return w.reshape(n, P, 16, P).transpose(2, 1, 0, 3).reshape(16, P, n * P)
    out["qkv1"] = np.concatenate([heads(a["L1_xattn_W" + n]) for n in "qkv"], axis=2)
    out["wo1"] = a["L1_xattn_Wo"].reshape(16, P, D)
    out["router1"] = tiles(a["L1_ffn_gate_w"].T)
    out["router2"] = tiles(a["L2_ffn_router_w"].T)
    return {n: np.ascontiguousarray(v) for n, v in out.items()}


def kernel(**inputs):
    import numpy as np
    import concourse.bacc as bacc
    from concourse.bass_utils import run_bass_kernel_spmd as run

    arrays = layout(inputs)

    def build(plan):
        nc = bacc.Bacc("TRN2", target_bir_lowering=False, num_devices=1)
        io = {n: nc.dram_tensor("in_" + n, v.shape, mybir.dt.from_np(v.dtype),
                                kind="ExternalInput").ap() for n, v in arrays.items()}
        io["out"] = nc.dram_tensor("out", (P, NT, D), F32, kind="ExternalOutput").ap()
        with ExitStack() as ctx:
            found = program(nc, io, plan, ctx)
        return nc, found

    _, plan = build({})
    nc, _ = build(plan)
    r = run(nc, [{"in_" + n: v for n, v in arrays.items()}], core_ids=[0])
    got = np.asarray(r.results[0]["out"])
    return np.ascontiguousarray(got.transpose(1, 0, 2).reshape(B, S, D))
```

```python
from contextlib import ExitStack

import concourse.bass as bass
from concourse import mybir
from concourse.alu_op_type import AluOpType as ALU

F32 = mybir.dt.float32
BF16 = mybir.dt.bfloat16
ACT = mybir.ActivationFunctionType
AX = mybir.AxisListType.X

P = 128
B, S, D = 4, 256, 256
T = B * S
NT = T // P
DC = D // P
C = 128
HALF = T // 2
F0 = 704
FB = [(f, min(P, F0 - f)) for f in range(0, F0, P)]
E1, E1K = 16, 4
E2, E2K = 8, 2
SET2 = 16
KEEP3 = 64
BIG = 3.0e38
ARENA = 34304


class Token:

    def __init__(self, sem, k, loop=None):
        self.sem, self.k, self.loop = sem, k, loop


class Loop:
    def __init__(self, number, n, base):
        self.number, self.n, self.base, self.i, self.now = number, n, base, None, {}


class Signals:

    START = 2048

    def __init__(self, nc, ctx, plan):
        self.nc, self.ctx, self.plan, self.found = nc, ctx, plan, {}
        self.sems, self.count, self.waited, self.last = {}, {}, {}, {}
        self.loop, self.loops = None, 0
        self.engines = {"pe": nc.tensor, "act": nc.scalar, "dve": nc.vector,
                        "pool": nc.gpsimd, "sp": nc.sync}
        for e in ("pe", "act", "dve", "pool"):
            self.sem(e)
            self.engines[e].sem_inc(self.sems[e], self.START)
            self.count[e] = self.START

    def sem(self, name):
        if name not in self.sems:
            self.sems[name] = self.ctx.enter_context(self.nc.semaphore("s_" + name))
            self.count[name] = 0
        return self.sems[name]

    def done(self, name, ins, label=None, by=1):
        ins.then_inc(self.sem(name), by)
        if self.loop is None:
            self.count[name] += by
            t = Token(name, self.count[name])
        else:
            now = self.loop.now
            now[name] = now.get(name, 0) + by
            t = Token(name, now[name], self.loop)
            if label:
                self.found["k", self.loop.number, label] = (name, now[name])
        if label:
            self.last[label] = t
        return t

    def relabel(self, label, other):
        t = self.last[label] = self.last[other]
        if self.loop is not None:
            self.found["k", self.loop.number, label] = (t.sem, t.k)
        return t

    def loaded(self, name, ins, label=None):
        return self.done("d_" + name, ins, label, 16)

    def before(self, label):
        found = self.plan.get(("k", self.loop.number, label))
        if found is None:
            assert not self.plan, label
            return None
        name, k = found
        return Token(name, k - self.gain(self.loop, name), self.loop)

    def latest(self, *labels):
        got = []
        for label in labels:
            t = self.last.get(label)
            if self.loop is not None and (t is None or t.loop is not self.loop) and (
                    not self.plan or ("k", self.loop.number, label) in self.plan):
                t = self.before(label)
            got.append(t)
        return got

    def settle(self, prefix, engines=("pe", "act", "dve", "pool", "sp")):
        for e in engines:
            self.wait(e, *[t for label, t in self.last.items() if label.startswith(prefix)])

    def gain(self, loop, name):
        return self.plan.get(("m", loop.number, name), 1)

    def wait(self, eng, *tokens):
        for t in tokens:
            if t is None:
                continue
            seen = self.waited.setdefault((eng, t.sem), {"const": 0, "loop": None})
            if t.loop is None:
                if t.k > seen["const"]:
                    self.engines[eng].wait_ge(self.sem(t.sem), t.k)
                    seen["const"] = t.k
                continue
            m, base = self.gain(t.loop, t.sem), t.loop.base.get(t.sem, 0)
            k = t.k
            if t.loop is self.loop:
                if seen["loop"] is None or k > seen["loop"]:
                    value = self.loop.i * m + (base + k)
                    self.engines[eng].wait_ge(self.sem(t.sem), value)
                    seen["loop"] = k
            else:
                v = base + (t.loop.n - 1) * m + k
                if v > seen["const"]:
                    self.engines[eng].wait_ge(self.sem(t.sem), v)
                    seen["const"] = v

    def repeat(self, n):
        return _Repeat(self, n)


class _Repeat:
    def __init__(self, sig, n):
        self.sig, self.n = sig, n

    def __enter__(self):
        s = self.sig
        s.loop = Loop(s.loops, self.n, dict(s.count))
        s.loops += 1
        for w in s.waited.values():
            w["loop"] = None
        self.fori = s.nc.Fori(0, self.n)
        s.loop.i = self.fori.__enter__()
        return s.loop.i

    def __exit__(self, *exc):
        s, loop = self.sig, self.sig.loop
        self.fori.__exit__(*exc)
        for name, m in loop.now.items():
            s.found["m", loop.number, name] = m
            s.count[name] = s.count.get(name, 0) + m * loop.n
        s.loop = None
        return False


def row_layout():
    at, rows = 0, {}
    for name, n in [("g", 8), ("down_s", D), ("bias1", E1), ("bq", D), ("bv", D),
                    ("bvd", D), ("bo", D), ("b2", D), ("b_r", 1), ("iota", P)]:
        rows[name] = (at, n)
        at += n
    return rows, at


ROWS, NROWS = row_layout()
COLS = {"gate_s": (0, 6), "up_s": (6, 6), "conv_w": (12, 8), "conv_b": (20, 2), "dt_b": (22, 2),
        "A_log": (24, 32), "Dp": (56, 2), "gq": (58, 1), "gk": (59, 1), "b1": (60, 8),
        "slot0": (68, 1)}
NCOLS = 69


class Core:

    def __init__(self, nc, ctx, io, plan):
        self.nc, self.io = nc, io
        self.s = Signals(nc, ctx, plan)

        def sb(name, shape, dt=F32):
            return ctx.enter_context(nc.sbuf_tensor(name, shape, dt))

        self.psum = ctx.enter_context(nc.psum_tensor("psum", [P, 8 * 512], F32))
        self.bank = [self.psum[:, b * 512:(b + 1) * 512] for b in range(8)]
        self.X = sb("X", [P, NT, D])
        self.xn = sb("xn", [P, NT, D])
        self.xT = sb("xT", [P, DC, T])
        self.cT = sb("cT", [P, T])
        self.sets = sb("sets", [P, 2, B, P])
        self.ident = sb("ident", [P, P])
        self.rows = sb("rows", [P, NROWS])
        self.cols = sb("cols", [P, NCOLS])
        self.tg = sb("tg", [P, 8])
        self.stats = sb("stats", [P, NT, 6])
        self.mv = sb("mv", [P, NT, 2])
        self.rstd = sb("rstd", [P, NT])
        self.idle = sb("idle", [P, 1])
        self.mhalf = sb("mhalf", [P, 128])
        self.phalf = sb("phalf", [P, 128])
        self.arena = sb("arena", [P, ARENA])
        self.at = 0
        self.bank_free = [None] * 8
        self.measured, self.deviated = {}, {}

    def place(self, *shape, dt=F32):
        n = 1
        for d in shape:
            n *= d
        words = n if dt == F32 else (n + 1) // 2
        words += -words % 16
        v = self.arena[:, self.at:self.at + words]
        self.at += words
        assert self.at <= ARENA, self.at
        if dt != F32:
            v = v.bitcast(dt)
        v = v[:, 0:n]
        if len(shape) == 2:
            v = v.rearrange("p (a b) -> p a b", a=shape[0])
        elif len(shape) == 3:
            v = v.rearrange("p (a b c) -> p a b c", a=shape[0], b=shape[1])
        elif len(shape) == 4:
            v = v.rearrange("p (a b c d) -> p a b c d", a=shape[0], b=shape[1], c=shape[2])
        return v

    def row(self, name):
        at, n = ROWS[name]
        return self.rows[:, at:at + n]

    def col(self, name, j=0):
        return self.cols[:, COLS[name][0] + j:COLS[name][0] + j + 1]

    def load_constants(self):
        nc, s, io = self.nc, self.s, self.io
        self.x_in = [s.loaded(f"x{h}", nc.sync.dma_start(
            self.X[:, 4 * h:4 * h + 4, :], io["x"][:, 4 * h:4 * h + 4, :])) for h in range(2)]
        self.ctx_in = s.loaded("cT", nc.scalar.dma_start(self.cT[:, :], io["cT"]))
        self.cols_in = s.loaded("cols", nc.scalar.dma_start(self.cols[:, :], io["cols"]))
        self.ident_in = s.loaded("ident", nc.scalar.dma_start(self.ident[:, :], io["ident"]))
        self.rows_in = s.loaded("rows", nc.scalar.dma_start(
            self.rows[:, :], io["rows"].partition_broadcast(P)))
        nc.gpsimd.memset(self.idle[:, :], 0.5)
        nc.gpsimd.memset(self.mhalf[:, :], -0.5)
        self.halves = s.done("pool", nc.gpsimd.memset(self.phalf[:, :], 0.5))
        s.wait("pool", self.halves)
        self.x_ready = list(self.x_in)

    def constants_ready(self):
        nc, s = self.nc, self.s
        s.wait("act", self.rows_in, self.cols_in)
        self.tg_done = s.done("act", nc.scalar.activation(self.tg[:, :], self.row("g"), ACT.Tanh))
        s.wait("pe", self.ident_in)
        s.wait("pool", self.rows_in, self.cols_in)
        s.wait("dve", self.cols_in, self.halves)

    def function(self, which):
        self.s.wait("act", self.halves, self.s.last.get("idle"))
        self.s.done("act", self.nc.scalar.activation(self.idle[:, :], self.idle[:, :], which), "idle")

    def gates_ready(self):
        self.s.wait("pool", self.tg_done)
        self.s.wait("dve", self.rows_in, self.tg_done)

    def split_context(self):
        nc, s = self.nc, self.s
        cleared = s.done("pool", nc.gpsimd.memset(self.sets[:, :, :, :], 0.0))
        s.wait("pool", cleared, self.ctx_in)
        second = self.cT[:, :].rearrange("p (b j t) -> p b j t", b=B, j=2)[:, :, 1, :]
        main = P - SET2
        nc.gpsimd.tensor_copy(self.sets[:, 0, :, 0:main], second[:, :, 0:main])
        self.sets_in = s.done("pool", nc.gpsimd.tensor_copy(self.sets[:, 1, :, main:], second[:, :, main:]))

    def tile_stats(self, t, *done):
        nc, s = self.nc, self.s
        s.wait("dve", *done)
        self.measured[t] = s.done("dve", nc.vector.bn_stats(self.stats[:, t, :], self.X[:, t, :]))

    def deviation(self, h):
        nc, s = self.nc, self.s
        tiles, half = range(4 * h, 4 * h + 4), slice(4 * h, 4 * h + 4)
        for t in tiles:
            if t not in self.measured:
                self.tile_stats(t, self.x_ready[h])
        s.wait("dve", *[self.measured.pop(t) for t in tiles])
        for t in tiles:
            ag = s.done("dve", nc.vector.bn_aggr(self.mv[:, t, :], self.stats[:, t, :]))
        s.wait("dve", ag)
        ve = s.done("dve", nc.vector.tensor_scalar(self.rstd[:, half], self.mv[:, half, 1],
                                                   1e-5, None, ALU.add))
        s.wait("pool", ve)
        self.deviated[h] = s.done("pool", nc.gpsimd.tensor_tensor(
            self.rstd[:, half], self.rstd[:, half], self.mhalf[:, 0:4], ALU.pow))

    def layernorm(self, readers=(), transpose=True):
        nc, s = self.nc, self.s
        ready = []
        for h in range(2):
            if h not in self.deviated:
                self.deviation(h)
        s.wait("dve", *readers)
        s.wait("act", *readers)
        for h in range(2):
            tiles = range(4 * h, 4 * h + 4)
            s.wait("dve", self.deviated.pop(h))
            for j, t in enumerate(tiles):
                xn = s.done("dve", nc.vector.tensor_scalar(
                    self.xn[:, t, :], self.X[:, t, :], self.mv[:, t, 0:1], self.rstd[:, t:t + 1],
                    ALU.subtract, ALU.mult))
                if not transpose:
                    continue
                s.wait("pe", xn)
                for c in range(DC):
                    b = 2 * h + c
                    if j == 0:
                        s.wait("pe", self.bank_free[b])
                    tr = s.done("pe", nc.tensor.transpose(
                        self.bank[b][:, j * P:(j + 1) * P], self.xn[:, t, c * P:(c + 1) * P],
                        self.ident[:, :]))
            if not transpose:
                ready.append((xn,))
                continue
            cols = slice(h * HALF, (h + 1) * HALF)
            s.wait("act", tr)
            a = s.done("act", nc.scalar.copy(self.xT[:, 0, cols], self.bank[2 * h][:, :]))
            eng, engine = ("dve", nc.vector.tensor_copy) if h else ("act", nc.scalar.copy)
            s.wait(eng, tr)
            v = s.done(eng, engine(self.xT[:, 1, cols], self.bank[2 * h + 1][:, :]))
            self.bank_free[2 * h], self.bank_free[2 * h + 1] = a, v
            ready.append((a, v))
        return ready

    def finish(self):
        nc, s = self.nc, self.s
        for h in range(2):
            s.wait("sp", self.x_ready[h])
            t = s.loaded("out", nc.sync.dma_start(self.io["out"][:, 4 * h:4 * h + 4, :],
                                                  self.X[:, 4 * h:4 * h + 4, :]))
        s.wait("sp", t)


def mamba(k):
    nc, s = k.nc, k.s
    NI, NSTATE, RANK, TAPS = 2, 16, 8, 4
    NBC = 2 * NSTATE
    k.at = 0
    Win = k.place(NI * P)
    Wx = k.place(NI, 3 * NBC + RANK)
    Wdt = k.place(NI * P)
    xp = k.place(NI, B, TAPS - 1 + S)
    U, DT, DU, Y = k.place(NI, T), k.place(NI, T), k.place(NI, T), k.place(NI, T)
    V, E = k.place(NI, T), k.place(NI, T)
    A = k.place(NI, NSTATE)
    low = k.place(T)
    bc3 = k.place(T, dt=BF16)
    part = k.place(T, dt=BF16)
    sel = k.place(NBC, P, dt=BF16)
    row = k.place(NBC)
    skip = k.place(NI, P)
    gate = k.place(NT, S)
    dA, dBu = k.place(2, B, S), k.place(2, T)
    Hs, HC = k.place(2, T), k.place(4, T)
    Cs = k.place(2, T)
    bcf = Cs[:, 0, :]
    bank = k.bank
    wi = s.loaded("mwi", nc.sync.dma_start(Win, k.io["in_proj"]))
    wx = s.loaded("mwx", nc.sync.dma_start(Wx, k.io["x_proj"]))
    wd = s.loaded("mwd", nc.sync.dma_start(Wdt[96:96 + RANK], k.io["dt_proj"]))
    nc.gpsimd.memset(dA[:, :, :, 0:1], 0.0)
    pads = s.done("pool", nc.gpsimd.memset(xp[:, :, :, 0:TAPS - 1], 0.0))
    s.wait("pe", k.ctx_in, wi)
    s.wait("act", pads)
    for c in range(NI):
        for h in range(2):
            mm = nc.tensor.matmul(bank[2 * c + h], Win[:, c * P:(c + 1) * P],
                                  k.cT[:, h * HALF:(h + 1) * HALF], start=True, stop=True)
            pd = s.done("pe", mm)
            s.wait("act", pd)
            xi = s.done("act", nc.scalar.copy(xp[:, c, 2 * h:2 * h + 2, TAPS - 1:],
                                              bank[2 * c + h].rearrange("p (b t) -> p b t", b=2)), f"mx{c}")
    z = k.layernorm(transpose=False)
    k.constants_ready()
    s.wait("act", *z[0], *z[1])
    gd = s.done("act", nc.scalar.activation(gate, k.xn[:, :, :], ACT.Silu))
    s.wait("pool", k.ident_in)
    ws = s.done("pool", nc.gpsimd.tensor_tensor(row, k.ident[:, 0:NBC], k.ident[:, NBC:2 * NBC], ALU.add))
    s.wait("pool", ws)
    ws = s.done("pool", nc.gpsimd.tensor_tensor(row, row, k.ident[:, 2 * NBC:3 * NBC], ALU.add))
    for c in range(NI):
        sk = s.done("pool", nc.gpsimd.tensor_scalar(skip[:, c, :], k.ident[:, :], k.col("Dp", c), None,
                                                    ALU.mult))
    s.wait("pool", ws)
    ws = s.done("pool", nc.gpsimd.tensor_copy(sel, row.unsqueeze(2).broadcast_to([P, NBC, P])))
    s.wait("dve", pads)
    n96 = 3 * NBC
    both = k.psum[:, 0:2 * 512]

    def skipped(c, wait):
        s.wait("pe", sk, wait)
        for h in range(2):
            mm = nc.tensor.matmul(bank[4 + 2 * c + h], skip[:, c, :], U[:, c, h * HALF:(h + 1) * HALF],
                                  start=True, stop=False)
        s.done("pe", mm)

    s.wait("pe", xi, wx)
    for c in range(NI):
        s.wait("dve", s.last[f"mx{c}"])
        yv = Y[:, c, :].rearrange("p (b t) -> p b t", b=B)
        for w in range(TAPS):
            tap, src = k.col("conv_w", c * TAPS + w), xp[:, c, :, w:w + S]
            if w == 0:
                r = s.done("dve", nc.vector.tensor_scalar(yv, src, tap, None, ALU.mult))
            else:
                s.wait("dve", r)
                r = s.done("dve", nc.vector.scalar_tensor_tensor(yv, src, tap, yv, ALU.mult, ALU.add))
        s.wait("act", r)
        ui = s.done("act", nc.scalar.activation(U[:, c, :], Y[:, c, :], ACT.Silu, bias=k.col("conv_b", c)))
        if c == 0:
            skipped(0, ui)
        s.wait("pe", ui)
        for h in range(2):
            xd = s.done("pe", nc.tensor.matmul(bank[h][0:n96 + RANK, :], Wx[:, c, :],
                                               U[:, c, h * HALF:(h + 1) * HALF], start=c == 0,
                                               stop=c == NI - 1))
    s.wait("act", xd)
    lo = s.done("act", nc.scalar.copy(low[96:96 + RANK], both[96:96 + RANK, :]))
    al = COLS["A_log"][0]
    s.wait("dve", xd, lo)
    r = s.done("dve", nc.vector.tensor_copy(bc3[0:n96], both[0:n96, :]))
    s.wait("dve", r)
    r = s.done("dve", nc.vector.tensor_tensor(bcf[0:n96], both[0:n96, :], bc3[0:n96], ALU.subtract))
    s.wait("dve", r)
    r = s.done("dve", nc.vector.tensor_copy(part[0:n96], bcf[0:n96]))
    s.wait("dve", r)
    nc.vector.tensor_copy(bc3[NBC:2 * NBC], part[NBC:2 * NBC])
    r = s.done("dve", nc.vector.tensor_tensor(bcf[0:n96], bcf[0:n96], part[0:n96], ALU.subtract))
    s.wait("dve", r)
    split = s.done("dve", nc.vector.tensor_copy(bc3[2 * NBC:n96], bcf[2 * NBC:n96]))
    s.wait("pe", lo, wd)
    vd = []
    for c in range(NI):
        for h in range(2):
            mm = nc.tensor.matmul(bank[2 + 4 * c + h], Wdt[96:96 + RANK, c * P:(c + 1) * P],
                                  low[96:96 + RANK, h * HALF:(h + 1) * HALF], start=True, stop=True)
        vd.append(s.done("pe", mm))
    ab, ex, ln = [], [], []
    for c in range(NI):
        s.wait("act", vd[c])
        pv = k.psum[:, (2 + 4 * c) * 512:(4 + 4 * c) * 512]
        ab.append(s.done("act", nc.scalar.activation(E[:, c, :], pv, ACT.Abs, bias=k.col("dt_b", c))))
        free = s.done("act", nc.scalar.activation(V[:, c, :], pv, ACT.Relu, bias=k.col("dt_b", c)), f"mV{c}")
    for c in range(NI):
        s.wait("act", ab[c])
        ex.append(s.done("act", nc.scalar.activation(E[:, c, :], E[:, c, :], ACT.Exp, scale=-1.0)))
    ae = s.done("act", nc.scalar.activation(A, k.cols[:, al:al + 32].rearrange("p (c n) -> p c n", c=2),
                                            ACT.Exp))
    for c in range(NI):
        s.wait("dve", ex[c])
        w1 = s.done("dve", nc.vector.tensor_scalar(DT[:, c, :], E[:, c, :], 1.0, None, ALU.add))
        s.wait("act", w1)
        ln.append(s.done("act", nc.scalar.activation(DU[:, c, :], DT[:, c, :], ACT.Ln)))
    k.function(ACT.Exp)
    s.wait("dve", ae)
    an = s.done("dve", nc.vector.tensor_scalar(A, A, -1.0, None, ALU.mult))
    s.wait("dve", w1)
    for c in (1, 0):
        r = s.done("dve", nc.vector.scalar_tensor_tensor(E[:, c, :], DT[:, c, :], -1.0, E[:, c, :],
                                                         ALU.add, ALU.subtract))
        eng, engine = (("dve", nc.vector), ("pool", nc.gpsimd))[c]
        s.wait(eng, r, free)
        r = s.done(eng, engine.tensor_tensor(E[:, c, :], V[:, c, :], E[:, c, :], ALU.subtract))
        s.wait(eng, ln[c], r)
        s.done(eng, engine.tensor_tensor(DT[:, c, :], DU[:, c, :], E[:, c, :], ALU.add), f"mDT{c}")
    for c in range(NI):
        s.wait("dve", s.last[f"mDT{c}"])
        r = s.done("dve", nc.vector.tensor_tensor(DU[:, c, :], DT[:, c, :], U[:, c, :], ALU.mult), f"mDU{c}")
    skipped(1, free)
    s.wait("pe", split, ws, free)
    s.wait("act", an, r)
    s.wait("dve", an, r)

    def rows_of(n):
        for row, b, label in ((n, 0, "mB"), (n + NSTATE, 2, "mC")):
            s.wait("pe", *s.latest(label))
            for h in range(2):
                mm = nc.tensor.matmul(bank[b + h], sel[0:n96, bass.ds(row, 1), :].rearrange("p a n -> p (a n)"),
                                      bc3[0:n96, h * HALF:(h + 1) * HALF], start=True, stop=True)
            s.done("pe", mm, label + "in")

    def state(n, v):
        Bp, Cp = k.psum[:, 0:2 * 512], k.psum[:, 2 * 512:4 * 512]
        s.wait("act", *s.latest("mCin", f"mhc1{v}"))
        s.done("act", nc.scalar.copy(Cs[:, v, :], Cp), "mC")
        for c in range(NI):
            s.wait("act", *s.latest(f"mscan{c}"))
            dtv = DT[:, c, :].rearrange("p (b t) -> p b t", b=B)
            s.done("act", nc.scalar.activation(dA[:, c, :, 1:S], dtv[:, :, 1:S], ACT.Exp,
                                               scale=A[:, c, bass.ds(n, 1)]), f"mdA{c}")
        for c in range(NI):
            s.wait("dve", *s.latest("mBin", f"mscan{c}"))
            s.done("dve", nc.vector.tensor_tensor(dBu[:, c, :], DU[:, c, :], Bp, ALU.mult), f"mdB{c}")
        s.relabel("mB", "mdB1")
        for c in range(NI):
            s.wait("dve", *s.latest(f"mdA{c}", f"mdB{c}", f"mhc{c}"))
            s.done("dve", nc.vector.tensor_tensor_scan(
                Hs[:, c, :], dA[:, c].rearrange("p b t -> p (b t)"), dBu[:, c, :], 0.0, ALU.mult, ALU.add),
                f"mscan{c}")
            s.wait("pool", *s.latest(f"mscan{c}", "mC", f"my{c}{v}"))
            s.done("pool", nc.gpsimd.tensor_tensor(HC[:, 2 * v + c, :], Hs[:, c, :], Cs[:, v, :],
                                                         ALU.mult), f"mhc{c}")
            s.relabel(f"mhc{c}{v}", f"mhc{c}")

    def add(c, v, last=False):
        s.wait("pe", *s.latest(f"mhc{c}{v}"))
        for h in range(2):
            mm = nc.tensor.matmul(bank[4 + 2 * c + h], k.ident[:, :], HC[:, 2 * v + c, h * HALF:(h + 1) * HALF],
                                  start=False, stop=last)
        s.done("pe", mm, f"my{c}{v}")

    rows_of(0)
    state(0, 0)
    rows_of(1)
    add(0, 0)
    s.settle("m", ("pe", "pool"))
    for prefix in ("mB", "mC", "md", "ms", "mh"):
        s.settle(prefix, ("dve", "act"))
    with s.repeat(NSTATE // 2 - 1) as i:
        state(i * 2 + 1, 1)
        rows_of(i * 2 + 2)
        add(1, 0)
        add(0, 1)
        state(i * 2 + 2, 0)
        rows_of(i * 2 + 3)
        add(1, 1)
        add(0, 0)
    state(NSTATE - 1, 1)
    add(1, 0)
    add(0, 1, True)
    add(1, 1, True)
    k.gates_ready()
    tr = {}
    for c in range(NI):
        s.wait("dve", s.last[f"my{c}1"], gd)
        g = s.done("dve", nc.vector.tensor_tensor(
            Y[:, c, :].rearrange("p (b t) -> p b t", b=B),
            k.psum[:, (4 + 2 * c) * 512:(6 + 2 * c) * 512].rearrange("p (b t) -> p b t", b=B),
            gate.rearrange("p (b c) t -> p b c t", c=NI)[:, :, c, :], ALU.mult))
        tr[c] = g
    s.wait("pe", *s.latest("mC", "mB"), tr[0], tr[1])
    for b in range(B):
        for j in range(2):
            for c in range(NI):
                mm = nc.tensor.transpose(bank[b][:, j * D + c * P:j * D + (c + 1) * P],
                                         Y[:, c, b * S + j * P:b * S + (j + 1) * P], k.ident[:, :])
        td = s.done("pe", mm)
        s.wait("dve", td)
        X2 = k.X[:, 2 * b:2 * b + 2, :]
        a = s.done("dve", nc.vector.scalar_tensor_tensor(
            X2, bank[b].rearrange("p (t d) -> p t d", t=2), k.tg[:, 0:1], X2, ALU.mult, ALU.add))
        k.bank_free[b] = a
        k.tile_stats(2 * b, a)
        k.tile_stats(2 * b + 1)
        if b % 2:
            k.x_ready[b // 2] = a
            k.deviation(b // 2)
    k.bank_free[4:] = [a] * 4
    k.split_context()
    return [td, a, *s.latest("mC", "mhc0", "mhc1"), gd]


def dense_ffn(k, readers):
    nc, s = k.nc, k.s
    k.at = 0
    nf = len(FB)
    gu = k.place(nf, 2, DC, P)
    down = k.place(nf, D)
    H = k.place(nf, T)
    G = k.place(2, HALF)
    Y = k.place(2, D)
    scale = k.place(D)
    s.wait("sp", *readers)
    w_in = [s.loaded("w0a", nc.sync.dma_start(gu[:, 0:1], k.io["gu0"][:, 0:1])),
            s.loaded("w0b", nc.sync.dma_start(gu[:, 1:nf], k.io["gu0"][:, 1:nf])),
            s.loaded("w0c", nc.sync.dma_start(down[:, :, :], k.io["down0"]))]
    k.function(ACT.Silu)
    ready = k.layernorm(readers)
    sc = s.done("dve", nc.vector.tensor_scalar(scale, k.row("down_s"), k.tg[:, 4:5], None, ALU.mult))
    free = k.bank_free
    n, muls, mul_done = 0, [], {}
    for h in range(2):
        cols = slice(h * HALF, (h + 1) * HALF)
        s.wait("pe", *ready[h], w_in[0])
        for f, (_, m) in enumerate(FB):
            if f == 1:
                s.wait("pe", w_in[1])
            g, u = 4 + n % 2 * 2, 5 + n % 2 * 2
            for b, which in ((g, 0), (u, 1)):
                s.wait("pe", free[b])
                for c in range(DC):
                    mm = nc.tensor.matmul(k.bank[b][0:m, :], gu[:, f, which, c, 0:m],
                                          k.xT[:, c, cols], start=c == 0, stop=c == DC - 1)
                if which == 0:
                    g_done = s.done("pe", mm)
            u_done = s.done("pe", mm)
            s.wait("act", g_done, muls[n - 2] if n >= 2 else None)
            si = s.done("act", nc.scalar.activation(G[0:m, n % 2, :], k.bank[g][0:m, :], ACT.Silu,
                                                    scale=k.col("gate_s", f)[0:m, :]))
            s.wait("dve", u_done, si)
            mu = s.done("dve", nc.vector.scalar_tensor_tensor(
                H[0:m, f, cols], k.bank[u][0:m, :], k.col("up_s", f)[0:m, :], G[0:m, n % 2, :],
                ALU.mult, ALU.mult))
            free[g], free[u] = si, mu
            muls.append(mu)
            n += 1
        mul_done[h] = muls[-1]
    s.wait("pe", w_in[2])
    added = []
    for t in range(NT):
        b = t % 4
        s.wait("pe", mul_done[t // 4], free[b])
        for f, (_, m) in enumerate(FB):
            mm = nc.tensor.matmul(k.bank[b][:, 0:D], H[0:m, f, t * P:(t + 1) * P], down[0:m, f, :],
                                  start=f == 0, stop=f == nf - 1)
        y_done = s.done("pe", mm)
        s.wait("dve", y_done, sc, added[t - 2] if t >= 2 else None)
        ys = s.done("dve", nc.vector.tensor_tensor(Y[:, t % 2, :], k.bank[b][:, 0:D], scale, ALU.mult))
        free[b] = ys
        s.wait("pool", ys)
        added.append(s.done("pool", nc.gpsimd.tensor_tensor(k.X[:, t, :], k.X[:, t, :],
                                                            Y[:, t % 2, :], ALU.add)))
        if t >= 2:
            k.tile_stats(t - 2, added[t - 2])
        if t == 5:
            k.deviation(0)
    k.x_ready = [added[3], added[7]]
    return [y_done, added[-1]]


def top_mask(k, ext, first, top, rep, mask, experts, keep):
    nc, s = k.nc, k.s
    s.wait("dve", first)
    for t in range(NT):
        mx = s.done("dve", nc.vector.max(top[:, t, :], ext[:, t, 0:experts]))
    s.wait("dve", mx)
    pads = s.done("dve", nc.vector.memset(top[:, :, keep:8], -BIG))
    s.wait("dve", pads)
    for t in range(NT):
        mr = s.done("dve", nc.vector.match_replace(rep[:, t, :], top[:, t, :], ext[:, t, :], BIG))
    s.wait("dve", mr)
    return s.done("dve", nc.vector.tensor_tensor(mask, rep[:, :, 0:experts], ext[:, :, 0:experts],
                                                 ALU.not_equal))


def moe(k, readers, tag, router, weights, experts, keep, gate, shared, ahead):
    nc, s = k.nc, k.s
    k.at = 0
    total = experts + shared
    W = k.place(2, 3, 256)
    wr = k.place(DC, experts)
    H = k.place(4, HALF)
    G = k.place(4, HALF)
    score = k.place(NT, experts)
    ext = k.place(NT, experts + 8 - keep)
    rep = k.place(NT, experts + 8 - keep)
    top = k.place(NT, 8)
    mask = k.place(NT, experts)
    cw = k.place(NT, experts)
    tot = k.place(NT)
    s.wait("sp", *readers)
    wr_in = s.loaded(tag + "wr", nc.sync.dma_start(wr[:, :, :], router))

    def load(slot, e):
        src = weights[bass.ds(e, 1)].rearrange("a p m n -> p (a m) n")
        return s.loaded(f"{tag}w{slot}", nc.sync.dma_start(W[:, slot, :, :], src), f"{tag}w{slot}")

    load(0, 0)
    load(1, 1)
    ahead.start(readers)
    k.function(ACT.Tanh if tag == "m1" else ACT.Exp)
    ready = k.layernorm(readers)
    s.wait("dve", *readers)
    s.wait("pool", *readers)
    padded = s.done("pool", nc.gpsimd.memset(ext[:, :, experts:experts + 8 - keep], -BIG))
    g = k.tg[:, gate:gate + 1]
    for h in range(2):
        s.wait("pe", *ready[h])
    s.wait("pe", wr_in, k.bank_free[7])
    for t in range(NT):
        for c in range(DC):
            mm = nc.tensor.matmul(k.bank[7][:, t * experts:(t + 1) * experts],
                                  k.xT[:, c, t * P:(t + 1) * P], wr[:, c, :],
                                  start=c == 0, stop=c == DC - 1)
    lg = s.done("pe", mm)
    lg_ps = k.bank[7][:, 0:NT * experts].rearrange("p (t e) -> p t e", t=NT)
    if tag == "m1":
        s.wait("act", lg)
        th = s.done("act", nc.scalar.activation(score[:, :, :], lg_ps, ACT.Tanh, scale=0.5))
        k.function(ACT.Silu)
        k.bank_free[7] = th
        s.wait("dve", th, padded)
        sg = s.done("dve", nc.vector.tensor_scalar(score, score, 0.5, 0.5, ALU.mult, ALU.add))
        s.wait("dve", sg)
        first = s.done("dve", nc.vector.tensor_tensor(
            ext[:, :, 0:experts], score, k.row("bias1").unsqueeze(1).broadcast_to([P, NT, experts]),
            ALU.add))
    else:
        s.wait("dve", lg, padded)
        first = s.done("dve", nc.vector.tensor_copy(ext[:, :, 0:experts], lg_ps))
        k.bank_free[7] = first
    mk = top_mask(k, ext, first, top, rep, mask, experts, keep)
    if tag == "m2":
        s.wait("dve", mk)
        d = s.done("dve", nc.vector.tensor_tensor(
            score, ext[:, :, 0:experts], top[:, :, 0:1].broadcast_to([P, NT, experts]), ALU.subtract))
        s.wait("act", d)
        ex = s.done("act", nc.scalar.activation(score[:, :, :], score[:, :, :], ACT.Exp))
        k.function(ACT.Silu)
        s.wait("dve", ex)
    s.wait("dve", mk)
    a = s.done("dve", nc.vector.tensor_tensor(cw, mask, score, ALU.mult))
    s.wait("dve", a)
    a = s.done("dve", nc.vector.tensor_reduce(tot, cw, AX, ALU.add))
    s.wait("dve", a)
    a = s.done("dve", nc.vector.reciprocal(tot, tot))
    s.wait("dve", a)
    a = s.done("dve", nc.vector.tensor_scalar(tot, tot, g, None, ALU.mult))
    s.wait("dve", a)
    a = s.done("dve", nc.vector.tensor_tensor(cw, cw, tot.unsqueeze(2).broadcast_to([P, NT, experts]),
                                              ALU.mult))
    s.wait("dve", a)

    def user(label, looped, same):
        if looped and not same:
            return s.before(label)
        return s.last.get(label)

    def gate_up(st, looped):
        r, slot, h = st % 4, st % 4 // 2, st % 2
        g, u, two = 2 * h, 2 * h + 1, (st + 2) % 4
        cols = slice(h * HALF, (h + 1) * HALF)
        s.wait("pe", user(f"{tag}w{slot}", looped, st == 4))
        s.wait("pe", user(f"{tag}silu{two}", looped, st >= 3))
        for c in range(DC):
            mm = nc.tensor.matmul(k.bank[g][:, :], W[:, slot, 0, c * P:(c + 1) * P], k.xT[:, c, cols],
                                  start=c == 0, stop=c == DC - 1)
        gd = s.done("pe", mm)
        s.wait("pe", user(f"{tag}mul{two}", looped, st >= 3))
        for c in range(DC):
            mm = nc.tensor.matmul(k.bank[u][:, :], W[:, slot, 1, c * P:(c + 1) * P], k.xT[:, c, cols],
                                  start=c == 0, stop=c == DC - 1)
        ud = s.done("pe", mm)
        s.wait("act", gd, user(f"{tag}mul{r}", looped, False))
        si = s.done("act", nc.scalar.activation(G[:, r, :], k.bank[g][:, :], ACT.Silu), f"{tag}silu{r}")
        s.wait("dve", ud, si, user(f"{tag}out{r}", looped, st == 4))
        s.done("dve", nc.vector.tensor_tensor(H[:, r, :], k.bank[u][:, :], G[:, r, :], ALU.mult),
               f"{tag}mul{r}")

    def down(st, looped, e, final=False):
        r, slot, h, two = st % 4, st % 4 // 2, st % 2, (st + 2) % 4
        s.wait("pe", user(f"{tag}mul{r}", looped, st >= 1))
        outs = []
        for j in range(4):
            b = 4 + 2 * h + j // 2
            if j % 2 == 0:
                s.wait("pe", user(f"{tag}acc{two}.{j + 1}", looped, st >= 2))
            mm = nc.tensor.matmul(k.bank[b][:, j % 2 * D:(j % 2 + 1) * D], H[:, r, j * P:(j + 1) * P],
                                  W[:, slot, 2, :], start=True, stop=True)
            if j % 2 == 1:
                outs.append(s.done("pe", mm, f"{tag}out{r}" if j == 3 else None))
        for j in range(4):
            t, b = 4 * h + j, 4 + 2 * h + j // 2
            w = g if e is None else cw[:, t, bass.ds(e, 1)]
            s.wait("dve", outs[j // 2], user(f"{tag}acc{two}.{j}", looped, st >= 2))
            s.done("dve", nc.vector.scalar_tensor_tensor(
                k.X[:, t, :], k.bank[b][:, j % 2 * D:(j % 2 + 1) * D], w, k.X[:, t, :],
                ALU.mult, ALU.add), f"{tag}acc{r}.{j}")
            if final and j % 2:
                k.tile_stats(t - 1, s.last[f"{tag}acc{r}.{j}"])
                k.tile_stats(t)
        if final:
            k.deviation(h)
        return outs[1]

    s.wait("pe", *[k.bank_free[b] for b in range(8)])
    s.wait("act", *[k.bank_free[b] for b in range(8)])
    pairs = total // 2 if shared else total // 2 - 1
    gate_up(0, False)
    ahead.finish()
    s.wait("pe", s.last[f"{tag}mul0"])
    with s.repeat(pairs) as i:
        for st in range(4):
            gate_up(st + 1, True)
            od = down(st, True, i * 2 + st // 2)
            if st % 2 == 1:
                s.wait("sp", od)
                load(st // 2, i * 2 + 2 + st // 2)
    e = 2 * pairs
    if shared:
        gate_up(1, False)
        down(0, False, None, True)
        od = down(1, False, None, True)
    else:
        for st in range(4):
            if st < 3:
                gate_up(st + 1, False)
            od = down(st, False, e + st // 2, st >= 2)
    r = 1 if shared else 3
    k.x_ready = [s.last[f"{tag}acc{r - 1}.3"], s.last[f"{tag}acc{r}.3"]]
    k.bank_free = [k.x_ready[1]] * 8
    return ([od, k.x_ready[1], s.last[f"{tag}silu{r}"], s.last[f"{tag}mul{r}"]]
            + [s.last[f"{tag}w{j}"] for j in range(2)])


def attention1(k, readers):
    nc, s = k.nc, k.s
    NH, HD = 16, P
    SCALE = HD ** -0.5
    bank = k.bank
    k.at = 0
    W = k.place(2, 3 * HD + P + D)
    M = k.place(2, D)
    Q, K = k.place(2, T), k.place(2, T)
    R = k.place(2, NT, HD)
    sq = k.place(2, NT, HD)
    ss, rr = k.place(2, 2, 4), k.place(2, 2, 4)
    Pr = k.place(2, 2, S)
    PT = k.place(2, 2, S)
    Z = k.place(2, S)
    ctok = k.place(NT, C)
    mx, nb = k.place(2, 2), k.place(2, 2)
    rs, ri = k.place(B, 2), k.place(B, 2)
    s.wait("sp", *readers)
    s.wait("act", *readers)
    cl = s.loaded("a1c", nc.scalar.dma_start(ctok, k.io["ctok"]))

    def load(slot, h):
        s.wait("sp", *s.latest(f"a1M{slot}", f"a1P{slot}"))
        s.loaded(f"a1w{slot}", nc.sync.dma_start(
            W[:, slot, :], k.io["w1"][bass.ds(h, 1)].rearrange("a p n -> p (a n)")), f"a1w{slot}")

    def project(p, q, half):
        b = 6 + q
        s.wait("pe", *s.latest(f"a1w{p}", f"a1b{b}"))
        for j in range(4):
            t = 4 * half + j
            if q:
                for c in range(DC):
                    mm = nc.tensor.matmul(bank[b][:, j * P:(j + 1) * P], k.xT[:, c, t * P:(t + 1) * P],
                                          W[:, p, c * P:(c + 1) * P], start=c == 0, stop=c == DC - 1)
            else:
                mm = nc.tensor.matmul(bank[b][:, j * P:(j + 1) * P], k.cT[:, t * P:(t + 1) * P],
                                      W[:, p, D:D + P], start=True, stop=True)
        done = s.done("pe", mm, f"a1P{p}")
        s.wait("act", done, *s.latest(f"a1ss{half}", f"a1turn{q}{half}"))
        tiles, v = slice(4 * half, 4 * half + 4), bank[b].rearrange("p (t d) -> p t d", t=4)
        s.done("act", nc.scalar.activation(sq[:, q, tiles, :], v, ACT.Square))
        s.done("act", nc.scalar.copy(R[:, q, tiles, :], v), f"a1b{b}")
        s.relabel(f"a1R{q}{half}", f"a1b{b}")

    def sums(half):
        s.wait("dve", *s.latest(f"a1R0{half}", f"a1R1{half}", f"a1rr{half}"))
        r = s.done("dve", nc.vector.tensor_reduce(ss[:, half], sq[:, :, 4 * half:4 * half + 4, :], AX, ALU.add),
                   f"a1ss{half}")
        s.wait("dve", r)
        r = s.done("dve", nc.vector.tensor_scalar(ss[:, half], ss[:, half], 1.0 / HD, 1e-5, ALU.mult, ALU.add))
        s.wait("pool", r, *s.latest(f"a1N{half}"))
        s.done("pool", nc.gpsimd.tensor_tensor(
            rr[:, half], ss[:, half], k.mhalf[:, 0:8].rearrange("p (q t) -> p q t", q=2), ALU.pow), f"a1rr{half}")

    def normalise(half):
        s.wait("dve", *s.latest(f"a1rr{half}"))
        v = R[:, :, 4 * half:4 * half + 4, :]
        s.done("dve", nc.vector.tensor_tensor(v, v, rr[:, half].unsqueeze(3).broadcast_to([P, 2, 4, HD]),
                                              ALU.mult), f"a1N{half}")

    def turn(p, q, half):
        b = 7 - q
        s.wait("pe", *s.latest(f"a1b{b}", f"a1N{half}"))
        for j in range(4):
            mm = nc.tensor.transpose(bank[b][:, j * P:(j + 1) * P], R[:, q, 4 * half + j, :], k.ident[:, :])
        td = s.done("pe", mm, f"a1turn{q}{half}")
        dst = (Q if q else K)[:, p, half * HALF:(half + 1) * HALF]
        s.wait("act", td, *s.latest(f"a1S{p}"))
        s.done("act", nc.scalar.activation(dst, bank[b], ACT.Identity, scale=k.col("gq" if q else "gk")),
               f"a1b{b}")
        s.relabel(f"a1in{p}{q}{half}", f"a1b{b}")

    def joined(p):
        s.wait("pe", *s.latest(f"a1w{p}", "a1b6"))
        mm = s.done("pe", nc.tensor.matmul(bank[6][:, 0:D], W[:, p, 3 * P:4 * P], W[:, p, 4 * P:],
                                           start=True, stop=True), f"a1M{p}")
        s.wait("act", mm, *s.latest(f"a1Y{p}"))
        s.done("act", nc.scalar.activation(M[:, p, :], bank[6][:, 0:D], ACT.Identity, scale=k.tg[:, 1:2]),
               "a1b6")
        s.relabel(f"a1Min{p}", "a1b6")

    def scores(p, b):
        u = b % 2
        s.wait("pe", *s.latest(f"a1in{p}0{b // 2}", f"a1in{p}1{b // 2}", f"a1E{u}"))
        for j in range(2):
            mm = nc.tensor.matmul(bank[u][:, j * S:(j + 1) * S], Q[:, p, b * S + j * P:b * S + (j + 1) * P],
                                  K[:, p, b * S:(b + 1) * S], start=True, stop=True)
        sd = s.done("pe", mm, f"a1S{p}")
        s.wait("dve", sd, *s.latest(f"a1E{u}"))
        r = s.done("dve", nc.vector.tensor_reduce(mx[:, u, :], bank[u].rearrange("p (t d) -> p t d", t=2),
                                                  AX, ALU.max))
        s.wait("dve", r)
        s.done("dve", nc.vector.tensor_scalar(nb[:, u, :], mx[:, u, :], -SCALE, None, ALU.mult), f"a1nb{u}")

    def exponentials(b):
        u = b % 2
        s.wait("act", *s.latest(f"a1nb{u}", f"a1T{u}", f"a1ri{b}"))
        for j in range(2):
            s.done("act", nc.scalar.activation(
                Pr[:, u, j, :], bank[u][:, j * S:(j + 1) * S], ACT.Exp, bias=nb[:, u, j:j + 1],
                scale=SCALE, accum_out=rs[:, b, j:j + 1]), f"a1E{u}")
        s.relabel(f"a1E.{b}", f"a1E{u}")

    def transposed(b):
        u = b % 2
        s.wait("pe", *s.latest(f"a1E.{b}", f"a1PT{u}"))
        for c in range(2):
            for j in range(2):
                mm = nc.tensor.transpose(bank[2 + u][:, c * S + j * P:c * S + (j + 1) * P],
                                         Pr[:, u, j, c * P:(c + 1) * P], k.ident[:, :])
        td = s.done("pe", mm, f"a1T{u}")
        s.wait("act", td, *s.latest(f"a1A{u}"))
        s.done("act", nc.scalar.copy(PT[:, u, :, :], bank[2 + u].rearrange("p (t d) -> p t d", t=2)), f"a1PT{u}")
        s.wait("dve", *s.latest(f"a1E.{b}", f"a1add{b}"))
        s.done("dve", nc.vector.reciprocal(ri[:, b, :], rs[:, b, :]), f"a1ri{b}")

    def attend(b):
        u = b % 2
        s.wait("pe", *s.latest(f"a1PT{u}", "a1Z"))
        for c in range(2):
            mm = nc.tensor.matmul(bank[4][:, 0:S], ctok[:, 2 * b + c, :], PT[:, u, c, :],
                                  start=c == 0, stop=c == 1)
        ad = s.done("pe", mm, f"a1A{u}")
        s.wait("dve", ad, *s.latest(f"a1YZ{u}"))
        s.done("dve", nc.vector.tensor_copy(Z[:, u, :], bank[4][:, 0:S]), "a1Z")
        s.relabel(f"a1Z{u}", "a1Z")

    def result(p, b):
        u = b % 2
        s.wait("pe", *s.latest(f"a1Z{u}", f"a1Min{p}", "a1add"))
        for j in range(2):
            mm = nc.tensor.matmul(bank[5][:, j * D:(j + 1) * D], Z[:, u, j * P:(j + 1) * P], M[:, p, :],
                                  start=True, stop=True)
        yd = s.done("pe", mm, f"a1Y{p}")
        s.relabel(f"a1YZ{u}", f"a1Y{p}")
        s.wait("dve", yd, *s.latest(f"a1ri{b}", f"a1add{b}"))
        for j in range(2):
            t = 2 * b + j
            s.done("dve", nc.vector.scalar_tensor_tensor(
                k.X[:, t, :], bank[5][:, j * D:(j + 1) * D], ri[:, b, j:j + 1], k.X[:, t, :],
                ALU.mult, ALU.add), "a1add")
        s.relabel(f"a1add{b}", "a1add")

    def head(p, prior, follow):
        n = 1 - p
        between = {
            (0, 0): lambda: project(n, 0, 0), (0, 1): lambda: project(n, 1, 0),
            (0, 2): lambda: project(n, 0, 1),
            (1, 1): lambda: project(n, 1, 1),
            (2, 0): lambda: turn(n, 0, 0), (2, 1): lambda: turn(n, 1, 0),
            (3, 0): lambda: joined(n), (3, 1): lambda: turn(n, 0, 1), (3, 2): lambda: turn(n, 1, 1)}

        def fill(b, place):
            if follow and (b, place) in between:
                between[b, place]()

        for b in range(B):
            if b < B - 1:
                scores(p, b + 1)
            elif follow:
                scores(n, 0)
            fill(b, 0)
            transposed(b)
            fill(b, 1)
            if b < B - 1 or follow:
                exponentials((b + 1) % B)
            if b or prior:
                attend((b - 1) % B)
            if follow and b in (1, 2):
                normalise(b - 1)
            fill(b, 2)
            if b >= 2:
                result(p, b - 2)
            elif prior:
                result(n, b + 2)
            if follow and b < 2:
                sums(b)
            if not follow and b >= 2:
                k.tile_stats(2 * b - 4, s.last["a1add"])
                k.tile_stats(2 * b - 3)

    load(0, 0)
    load(1, 1)
    k.function(ACT.Exp)
    s.wait("pe", k.ctx_in, *k.bank_free)
    s.wait("act", k.tg_done, *k.bank_free)
    joined(0)
    project(0, 0, 0)
    project(0, 0, 1)
    ready = k.layernorm(readers)
    s.wait("dve", *readers)
    for half in range(2):
        s.wait("pe", *ready[half])
        project(0, 1, half)
        sums(half)
    s.wait("pe", cl)
    for half in range(2):
        normalise(half)
        for q in range(2):
            turn(0, q, half)
    scores(0, 0)
    exponentials(0)
    head(0, False, True)
    load(0, 2)
    head(1, True, True)
    load(1, 3)
    s.settle("a1")
    with s.repeat(NH // 2 - 2) as i:
        head(0, True, True)
        load(0, i * 2 + 4)
        head(1, True, True)
        load(1, i * 2 + 5)
    head(0, True, True)
    head(1, True, False)
    k.deviation(0)
    attend(3)
    result(1, 2)
    k.tile_stats(4, s.last["a1add"])
    k.tile_stats(5)
    result(1, 3)
    k.x_ready = [s.last["a1add1"], s.last["a1add3"]]
    k.bank_free = [s.last["a1add3"], s.last["a1b6"], s.last["a1b7"], s.last["a1E1"], s.last["a1PT1"]]
    k.bank_free = (k.bank_free + k.bank_free)[:8]
    return [s.last[n] for n in ("a1Y1", "a1add3", "a1b6", "a1b7", "a1PT0", "a1PT1", "a1E0", "a1E1",
                                "a1A0", "a1A1")]


class Ahead:

    def __init__(self, k, words):
        self.k, self.s, self.nc, self.words = k, k.s, k.nc, words

    def place(self):
        at, self.k.at = self.k.at, ARENA - self.words
        self.layout()
        self.k.at = at


class Attention2Ahead(Ahead):

    def __init__(self, k):
        super().__init__(k, 3696)

    def layout(self):
        k = self.k
        self.tiles = (
            k.place(6, D),
            k.place(DC, D),
            k.place(2, D),
            k.place(2, P),
            k.place(D),
            k.place(D), k.place(D),
            k.place(10),
            k.place(64))

    def start(self, readers):
        k, s, nc = self.k, self.s, self.nc
        self.place()
        W, Wo, bias, ind, bQ, bO, bV, aff, mean = self.tiles
        s.wait("sp", *readers)
        s.wait("act", *readers)
        s.wait("pool", *readers)
        self.w_in = s.loaded("a2w", nc.sync.dma_start(W, k.io["w2"]))
        l2 = s.loaded("a2b", nc.sync.dma_start(bias[0:2], k.io["bias2"]))
        l3 = s.loaded("a2i", nc.sync.dma_start(ind[0:2], k.io["ind2"]))
        l6 = s.loaded("a2a", nc.sync.dma_start(aff, k.io["aff2"]))
        l5 = s.loaded("a2o", nc.sync.dma_start(Wo, k.io["wo2"]))
        bv = s.done("pool", nc.gpsimd.tensor_tensor(bV, k.row("bv"), k.row("bvd"), ALU.add))
        bo = s.done("pool", nc.gpsimd.tensor_scalar(bO, k.row("bo"), k.tg[:, 2:3], None, ALU.mult))
        self.tokens = (l2, l3, l5, l6, bv, bo)

    def centre(self, dst, v, n):
        s, nc, mean = self.s, self.nc, self.tiles[-1]
        r = s.done("dve", nc.vector.tensor_reduce(mean[:, 0:n], v, AX, ALU.add))
        s.wait("dve", r)
        r = s.done("dve", nc.vector.tensor_scalar(mean[:, 0:n], mean[:, 0:n], 1.0 / 16, None, ALU.mult))
        s.wait("dve", r)
        r = s.done("dve", nc.vector.tensor_tensor(
            dst, v, mean[:, 0:n].unsqueeze(2).broadcast_to([P, n, 16]), ALU.subtract))
        s.wait("dve", r)
        return r

    @staticmethod
    def heads(v):
        return v.rearrange("p (h d) -> p h d", d=16)

    def finish(self):
        W, bQ = self.tiles[0], self.tiles[4]
        self.s.wait("dve", self.w_in)
        wv = self.heads(W[:, 0:4, :].rearrange("p a n -> p (a n)"))
        wc = self.centre(wv, wv, 64)
        self.centre(self.heads(bQ), self.heads(self.k.row("bq")), 16)
        self.tokens += (wc,)


def attention2(k, readers, ahead):
    nc, s = k.nc, k.s
    NH, HD, KM = 16, 16, S - SET2
    SCALE = HD ** -0.5
    k.at = 0
    bank = k.bank
    W, Wo, bias, ind, bQ, bO, bV, aff, mean = ahead.tiles
    bK = k.place(2, D)
    N = k.place(NT, 2, D)
    V = k.place(NT, NH, 32)
    KT = k.place(DC, T)
    QT = k.place(DC, T)
    xc, sq = k.place(4, 2 * NH, HD), k.place(2, 2 * NH, HD)
    va, rt = k.place(4, 2 * NH), k.place(4, 2 * NH)
    l2, l3, l5, l6, bv, bo, wc = ahead.tokens
    s.wait("pool", *readers)
    for b in range(B):
        nc.gpsimd.memset(V[:, 2 * b, :, HD:32], 0.0)
    s.wait("pe", l2, l3, *readers, *k.bank_free)
    for j in range(2):
        mm = nc.tensor.matmul(bank[7][:, j * D:(j + 1) * D], ind[0:2, j, :], bias[0:2, 0, :],
                              start=True, stop=True)
    bd = s.done("pe", mm)
    s.wait("dve", bd, *readers)
    heads = ahead.heads
    bc = ahead.centre(heads(bK.rearrange("p j n -> p (j n)")), heads(bank[7]), 2 * NH)
    s.last["a2p7"] = bc
    ready = k.layernorm(readers)
    s.wait("act", bv, bo, l6)
    s.wait("pool", bo, *ready[1], *ready[0])
    for h in range(2):
        xb = s.done("pool", nc.gpsimd.tensor_tensor(
            k.X[:, 4 * h:4 * h + 4, :], k.X[:, 4 * h:4 * h + 4, :],
            bO.unsqueeze(1).broadcast_to([P, 4, D]), ALU.add))
    ring = [0]

    def next_bank():
        b = 4 + ring[0] % 4
        ring[0] += 1
        s.wait("pe", s.last.get(f"a2p{b}"))
        return b

    def biased(n, b, biases):
        s.wait("dve", s.last.get(f"a2n{n - 4}"))
        r = s.done("dve", nc.vector.tensor_tensor(xc[:, n % 4].rearrange("p h d -> p (h d)"), bank[b],
                                                  biases, ALU.add), f"a2p{b}")
        s.wait("act", r, s.last.get(f"a2v{n - 2}"))
        s.done("act", nc.scalar.activation(sq[:, n % 2], xc[:, n % 4], ACT.Square), f"a2s{n}")

    def variance(n):
        s.wait("dve", s.last[f"a2s{n}"])
        r = s.done("dve", nc.vector.tensor_reduce(va[:, n % 4, :], sq[:, n % 2], AX, ALU.add), f"a2v{n}")
        s.wait("dve", r)
        r = s.done("dve", nc.vector.tensor_scalar(va[:, n % 4, :], va[:, n % 4, :], 1.0 / HD, 1e-6,
                                                  ALU.mult, ALU.add))
        s.wait("dve", r)
        r = s.done("dve", nc.vector.reciprocal(va[:, n % 4, :], va[:, n % 4, :]))
        s.wait("act", r)
        s.done("act", nc.scalar.activation(rt[:, n % 4, :], va[:, n % 4, :], ACT.Sqrt), f"a2r{n}")

    def scaled(n):
        s.wait("pool", s.last[f"a2r{n}"])
        b, q = n % 4, n // 4
        s.done("pool", nc.gpsimd.tensor_tensor(
            N[:, 2 * b:2 * b + 2, q, :].rearrange("p t (h d) -> p t h d", d=HD),
            xc[:, n % 4].rearrange("p (t h) d -> p t h d", t=2),
            rt[:, n % 4, :].rearrange("p (t h) -> p t h", t=2).unsqueeze(3).broadcast_to([P, 2, NH, HD]),
            ALU.mult), f"a2n{n}")

    def advance(n):
        if n - 1 >= 0:
            variance(n - 1)
        if n - 2 >= 0:
            scaled(n - 2)

    s.wait("pe", wc, bc, k.sets_in)
    for b in range(B):
        first, sets = k.cT[:, 2 * b * P:(2 * b + 1) * P], [k.sets[:, n, b, :] for n in range(2)]
        kb = next_bank()
        nc.tensor.matmul(bank[kb][:, 0:D], first, W[:, 2, :], start=True, stop=True)
        nc.tensor.matmul(bank[kb][:, D:], sets[0], W[:, 2, :], start=True, stop=False)
        kd = s.done("pe", nc.tensor.matmul(bank[kb][:, D:], sets[1], W[:, 3, :], start=False, stop=True))
        vb = next_bank()
        nc.tensor.matmul(bank[vb][:, 0:D], first, W[:, 4, :], start=True, stop=True)
        vd = s.done("pe", nc.tensor.matmul(bank[vb][:, D:], sets[0], W[:, 4, :], start=True, stop=True))
        v2 = next_bank()
        v2d = s.done("pe", nc.tensor.matmul(bank[v2][:, 0:D], sets[1], W[:, 5, :], start=True, stop=True))
        s.wait("dve", kd)
        biased(b, kb, bK.rearrange("p j n -> p (j n)"))
        s.wait("act", vd)
        s.done("act", nc.scalar.copy(
            V[:, 2 * b:2 * b + 2, :, 0:HD].rearrange("p t h d -> p (t h) d"), heads(bank[vb])), f"a2p{vb}")
        s.wait("act", v2d)
        vin = s.done("act", nc.scalar.copy(V[:, 2 * b + 1, :, HD:32], heads(bank[v2][:, 0:D])), f"a2p{v2}")
        advance(b)
    def turned_over(q, half):
        for c in range(DC):
            b = (2 * half + c) % 4
            s.wait("pe", s.last[f"a2n{4 * q + 2 * half + 1}"], s.last.get(f"a2q{b}"))
            for j in range(4):
                mm = nc.tensor.transpose(bank[b][:, j * P:(j + 1) * P],
                                         N[:, 4 * half + j, q, c * P:(c + 1) * P], k.ident[:, :])
            td = s.done("pe", mm)
            cols = slice(half * HALF, (half + 1) * HALF)
            if q:
                s.wait("act", td)
                s.done("act", nc.scalar.activation(QT[:, c, cols], bank[b], ACT.Identity, scale=aff[:, 0:1],
                                                   bias=aff[:, 1:2]), f"a2q{b}")
                continue
            s.wait("dve", td)
            dv = KT[:, c, cols].rearrange("p (b t) -> p b t", b=2)
            sv = bank[b].rearrange("p (b t) -> p b t", b=2)
            for n, keys in ((2, slice(0, KM)), (4, slice(KM, S))):
                s.done("dve", nc.vector.tensor_scalar(dv[:, :, keys], sv[:, :, keys], aff[:, n:n + 1],
                                                      aff[:, n + 1:n + 2], ALU.mult, ALU.add), f"a2q{b}")
            s.relabel("a2keys", f"a2q{b}")

    s.wait("dve", l6)
    for b in range(B):
        qb = next_bank()
        for j in range(2):
            for c in range(DC):
                t = 2 * b + j
                mm = nc.tensor.matmul(bank[qb][:, j * D:(j + 1) * D], k.xT[:, c, t * P:(t + 1) * P],
                                      W[:, c, :], start=c == 0, stop=c == DC - 1)
        qd = s.done("pe", mm)
        s.wait("dve", qd)
        s.wait("dve", s.last.get(f"a2n{b}"))
        s.done("dve", nc.vector.tensor_tensor(
            xc[:, b].rearrange("p (t h) d -> p t (h d)", t=2), bank[qb].rearrange("p (t n) -> p t n", t=2),
            bQ.unsqueeze(1).broadcast_to([P, 2, D]), ALU.add), f"a2p{qb}")
        s.wait("act", s.last[f"a2p{qb}"], s.last[f"a2v{b + 2}"])
        s.done("act", nc.scalar.activation(sq[:, b % 2], xc[:, b], ACT.Square), f"a2s{b + 4}")
        advance(b + 4)
        if b >= 2:
            turned_over(0, b - 2)
    advance(2 * B)
    scaled(2 * B - 1)
    k.function(ACT.Exp)
    turned_over(1, 0)
    made, keys_made = s.last["a2q1"], s.last["a2keys"]

    Kb = k.place(DC, S)
    Qb = k.place(4, DC, S)
    Vb = k.place(2, NH, 32)
    OS = k.place(4, S)
    Pr = k.place(2, 4, S)
    PT = k.place(4, 2, S)
    mx, nb, mxd = k.place(2, 4), k.place(2, 4), k.place(2, 4)
    sums, inv = k.place(2, NH, 2), k.place(2, NH, 2)
    Ob, Od = k.place(2, NH, HD), k.place(2, NH, HD)
    obv = Ob.rearrange("p j h d -> p j (h d)")
    OT = k.place(DC, S)
    for e in ("pe", "dve", "act", "pool"):
        s.wait(e, made, keys_made, vin, l5, xb, s.last["a2p4"], s.last["a2p5"], s.last["a2p6"], s.last["a2p7"])

    def fetch(b, c):
        cols = bass.ds(b * S, S)
        s.wait("dve", *s.latest(f"a2S{4 * c + 3}"))
        s.wait("pool", *s.latest(f"a2S{4 * c + 3}"))
        s.done("dve", nc.vector.tensor_scalar(Qb[:, 0, c], QT[:, c, cols], aff[:, 6:7], None, ALU.mult))
        s.done("dve", nc.vector.tensor_copy(Kb[:, c], KT[:, c, cols]))
        s.done("dve", nc.vector.tensor_scalar(Qb[:, 1, c], QT[:, c, cols], aff[:, 7:8], None, ALU.mult),
               f"a2Qb{c}")
        for v in (2, 3):
            s.done("pool", nc.gpsimd.tensor_tensor(
                Qb[:, v, c], QT[:, c, cols], aff[:, 6 + v:7 + v].broadcast_to([P, S]), ALU.mult), f"a2Qc{c}")

    def fetch_values(b, half):
        s.wait("pool", *s.latest("a2AV1"))
        hs = slice(half * 8, half * 8 + 8)
        s.done("pool", nc.gpsimd.tensor_copy(Vb[:, :, hs, :], V[:, bass.ds(b * 2, 2), hs, :]), f"a2Vb{half}")

    def scores(g):
        u, h0 = g % 2, 2 * g
        s.wait("pe", *s.latest(f"a2E{u}", f"a2sub{u}", f"a2Qb{g // 4}"))
        if g % 2:
            s.wait("pe", *s.latest(f"a2Qc{g // 4}"))
        pr, made = Pr[:, u], []
        for h in (h0, h0 + 1):
            c, r, e = h // 8, h % 8 // 4 * 64, h % 2
            for j in range(2):
                mm = nc.tensor.matmul(
                    bank[2 * u + e][:, j * S:(j + 1) * S], Qb[r:r + 64, h % 4, c, j * P:(j + 1) * P],
                    Kb[r:r + 64, c, :], start=True, stop=True)
            made.append(s.done("pe", mm, f"a2S{g}"))
        s.wait("dve", *s.latest(f"a2T{u}", f"a2E{u}", f"a2sub{u}"))
        for e in range(2):
            v, two = bank[2 * u + e].rearrange("p (a t) -> p a t", t=S), slice(2 * e, 2 * e + 2)
            s.wait("dve", made[e])
            r1 = s.done("dve", nc.vector.tensor_reduce(mxd[:, u, two], v[:, :, KM:S], AX, ALU.max))
            r = s.done("dve", nc.vector.tensor_reduce(mx[:, u, two], v[:, :, 0:KM], AX, ALU.max))
            s.wait("dve", r1)
            s.done("dve", nc.vector.tensor_tensor(
                pr[:, two, KM:S], v[:, :, KM:S], mxd[:, u, two].unsqueeze(2).broadcast_to([P, 2, S - KM]),
                ALU.subtract), f"a2sub{u}")
            s.wait("dve", r)
            s.done("dve", nc.vector.tensor_scalar(nb[:, u, two], mx[:, u, two], -SCALE, None, ALU.mult),
                   f"a2nb{u}{e}")

    def exponentials(g):
        u, h0 = g % 2, 2 * g
        v, pr = k.psum[:, 2 * u * 512:(2 * u + 2) * 512].rearrange("p (a t) -> p a t", t=S), Pr[:, u]
        s.wait("act", *s.latest(f"a2inv{g}", f"a2T{u}"))
        for a in range(4):
            if a % 2 == 0:
                s.wait("act", *s.latest(f"a2nb{u}{a // 2}"))
            s.done("act", nc.scalar.activation(pr[:, a, 0:KM], v[:, a, 0:KM], ACT.Exp, bias=nb[:, u, a:a + 1],
                                               scale=SCALE, accum_out=sums[:, a % 2, h0 + a // 2, 0:1]))
        s.done("act", nc.scalar.activation(pr[:, :, KM:S], pr[:, :, KM:S], ACT.Exp, scale=SCALE),
               f"a2E{u}")

    def second_sums(g):
        u = g % 2
        s.wait("dve", *s.latest(f"a2E{u}"))
        s.done("dve", nc.vector.tensor_reduce(
            sums[:, :, 2 * g:2 * g + 2, 1].rearrange("p j h -> p h j"),
            Pr[:, u, :, KM:S].rearrange("p (h j) t -> p h j t", h=2), AX, ALU.add), f"a2sum{u}")

    def inverse(g):
        s.wait("dve", *s.latest(f"a2sum{g % 2}", "a2O"))
        s.done("dve", nc.vector.reciprocal(inv[:, :, 2 * g:2 * g + 2, :], sums[:, :, 2 * g:2 * g + 2, :]),
               f"a2inv{g}")

    def transposed(g):
        u = g % 2
        s.wait("pe", *s.latest(f"a2E{u}"))
        for w in range(2):
            s.wait("pe", *s.latest(f"a2t{w}"))
            for c in range(2):
                for j in range(2):
                    mm = nc.tensor.transpose(bank[4 + w][:, c * S + j * P:c * S + (j + 1) * P],
                                             Pr[:, u, 2 * w + j, c * P:(c + 1) * P], k.ident[:, :])
            td = s.done("pe", mm, f"a2T{u}")
            eng, engine = ("dve", nc.vector.tensor_copy) if w else ("act", nc.scalar.copy)
            s.wait(eng, td, *s.latest(f"a2AV{u}"))
            s.done(eng, engine(PT[:, 2 * u + w, :, :], bank[4 + w].rearrange("p (t d) -> p t d", t=2)),
                   f"a2t{w}")
            s.relabel(f"a2PT{u}{w}", f"a2t{w}")

    def attend(g):
        u = g % 2
        s.wait("pe", *s.latest("a2OSa", "a2OS", "a2O", f"a2Vb{g // 4}"))
        for w in range(2):
            h = 2 * g + w
            s.wait("pe", *s.latest(f"a2PT{u}{w}"))
            at = 6 * 512 + h // 4 * S
            for c in range(2):
                mm = nc.tensor.matmul(
                    k.psum[h % 4 * 32:(h % 4 + 1) * 32, at:at + S], Vb[:, c, h, :],
                    PT[:, 2 * u + w, c, :], start=c == 0, stop=c == 1)
        return s.done("pe", mm, f"a2AV{u}")

    def turned():
        s.wait("pe", *s.latest("a2OSa", "a2OS"))
        for j in range(2):
            for q in range(4):
                mm = nc.tensor.transpose(bank[6 + j][:, q * P:(q + 1) * P], OS[:, q, j * P:(j + 1) * P],
                                         k.ident[:, :])
        s.done("pe", mm, "a2OSr")

    def normalised(eng="pool", engine=nc.gpsimd):
        s.wait("dve", *s.latest("a2OSr", "a2inv7", "a2OTr"))
        o = k.psum[:, 6 * 512:8 * 512].rearrange("p (h e d) -> p h e d", e=2, d=HD)
        iv = inv.rearrange("p j h e -> p (j h) e")
        for e, dst in ((0, Ob), (1, Od)):
            r = s.done("dve", nc.vector.tensor_tensor(
                dst.rearrange("p j h d -> p (j h) d"), o[:, :, e, :],
                iv[:, :, e].unsqueeze(2).broadcast_to([P, 2 * NH, HD]), ALU.mult), "a2O")
        s.wait(eng, r)
        r = s.done(eng, engine.tensor_tensor(Ob, Ob, Od, ALU.add))
        s.wait(eng, r)
        s.done(eng, engine.tensor_tensor(obv, obv, bV.unsqueeze(1).broadcast_to([P, 2, D]), ALU.add),
               "a2Ob")

    def out_transposed():
        s.wait("pe", *s.latest("a2Ob", "a2t0"))
        for c in range(DC):
            for j in range(2):
                mm = nc.tensor.transpose(bank[4][:, c * S + j * P:c * S + (j + 1) * P],
                                         obv[:, j, c * P:(c + 1) * P], k.ident[:, :])
        td = s.done("pe", mm, "a2OTr")
        s.wait("act", td, *s.latest("a2Y"))
        s.done("act", nc.scalar.copy(OT, bank[4].rearrange("p (c t) -> p c t", c=DC)), "a2OT")
        s.relabel("a2t0", "a2OT")

    def project(b, measured=False):
        s.wait("pe", *s.latest("a2OT", "a2t1"))
        for j in range(2):
            for c in range(DC):
                mm = nc.tensor.matmul(bank[5][:, j * D:(j + 1) * D], OT[:, c, j * P:(j + 1) * P],
                                      Wo[:, c, :], start=c == 0, stop=c == DC - 1)
        yd = s.done("pe", mm, "a2Y")
        s.wait("dve", yd)
        X2 = k.X[:, bass.ds(b * 2, 2), :]
        s.done("dve", nc.vector.scalar_tensor_tensor(
            X2, bank[5].rearrange("p (t d) -> p t d", t=2), k.tg[:, 2:3], X2, ALU.mult, ALU.add), "a2t1")
        if measured:
            k.tile_stats(2 * b, s.last["a2t1"])
            k.tile_stats(2 * b + 1)
        return yd

    def batch(b, prior, follow):
        steps = NH // 2
        for g in range(steps):
            if g + 1 < steps:
                scores(g + 1)
            elif follow:
                scores(0)
            if follow and g in (4, 7):
                fetch(b + 1, g // 7)
            second_sums(g)
            transposed(g)
            if g + 1 < steps or follow:
                exponentials((g + 1) % steps)
            if prior is not None:
                if g == 0:
                    turned()
                    normalised()
                elif g == 2:
                    out_transposed()
                elif g == 3:
                    project(prior, not follow)
            inverse(g)
            if g == 0:
                fetch_values(b, 1)
            if g == steps - 2 and follow:
                fetch_values(b + 1, 0)
            if g >= 1:
                attend(g - 1)
        ad = attend(steps - 1)
        s.wait("act", ad, *s.latest("a2OSr"))
        s.wait("dve", ad, *s.latest("a2OSr"))
        s.done("act", nc.scalar.copy(OS[:, 0:2, :], bank[6].rearrange("p (q t) -> p q t", q=2)), "a2OSa")
        s.done("dve", nc.vector.tensor_copy(OS[:, 2:4, :], bank[7].rearrange("p (q t) -> p q t", q=2)),
               "a2OS")

    fetch(0, 0)
    fetch(0, 1)
    fetch_values(0, 0)
    scores(0)
    turned_over(1, 1)
    exponentials(0)
    for e in ("pe", "dve", "act", "pool"):
        s.wait(e, s.last["a2q3"])
    batch(0, None, True)
    s.settle("a2")
    with s.repeat(B - 2) as it:
        batch(it + 1, it, True)
    batch(B - 1, B - 2, False)
    turned()
    normalised("dve", nc.vector)
    out_transposed()
    for tile in range(4):
        k.tile_stats(tile)
    k.deviation(0)
    yd = project(B - 1, True)
    k.x_ready = [s.last["a2t1"]] * 2
    k.bank_free = [s.last["a2t1"]] * 8
    return [yd, s.last["a2t1"], s.last["a2E0"], s.last["a2E1"], s.last["a2t0"]]


class QuantisedAhead(Ahead):
    EPS = 1e-6

    def __init__(self, k):
        super().__init__(k, 5152)

    def layout(self):
        k = self.k
        self.tiles = (
            k.place(NT, D),
            k.place(DC, T),
            k.place(NT, C),
            k.place(2, 16))

    def start(self, readers):
        k, s, nc = self.k, self.s, self.nc
        self.place()
        w1, w1T, w2, _ = self.tiles
        s.wait("sp", *readers)
        self.tokens = [s.loaded("q1T", nc.sync.dma_start(w1T, k.io["fsideT"])),
                       s.loaded("q1", nc.sync.dma_start(w1, k.io["fside"])),
                       s.loaded("q2", nc.sync.dma_start(w2, k.io["ctok"]))]

    def finish(self):
        k, s, nc = self.k, self.s, self.nc
        w1T, largest = self.tiles[1], self.tiles[3]
        s.wait("dve", self.tokens[0])
        self.inverse = []
        for j, v in enumerate((w1T.rearrange("p c (b t) -> p (c b) t", b=B),
                               k.cT[:, :].rearrange("p (b t) -> p b t", b=B))):
            aw = largest[:, j, 0:v.shape[1]]
            r = s.done("dve", nc.vector.tensor_reduce(aw, v, AX, ALU.max, apply_absolute_value=True))
            s.wait("dve", r)
            r = s.done("dve", nc.vector.tensor_scalar(aw, aw, self.EPS, None, ALU.max))
            s.wait("dve", r)
            self.tokens.append(s.done("dve", nc.vector.reciprocal(aw, aw)))
            self.inverse.append(aw)


def quantised_layer(k, readers, ahead):
    nc, s = k.nc, k.s
    EPS, QMAX, MAGIC = ahead.EPS, 127.0, 1.5 * 2.0 ** 23
    k.at = 0
    bank = k.bank
    w1, w1T, w2, _ = ahead.tiles
    XS, WS = k.place(NT, D), k.place(NT, D)
    XQ, WQ = k.place(NT, D, dt=BF16), k.place(NT, D, dt=BF16)
    XQT, WQT = k.place(DC, T, dt=BF16), k.place(DC, T, dt=BF16)
    hid, act = k.place(NT, D), k.place(NT, P)
    identb = k.place(P, dt=BF16)
    small = k.place(12, 8)
    magic = k.place(2)
    sB = k.place(NT * P)
    s.wait("pool", *readers, k.ident_in)
    nc.gpsimd.memset(magic[:, 0:1], MAGIC)
    nc.gpsimd.memset(magic[:, 1:2], -MAGIC)
    cst = s.done("pool", nc.gpsimd.tensor_copy(identb, k.ident[:, :]))
    for e in ("dve", "act", "pe", "pool"):
        s.wait(e, *readers, *ahead.tokens, cst)

    def dve(ins):
        t = s.done("dve", ins)
        s.wait("dve", t)
        return t

    def rows_of(cols, b0):
        for j, col in enumerate(cols):
            mm = nc.tensor.transpose(bank[b0 + j // 4][:, j % 4 * P:(j % 4 + 1) * P],
                                     col.broadcast_to([P, P]), k.ident[:, :])
        return s.done("pe", mm)

    def scale_of(v, scale, inv):
        dve(nc.vector.tensor_reduce(scale, v, AX, ALU.max, apply_absolute_value=True))
        dve(nc.vector.tensor_scalar(scale, scale, EPS, 1.0 / QMAX, ALU.max, ALU.mult))
        return dve(nc.vector.reciprocal(inv, scale))

    def linear(x_tok, x_feat, w_rows, aw, nd, evacuate, at_once=None):
        ax, sm, rs = (small[:, j, 0:nd * B] for j in range(3))
        xsc, wsc, xin, win = (small[:, j, :] for j in range(4, 8))
        F = nd * P
        dve(nc.vector.tensor_reduce(ax, x_feat, AX, ALU.max, apply_absolute_value=True))
        dve(nc.vector.tensor_scalar(ax, ax, EPS, None, ALU.max))
        t = dve(nc.vector.tensor_tensor(sm, ax, aw, ALU.mult))
        s.wait("pool", t)
        t = s.done("pool", nc.gpsimd.tensor_tensor(sm, sm, k.phalf[:, 0:nd * B], ALU.pow))
        s.wait("dve", t)
        tm = dve(nc.vector.tensor_scalar(sm, sm, EPS, None, ALU.max))
        tr = dve(nc.vector.reciprocal(rs, sm))

        def along(v):
            return [v[:, c * B + b:c * B + b + 1] for b in range(B) for c in range(nd)]

        def scaled(engine, dst, src, r):
            r = r.rearrange("p (b f) -> p b f", b=B)
            return engine.tensor_tensor(
                dst.rearrange("p (b j) f -> p b j f", b=B), src.rearrange("p (b j) f -> p b j f", b=B),
                r.unsqueeze(2).broadcast_to([P, B, 2, F]), ALU.mult)

        xs, ws = XS[:, :, 0:F], WS[:, :, 0:F]
        xq, wq = XQ[:, :, 0:F], WQ[:, :, 0:F]
        s.wait("pe", tm, tr)
        rx = rows_of(along(rs), 0)
        rw = rows_of(along(sm), 2)
        s.wait("act", rw)
        rc = s.done("act", nc.scalar.copy(sB[:, 0:B * F], k.psum[:, 1024:1024 + B * F]))
        s.wait("pool", rc)
        wd = s.done("pool", scaled(nc.gpsimd, ws, w_rows, sB[:, 0:B * F]))
        s.wait("dve", rx)
        dve(scaled(nc.vector, xs, x_tok, k.psum[:, 0:B * F]))
        tx = scale_of(xs, xsc, xin)
        s.wait("act", tx)
        for t in range(NT):
            if t % 2:
                hx = s.done("act", nc.scalar.activation(xs[:, t, :], xs[:, t, :], ACT.Identity,
                                                        scale=xin[:, t:t + 1], bias=magic[:, 0:1]))
            else:
                hd = s.done("dve", nc.vector.tensor_scalar(xs[:, t, :], xs[:, t, :], xin[:, t:t + 1],
                                                           MAGIC, ALU.mult, ALU.add))
        s.wait("dve", hx, hd)
        tb = s.done("dve", nc.vector.tensor_scalar(xs, xs, MAGIC + QMAX, MAGIC - QMAX, ALU.min, ALU.max))
        s.wait("act", tb)
        tq = s.done("act", nc.scalar.activation(xq, xs, ACT.Identity, bias=magic[:, 1:2]))
        s.wait("dve", wd)
        t = scale_of(ws, wsc, win)
        s.wait("act", t)
        s.wait("pe", t, rw)
        wr = rows_of([wsc[:, t:t + 1] for t in range(NT)], 0)
        for t in range(NT):
            if t % 2:
                hx = s.done("act", nc.scalar.activation(ws[:, t, :], ws[:, t, :], ACT.Identity,
                                                        scale=win[:, t:t + 1], bias=magic[:, 0:1]))
            else:
                hd = s.done("dve", nc.vector.tensor_scalar(ws[:, t, :], ws[:, t, :], win[:, t:t + 1],
                                                           MAGIC, ALU.mult, ALU.add))
        s.wait("act", wr, wd)
        tr = s.done("act", nc.scalar.copy(sB, k.psum[:, 0:2 * 512]))
        s.wait("dve", hx, hd)
        tb = dve(nc.vector.tensor_scalar(ws, ws, MAGIC + QMAX, MAGIC - QMAX, ALU.min, ALU.max))
        tw = dve(nc.vector.tensor_scalar(wq, ws, MAGIC, None, ALU.subtract))
        n = 0
        for src, dst, ready_q in ((xq, XQT, tq), (wq, WQT, tw)):
            s.wait("pe", ready_q)
            for c in range(nd):
                bb = 4 + n % 2
                n += 1
                s.wait("pe", s.last.get(f"qb{bb}"))
                half = bank[bb].bitcast(BF16)
                for t in range(NT):
                    mm = nc.tensor.transpose(half[:, t * P:(t + 1) * P], src[:, t, c * P:(c + 1) * P],
                                             identb)
                td = s.done("pe", mm)
                s.wait("act", td)
                s.done("act", nc.scalar.copy(dst[:, c, :], half), f"qb{bb}")
        s.wait("dve", tr)
        s.wait("pe", s.last["qb4"], s.last["qb5"])
        for b in range(B):
            for j in range(2):
                t, bb = 2 * b + j, 4 + b % 4
                if j == 0:
                    s.wait("pe", s.last.get(f"qo{bb}"))
                for c in range(nd):
                    mm = nc.tensor.matmul(bank[bb][:, j * D:(j + 1) * D], XQT[:, c, t * P:(t + 1) * P],
                                          WQT[:, c, b * D:(b + 1) * D], start=c == 0, stop=c == nd - 1)
            td = s.done("pe", mm)
            s.wait("dve", td)
            for j in range(2):
                t = 2 * b + j
                r = s.done("dve", nc.vector.scalar_tensor_tensor(
                    hid[:, t, :], bank[bb][:, j * D:(j + 1) * D], xsc[:, t:t + 1],
                    sB[:, b * D:(b + 1) * D], ALU.mult, ALU.mult),
                    f"qo{bb}")
            if at_once:
                at_once(b)
            if b:
                evacuate(b - 1)
        evacuate(B - 1)

    def silu(b):
        s.wait("act", s.last[f"qo{4 + b}"])
        tiles = slice(2 * b, 2 * b + 2)
        s.done("act", nc.scalar.activation(act[:, tiles, :], hid[:, tiles, 0:P], ACT.Silu), f"qg{b}")

    def gated(b):
        tiles = slice(2 * b, 2 * b + 2)
        s.wait("dve", s.last[f"qo{4 + b}"], s.last[f"qg{b}"])
        s.done("dve", nc.vector.tensor_tensor(act[:, tiles, :], act[:, tiles, :], hid[:, tiles, P:D],
                                              ALU.mult), "qact")

    aw1, aw2 = ahead.inverse
    k.function(ACT.Silu)
    ready = k.layernorm(readers)
    for e in ("dve", "act", "pe", "pool"):
        s.wait(e, *readers, *ready[0], *ready[1], *k.bank_free)
    linear(k.xn[:, :, :], k.xT[:, :, :].rearrange("p c (b t) -> p (c b) t", b=B), w1, aw1, DC, gated,
           silu)
    s.wait("pe", s.last["qact"], s.last["qo6"], s.last["qo7"])
    for t in range(NT):
        mm = nc.tensor.transpose(bank[6 + t // 4][:, t % 4 * P:(t % 4 + 1) * P], act[:, t, :],
                                 k.ident[:, :])
    td = s.done("pe", mm)
    s.wait("dve", td, s.last["qact"])
    s.wait("pe", s.last["qo4"], s.last["qo5"])

    def added(b):
        s.wait("dve", s.last[f"qo{4 + b}"])
        X2 = k.X[:, 2 * b:2 * b + 2, :]
        s.done("dve", nc.vector.scalar_tensor_tensor(
            X2, hid[:, 2 * b:2 * b + 2, :], k.tg[:, 3:4], X2, ALU.mult, ALU.add), f"qx{b // 2}")
        k.tile_stats(2 * b, s.last[f"qx{b // 2}"])
        k.tile_stats(2 * b + 1)
        if b == 1:
            k.deviation(0)

    linear(act, k.psum[:, 6 * 512:8 * 512].rearrange("p (b t) -> p b t", b=B), w2, aw2, 1, added)
    k.x_ready = [s.last["qx0"], s.last["qx1"]]
    k.bank_free = [s.last["qx1"]] * 8
    return [s.last["qx1"], s.last["qb4"], s.last["qb5"], td]


def chosen_ffn(k, readers):
    nc, s = k.nc, k.s
    KEEP, NF = KEEP3, 8
    k.at = 0
    bank = k.bank
    W1, W2 = k.place(DC, NF, P), k.place(NF, D)
    wr = k.place(DC, B, B)
    w4, left, top, mask = k.place(S), k.place(S), k.place(8), k.place(S)
    pos, zero = k.place(S), k.place(S)
    R = k.place(S)
    RT = k.place(2, 96)
    sel = k.place(NT, P)
    selT = k.place(NT, P)
    xg = k.place(DC, 2 * P)
    H = k.place(NF, 2 * P)
    blk = k.place(2, D)
    s.wait("sp", *readers)
    l0 = s.loaded("cr", nc.sync.dma_start(wr, k.io["router3"]))
    l1 = s.loaded("c1", nc.sync.dma_start(W1, k.io["w31"]))
    l2 = s.loaded("c2", nc.sync.dma_start(W2, k.io["w32"]))
    s.wait("pool", *readers)
    nc.gpsimd.memset(zero, 0.0)
    cleared = s.done("pool", nc.gpsimd.memset(R, 0.0))
    k.function(ACT.Gelu_apprx_tanh)
    ready = k.layernorm(readers)
    for e in ("dve", "act"):
        s.wait(e, *readers, cleared, *ready[0], *ready[1], *k.bank_free)
    s.wait("pe", *readers, cleared, *k.bank_free)

    def dve(ins):
        t = s.done("dve", ins)
        s.wait("dve", t)
        return t

    s.wait("pe", l0)
    for b in range(B):
        s.wait("pe", *ready[b // 2])
        for c in range(DC):
            mm = nc.tensor.matmul(bank[0][0:B, 0:S], wr[:, c, b, :], k.xT[:, c, b * S:(b + 1) * S],
                                  start=b == 0 and c == 0, stop=b == B - 1 and c == DC - 1)
    t = s.done("pe", mm)
    s.wait("dve", t)
    r4 = slice(0, B)
    dve(nc.vector.tensor_scalar(w4[r4], bank[0][r4, 0:S], k.row("b_r")[r4], None, ALU.add))
    dve(nc.vector.tensor_copy(left[r4], w4[r4]))
    for n in range(KEEP // 8):
        dve(nc.vector.max(top[r4], left[r4]))
        if n < KEEP // 8 - 1:
            dve(nc.vector.match_replace(left[r4], top[r4], left[r4], -BIG))
    dve(nc.vector.tensor_scalar(mask[r4], w4[r4], top[r4, 7:8], None, ALU.is_gt))
    dve(nc.vector.tensor_tensor_scan(pos[r4], mask[r4], zero[r4], 0.0, ALU.add, ALU.add))
    dve(nc.vector.scalar_tensor_tensor(R[r4], pos[r4], k.col("slot0")[r4], mask[r4], ALU.add, ALU.mult))
    dve(nc.vector.tensor_scalar(R[r4], R[r4], 1.0, None, ALU.subtract))
    dve(nc.vector.tensor_tensor(R[32:32 + B], w4[r4], mask[r4], ALU.mult))
    t = dve(nc.vector.tensor_scalar(R[64:64 + B], mask[r4], -1.0, 1.0, ALU.mult, ALU.add))
    s.wait("pe", t)
    for j in range(2):
        mm = nc.tensor.transpose(bank[1][:, j * P:j * P + 96], R[0:96, j * P:(j + 1) * P],
                                 k.ident[0:96, 0:96])
    t = s.done("pe", mm)
    s.wait("dve", t)
    b1v = bank[1][:, 0:2 * P].rearrange("p (j n) -> p j n", j=2)
    dve(nc.vector.tensor_copy(RT[:, :, 0:32], b1v[:, :, 0:32]))
    rt = dve(nc.vector.tensor_scalar(RT[:, :, 32:96], b1v[:, :, 32:96], k.tg[:, 7:8], None, ALU.mult))
    for t8 in range(NT):
        b, j = t8 // 2, t8 % 2
        t = s.done("dve", nc.vector.tensor_scalar(sel[:, t8, :], k.row("iota"), RT[:, j, b:b + 1], None,
                                                  ALU.is_equal))
    s.wait("pe", t)
    for c in range(DC):
        for t8 in range(NT):
            g = t8 // 4
            mm = nc.tensor.matmul(bank[2][:, (2 * c + g) * P:(2 * c + g + 1) * P],
                                  k.xn[:, t8, c * P:(c + 1) * P], sel[:, t8, :],
                                  start=t8 % 4 == 0, stop=t8 % 4 == 3)
    t = s.done("pe", mm)
    s.wait("act", t)
    xgd = s.done("act", nc.scalar.copy(xg, bank[2].rearrange("p (c n) -> p c n", c=DC)))
    for t8 in range(NT):
        mm = nc.tensor.transpose(bank[6 + t8 // 4][:, t8 % 4 * P:(t8 % 4 + 1) * P], sel[:, t8, :],
                                 k.ident[:, :])
    t = s.done("pe", mm)
    s.wait("dve", t)
    stt = s.done("dve", nc.vector.tensor_copy(selT.rearrange("p t n -> p (t n)"),
                                              k.psum[:, 6 * 512:8 * 512]))
    for t8 in range(NT):
        b, j = t8 // 2, t8 % 2
        ps = s.done("dve", nc.vector.scalar_tensor_tensor(
            k.X[:, t8, :], k.xn[:, t8, :], RT[:, j, 64 + b:65 + b], k.X[:, t8, :], ALU.mult, ALU.add))
    s.wait("pe", xgd, l1)
    for f in range(NF):
        bb = 3 + f % 2
        s.wait("pe", s.last.get(f"cb{bb}"))
        for c in range(DC):
            mm = nc.tensor.matmul(bank[bb][:, 0:2 * P], W1[:, c, f, :], xg[:, c, :], start=c == 0,
                                  stop=c == DC - 1)
        t = s.done("pe", mm)
        s.wait("act", t)
        hd = s.done("act", nc.scalar.activation(H[:, f, :], bank[bb][:, 0:2 * P], ACT.Gelu_apprx_tanh,
                                                bias=k.col("b1", f)), f"cb{bb}")
    s.wait("pe", hd, l2)
    s.wait("dve", ps)

    def second(g, chunks):
        for f in chunks:
            mm = nc.tensor.matmul(bank[(5, 1)[g]][:, 0:D], H[:, f, g * P:(g + 1) * P], W2[:, f, :],
                                  start=f == 0, stop=f == NF - 1)
        if chunks[-1] == NF - 1:
            td = s.done("pe", mm)
            s.wait("dve", td)
            s.done("dve", nc.vector.tensor_tensor(blk[:, g, :], bank[(5, 1)[g]][:, 0:D], k.row("b2"),
                                                  ALU.add), f"cblk{g}")

    def scatter(g):
        s.wait("pe", s.last[f"cblk{g}"], stt, ps)
        for i in range(4):
            t8 = 4 * g + i
            b, j, bb = t8 // 2, t8 % 2, (0, 2, 3, 4, 6, 7, 0, 2)[t8]
            s.wait("pe", s.last.get(f"cs{bb}"))
            mm = nc.tensor.matmul(bank[bb][:, 0:D], selT[:, t8, :], blk[:, g, :], start=True, stop=True)
            td = s.done("pe", mm)
            s.wait("dve", td)
            a = s.done("dve", nc.vector.scalar_tensor_tensor(
                k.X[:, t8, :], bank[bb][:, 0:D], RT[:, j, 32 + b:33 + b], k.X[:, t8, :],
                ALU.mult, ALU.add), f"cs{bb}")
        k.x_ready[g] = a
        return a, td

    second(0, range(NF))
    second(1, range(NF // 2))
    scatter(0)
    second(1, range(NF // 2, NF))
    a, t = scatter(1)
    k.bank_free = [a] * 8
    return [a, t, hd]


def program(nc, io, plan, ctx):
    k = Core(nc, ctx, io, plan)
    k.load_constants()
    ahead2, ahead3 = Attention2Ahead(k), QuantisedAhead(k)
    readers = mamba(k)
    readers = dense_ffn(k, readers)
    readers = attention1(k, readers)
    readers = moe(k, readers, "m1", io["router1"], io["moe1"], E1, E1K, 5, 1, ahead2)
    readers = attention2(k, readers, ahead2)
    readers = moe(k, readers, "m2", io["router2"], io["moe2"], E2, E2K, 6, 0, ahead3)
    readers = quantised_layer(k, readers, ahead3)
    chosen_ffn(k, readers)
    k.finish()
    return k.s.found


def layout(inputs):
    import numpy as np

    a = {n: np.asarray(v) for n, v in inputs.items()}

    def tiles(v):
        return v.reshape(-1, P, *v.shape[1:]).swapaxes(0, 1)

    def chunks(v, n):
        z = np.zeros((n * P,), v.dtype)
        z[:v.size] = v
        return z.reshape(n, P).T

    def joined(wk, wv):
        w = np.concatenate([wk, wv], axis=-1).reshape(-1, 16, 2, 16)
        return w[:, :, 0].reshape(-1, D), w[:, :, 1].reshape(-1, D)

    wk2, wv2 = joined(a["L2_xattn_Wk"], a["L2_xattn_Wv"])
    bk2, bv2 = (v.reshape(-1) for v in joined(a["L2_xattn_bk"], a["L2_xattn_bv"]))
    out = {}
    out["x"] = tiles(a["x"].reshape(T, D))
    out["cT"] = a["ctx_1024"].reshape(T, C).T
    out["ident"] = np.eye(P, dtype=np.float32)
    g = np.concatenate([a["g_xattn"], a["g_ffn"]])
    rows = {"g": g, "down_s": a["L0_ffn_down_s"], "bias1": a["L1_ffn_expert_bias"],
            "bq": a["L2_xattn_bq"], "bv": bv2, "bvd": a["L2_xattn_bkv_dca"][D:],
            "bo": a["L2_xattn_bo"], "b2": a["L3_ffn_b2"], "b_r": a["L3_ffn_b_r"],
            "iota": np.arange(P, dtype=np.float32)}
    out["rows"] = np.concatenate([rows[n].reshape(-1) for n in ROWS])
    cw = a["L0_xattn_conv_w"].reshape(2, P, 4).transpose(1, 0, 2).reshape(P, 8)
    al = a["L0_xattn_A_log"].reshape(2, P, 16).transpose(1, 0, 2).reshape(P, 32)
    out["cols"] = np.concatenate(
        [chunks(a["L0_ffn_gate_s"], 6), chunks(a["L0_ffn_up_s"], 6), cw,
         chunks(a["L0_xattn_conv_b"], 2), chunks(a["L0_xattn_dt_proj_b"], 2), al,
         chunks(a["L0_xattn_D"], 2), chunks(a["L1_xattn_gq"], 1), chunks(a["L1_xattn_gk"], 1),
         chunks(a["L3_ffn_b1"], 8), (KEEP3 * np.arange(P) % P).astype(np.float32)[:, None]], axis=1)
    nf = len(FB)
    gu = np.zeros((2, nf * P, D), np.float32)
    gu[0, :F0], gu[1, :F0] = a["L0_ffn_gate_w"], a["L0_ffn_up_w"]
    out["gu0"] = gu.reshape(2, nf, P, DC, P).transpose(4, 1, 0, 3, 2)
    dn = np.zeros((nf * P, D), np.float32)
    dn[:F0] = a["L0_ffn_down_w"].T
    out["down0"] = tiles(dn)
    def expert(wg, wu, wd):
        n = wg.shape[0]
        gu = [w.reshape(n, DC, P, P).transpose(0, 2, 1, 3).reshape(n, P, 256) for w in (wg, wu)]
        return np.stack([gu[0], gu[1], wd], axis=2)
    m1 = [np.concatenate([a["L1_ffn_w_" + n], a["L1_ffn_sw_" + n][None],
                          a["L1_ffn_sw_" + n][None]]) for n in ("gate", "up", "down")]
    out["moe1"] = expert(*[m.transpose(0, 2, 1) for m in m1])
    out["moe2"] = expert(a["L2_ffn_w1"], a["L2_ffn_w2"], a["L2_ffn_w3"])
    w = a["fside_BxS2xS2_0"]
    out["fside"] = tiles(w.reshape(B * D, D))
    out["fsideT"] = tiles(w.transpose(2, 0, 1).reshape(D, B * D))
    out["ctok"] = tiles(a["ctx_1024"].reshape(T, C))
    rw = np.zeros((DC, P, B, B), np.float32)
    rw[:, :, np.arange(B), np.arange(B)] = a["L3_ffn_W_r"].reshape(DC, P, 1)
    out["router3"] = rw.transpose(1, 0, 2, 3)
    out["w31"] = a["L3_ffn_W1"].reshape(DC, P, 8, P).transpose(1, 0, 2, 3)
    out["w32"] = tiles(a["L3_ffn_W2"])
    out["in_proj"] = a["L0_xattn_in_proj_w"].T
    xw = a["L0_xattn_x_proj_w"]
    out["x_proj"] = tiles(np.concatenate([xw[8:], xw[8:], xw[8:], xw[:8]]).T)
    out["dt_proj"] = a["L0_xattn_dt_proj_w"].T
    wd = a["L2_xattn_Wkv_dca"]
    out["w2"] = np.stack([a["L2_xattn_Wq"][:P], a["L2_xattn_Wq"][P:], wk2, wd[:, :D], wv2, wd[:, D:]], axis=1)
    out["bias2"] = np.stack([bk2, a["L2_xattn_bkv_dca"][:D]])[:, None].repeat(2, axis=1)
    ind = np.zeros((2, 2, P), np.float32)
    ind[0, 0], ind[0, 1, :P - SET2], ind[1, 1, P - SET2:] = 1, 1, 1
    out["ind2"] = ind
    out["wo2"] = tiles(a["L2_xattn_Wo"])
    aff = np.zeros((2, 4, 16, 10), np.float32)
    for j, n in enumerate(["qn_w", "qn_b", "kn_w", "kn_b", "kn_dca_w", "kn_dca_b"]):
        aff[..., j] = a["L2_xattn_" + n]
    for j in range(4):
        aff[:, j, :, 6 + j] = 1
    out["aff2"] = aff.reshape(P, 10)
    def heads(w):
        n = w.shape[0] // P
        return w.reshape(n, P, 16, P).transpose(2, 1, 0, 3).reshape(16, P, n * P)
    wvT = a["L1_xattn_Wv"].reshape(P, 16, P).transpose(1, 2, 0)
    out["w1"] = np.concatenate([heads(a["L1_xattn_Wq"]), heads(a["L1_xattn_Wk"]), wvT,
                                a["L1_xattn_Wo"].reshape(16, P, D)], axis=2)
    out["router1"] = tiles(a["L1_ffn_gate_w"].T)
    out["router2"] = tiles(a["L2_ffn_router_w"].T)
    return {n: np.ascontiguousarray(v) for n, v in out.items()}


def kernel(**inputs):
    import numpy as np
    import concourse.bacc as bacc
    from concourse.bass_utils import run_bass_kernel_spmd as run

    arrays = layout(inputs)

    def build(plan):
        nc = bacc.Bacc("TRN2", target_bir_lowering=False, num_devices=1)
        io = {n: nc.dram_tensor("in_" + n, v.shape, mybir.dt.from_np(v.dtype),
                                kind="ExternalInput").ap() for n, v in arrays.items()}
        io["out"] = nc.dram_tensor("out", (P, NT, D), F32, kind="ExternalOutput").ap()
        with ExitStack() as ctx:
            found = program(nc, io, plan, ctx)
        return nc, found

    _, plan = build({})
    nc, _ = build(plan)
    r = run(nc, [{"in_" + n: v for n, v in arrays.items()}], core_ids=[0])
    got = np.asarray(r.results[0]["out"])
    return np.ascontiguousarray(got.transpose(1, 0, 2).reshape(B, S, D))
```
